# Optimizing a Trainium2 kernel written in Bass

```python
import numpy as np
import jax
import jax.numpy as jnp

def _softmax(x, axis=-1):
    return jax.nn.softmax(x, axis=axis)

def _gelu(x):
    return jax.nn.gelu(x, approximate=True)

def _silu(x):
    return jax.nn.silu(x)

def _sigmoid(x):
    return jax.nn.sigmoid(x)

def _layernorm(x, axis=-1, eps=1e-05):
    m = jnp.mean(x, axis=axis, keepdims=True)
    v = jnp.var(x, axis=axis, keepdims=True)
    return (x - m) / jnp.sqrt(v + eps)

def _scatter_add(tgt, idx, src, axis=0):
    return tgt.at[idx].add(src)

def _segment_sum(src, seg, n):
    return jax.ops.segment_sum(src, seg, n)
kernel_name = 'mk_decoder_preln_d1_seqx_r2_624083'

def setup_inputs(seed: int=0):
    np.random.seed(seed)
    _w = jnp.asarray

    def _rec_inputs():
        import jax
        import jax.numpy as jnp
        _rk = jax.random.key(seed)
        x = 7.22e-05 + 1 * jax.random.normal(jax.random.fold_in(_rk, 1), (2, 2048, 512), jnp.float32)
        _lenS = 2048 - jax.random.randint(jax.random.fold_in(_rk, 7), (2,), 0, max(1, 2048 // 4) + 1, jnp.int32)
        _lenS2 = 128 - jax.random.randint(jax.random.fold_in(_rk, 8), (2,), 0, max(1, 128 // 4) + 1, jnp.int32)
        _ctx_1024P = jax.random.normal(jax.random.fold_in(_rk, 11), (2, 16, 512), jnp.float32)
        _ctx_1024c = jax.random.dirichlet(jax.random.fold_in(_rk, 511), 0.3 * jnp.ones((16,), jnp.float32), (2, 128))
        _ctx_1024t = jnp.einsum('bsk,bkd->bsd', _ctx_1024c, _ctx_1024P)
        _ctx_1024t = _ctx_1024t * jax.lax.rsqrt(jnp.mean(jnp.square(_ctx_1024t)) + 1e-12) * 0.953939
        ctx_1024 = 4.13588e-05 + 0.999923 * (_ctx_1024t + 0.3 * jax.random.normal(jax.random.fold_in(_rk, 611), (2, 128, 512), jnp.float32))
        return (x, ctx_1024)
    x, ctx_1024 = _rec_inputs()

    def _L0_attn_setup():
        import jax, jax.numpy as jnp
        import numpy as np
        DIM = 512
        DIM_HEAD = 64
        HEADS = DIM // DIM_HEAD
        B, N = (2, 1024)
        LN_EPS = 1e-05
        RMS_EPS = 1e-08

        def _rmsnorm(x, gamma):
            d = x.shape[-1]
            norm = jnp.linalg.norm(x, axis=-1, keepdims=True) * d ** (-0.5)
            return x / jnp.maximum(norm, RMS_EPS) * gamma

        def _layernorm(x, gamma, beta):
            mu = jnp.mean(x, axis=-1, keepdims=True)
            var = jnp.var(x, axis=-1, keepdims=True)
            return (x - mu) * jax.lax.rsqrt(var + LN_EPS) * gamma + beta
        key = jax.random.key(seed)
        ks = jax.random.split(key, 8)
        s = DIM ** (-0.5)
        return {'x': jax.random.normal(ks[0], (B, N, DIM), dtype=jnp.float32), 'ln_gamma': jnp.ones((DIM,), jnp.float32), 'ln_beta': jnp.zeros((DIM,), jnp.float32), 'q_gamma': jnp.ones((DIM_HEAD,), jnp.float32), 'k_gamma': jnp.ones((DIM_HEAD,), jnp.float32), 'w_q': jax.random.normal(ks[1], (DIM, DIM), jnp.float32) * s, 'w_k': jax.random.normal(ks[2], (DIM, DIM), jnp.float32) * s, 'w_v': jax.random.normal(ks[3], (DIM, DIM), jnp.float32) * s, 'w_o': jax.random.normal(ks[4], (DIM, DIM), jnp.float32) * s, 'b_o': jnp.zeros((DIM,), jnp.float32)}
    _L0_attn_all = _L0_attn_setup()
    _L0_attn_in = {k: v for k, v in _L0_attn_all.items() if k in ('ln_gamma', 'ln_beta', 'q_gamma', 'k_gamma', 'w_q', 'w_k', 'w_v', 'w_o', 'b_o')}
    del _L0_attn_all

    def _L0_xattn_setup():
        import jax, jax.numpy as jnp
        import numpy as np
        NUM_HEADS = 16
        KEY_DIM = 512
        DEPTH = KEY_DIM // NUM_HEADS

        def _split_heads(x):
            B, S, _ = x.shape
            return x.reshape(B, S, NUM_HEADS, DEPTH).transpose(0, 2, 1, 3)
        key = jax.random.key(seed)
        ks = jax.random.split(key, 11)
        B, S, D = (4, 1024, KEY_DIM)
        s = 1.0 / np.sqrt(D)
        return {'q': jax.random.normal(ks[0], (B, S, D), jnp.float32), 'k': jax.random.normal(ks[1], (B, S, D), jnp.float32), 'v': jax.random.normal(ks[2], (B, S, D), jnp.float32), 'Wq': jax.random.normal(ks[3], (D, D), jnp.float32) * s, 'bq': jnp.zeros((D,), jnp.float32), 'Wk': jax.random.normal(ks[4], (D, D), jnp.float32) * s, 'bk': jnp.zeros((D,), jnp.float32), 'Wv': jax.random.normal(ks[5], (D, D), jnp.float32) * s, 'bv': jnp.zeros((D,), jnp.float32), 'Wo': jax.random.normal(ks[6], (D, D), jnp.float32) * s, 'bo': jnp.zeros((D,), jnp.float32)}
    _L0_xattn_all = _L0_xattn_setup()
    _L0_xattn_in = {k: v for k, v in _L0_xattn_all.items() if k in ('Wq', 'bq', 'Wk', 'bk', 'Wv', 'bv', 'Wo', 'bo')}
    del _L0_xattn_all

    def _L0_ffn_setup():
        import jax, jax.numpy as jnp
        import numpy as np
        TOP_K = 2
        key = jax.random.key(seed)
        ks = jax.random.split(key, 6)
        B, S, D, E = (8, 2048, 512, 8)
        s = 1.0 / np.sqrt(D)
        return {'x': jax.random.normal(ks[0], (B, S, D), dtype=jnp.float32), 'Wr': jax.random.normal(ks[1], (D, E), dtype=jnp.float32) * s, 'br': jnp.zeros((E,), dtype=jnp.float32), 'W1': jax.random.normal(ks[2], (E, D, D), dtype=jnp.float32) * s, 'b1': jnp.zeros((E, D), dtype=jnp.float32), 'W2': jax.random.normal(ks[3], (E, D, D), dtype=jnp.float32) * s, 'b2': jnp.zeros((E, D), dtype=jnp.float32)}
    _L0_ffn_all = _L0_ffn_setup()
    _L0_ffn_in = {k: v for k, v in _L0_ffn_all.items() if k in ('Wr', 'br', 'W1', 'b1', 'W2', 'b2')}
    del _L0_ffn_all
    return {'x': x, 'ctx_1024': ctx_1024, 'L0_attn_ln_gamma': _L0_attn_in['ln_gamma'], 'L0_attn_ln_beta': _L0_attn_in['ln_beta'], 'L0_attn_q_gamma': _L0_attn_in['q_gamma'], 'L0_attn_k_gamma': _L0_attn_in['k_gamma'], 'L0_attn_w_q': _L0_attn_in['w_q'], 'L0_attn_w_k': _L0_attn_in['w_k'], 'L0_attn_w_v': _L0_attn_in['w_v'], 'L0_attn_w_o': _L0_attn_in['w_o'], 'L0_attn_b_o': _L0_attn_in['b_o'], 'L0_xattn_Wq': _L0_xattn_in['Wq'], 'L0_xattn_bq': _L0_xattn_in['bq'], 'L0_xattn_Wk': _L0_xattn_in['Wk'], 'L0_xattn_bk': _L0_xattn_in['bk'], 'L0_xattn_Wv': _L0_xattn_in['Wv'], 'L0_xattn_bv': _L0_xattn_in['bv'], 'L0_xattn_Wo': _L0_xattn_in['Wo'], 'L0_xattn_bo': _L0_xattn_in['bo'], 'L0_ffn_Wr': _L0_ffn_in['Wr'], 'L0_ffn_br': _L0_ffn_in['br'], 'L0_ffn_W1': _L0_ffn_in['W1'], 'L0_ffn_b1': _L0_ffn_in['b1'], 'L0_ffn_W2': _L0_ffn_in['W2'], 'L0_ffn_b2': _L0_ffn_in['b2']}

def reference(x, ctx_1024, L0_attn_ln_gamma, L0_attn_ln_beta, L0_attn_q_gamma, L0_attn_k_gamma, L0_attn_w_q, L0_attn_w_k, L0_attn_w_v, L0_attn_w_o, L0_attn_b_o, L0_xattn_Wq, L0_xattn_bq, L0_xattn_Wk, L0_xattn_bk, L0_xattn_Wv, L0_xattn_bv, L0_xattn_Wo, L0_xattn_bo, L0_ffn_Wr, L0_ffn_br, L0_ffn_W1, L0_ffn_b1, L0_ffn_W2, L0_ffn_b2):
    import jax
    import jax.numpy as jnp

    def _L0_attn_ref(x, ln_gamma, ln_beta, q_gamma, k_gamma, w_q, w_k, w_v, w_o, b_o):
        import jax, jax.numpy as jnp
        import numpy as np
        DIM = 512
        DIM_HEAD = 64
        HEADS = DIM // DIM_HEAD
        B, N = (2, 1024)
        LN_EPS = 1e-05
        RMS_EPS = 1e-08

        def _rmsnorm(x, gamma):
            d = x.shape[-1]
            norm = jnp.linalg.norm(x, axis=-1, keepdims=True) * d ** (-0.5)
            return x / jnp.maximum(norm, RMS_EPS) * gamma

        def _layernorm(x, gamma, beta):
            mu = jnp.mean(x, axis=-1, keepdims=True)
            var = jnp.var(x, axis=-1, keepdims=True)
            return (x - mu) * jax.lax.rsqrt(var + LN_EPS) * gamma + beta
        h, dh = (HEADS, DIM_HEAD)
        xn = _layernorm(x, ln_gamma, ln_beta)

        def proj(w):
            y = xn @ w.T
            b, n, _ = y.shape
            return y.reshape(b, n, h, dh).transpose(0, 2, 1, 3)
        q = proj(w_q)
        k = proj(w_k)
        v = proj(w_v)
        qn = _rmsnorm(q, q_gamma) * dh ** (-0.5)
        kn = _rmsnorm(k, k_gamma)
        sim = jnp.einsum('bhid,bhjd->bhij', qn, kn)
        attn = jax.nn.softmax(sim, axis=-1)
        out = jnp.einsum('bhij,bhjd->bhid', attn, v)
        b, _, n, _ = out.shape
        out = out.transpose(0, 2, 1, 3).reshape(b, n, h * dh)
        return out @ w_o.T + b_o

    def _L0_xattn_ref(q, k, v, Wq, bq, Wk, bk, Wv, bv, Wo, bo):
        import jax, jax.numpy as jnp
        import numpy as np
        NUM_HEADS = 16
        KEY_DIM = 512
        DEPTH = KEY_DIM // NUM_HEADS

        def _split_heads(x):
            B, S, _ = x.shape
            return x.reshape(B, S, NUM_HEADS, DEPTH).transpose(0, 2, 1, 3)
        qh = _split_heads(q @ Wq + bq)
        kh = _split_heads(k @ Wk + bk)
        vh = _split_heads(v @ Wv + bv)
        scale = 1.0 / jnp.sqrt(jnp.asarray(DEPTH, jnp.float32))
        logits = jnp.einsum('bhqd,bhkd->bhqk', qh, kh) * scale
        weights = jax.nn.softmax(logits, axis=-1)
        out = jnp.einsum('bhqk,bhkd->bhqd', weights, vh)
        B, H, S, d = out.shape
        concat = out.transpose(0, 2, 1, 3).reshape(B, S, H * d)
        return concat @ Wo + bo

    def _L0_ffn_ref(x, Wr, br, W1, b1, W2, b2):
        import jax, jax.numpy as jnp
        import numpy as np
        TOP_K = 2
        k = TOP_K
        scores0 = x[:, 0, :] @ Wr + br
        _, idx = jax.lax.top_k(scores0, k)
        W1g, b1g = (W1[idx], b1[idx])
        W2g, b2g = (W2[idx], b2[idx])
        h = jnp.einsum('bsd,bkde->bkse', x, W1g) + b1g[:, :, None, :]
        h = jax.nn.gelu(h, approximate=False)
        o = jnp.einsum('bkse,bkef->bksf', h, W2g) + b2g[:, :, None, :]
        return jnp.sum(o, axis=1) / k
    x = x + _L0_attn_ref(_layernorm(x, axis=-1), L0_attn_ln_gamma, L0_attn_ln_beta, L0_attn_q_gamma, L0_attn_k_gamma, L0_attn_w_q, L0_attn_w_k, L0_attn_w_v, L0_attn_w_o, L0_attn_b_o)
    x = x + _L0_xattn_ref(_layernorm(x, axis=-1), ctx_1024, ctx_1024, L0_xattn_Wq, L0_xattn_bq, L0_xattn_Wk, L0_xattn_bk, L0_xattn_Wv, L0_xattn_bv, L0_xattn_Wo, L0_xattn_bo)
    x = x + _L0_ffn_ref(_layernorm(x, axis=-1), L0_ffn_Wr, L0_ffn_br, L0_ffn_W1, L0_ffn_b1, L0_ffn_W2, L0_ffn_b2)
    return x

_drawn_inputs = setup_inputs


def setup_inputs(seed=0):
    import zlib

    import numpy as np

    out = dict(_drawn_inputs(seed))
    spreads = {'L0_attn_ln_gamma': (1.0, 0.6),
     'L0_attn_ln_beta': (0.0, 0.1),
     'L0_attn_q_gamma': (1.0, 0.6),
     'L0_attn_k_gamma': (1.0, 0.6),
     'L0_attn_b_o': (0.0, 0.1),
     'L0_xattn_bq': (0.0, 0.38),
     'L0_xattn_bk': (0.0, 0.8),
     'L0_xattn_bv': (0.0, 0.1),
     'L0_xattn_bo': (0.0, 0.1),
     'L0_ffn_br': (0.0, 0.1),
     'L0_ffn_b1': (0.0, 0.1),
     'L0_ffn_b2': (0.0, 0.1)}
    factors = {}
    for name, (base, spread) in spreads.items():
        noise = np.random.default_rng([zlib.crc32(name.encode()), seed]).standard_normal(out[name].shape)
        drawn = base * np.exp(spread * noise) if base else spread * noise
        out[name] = jnp.asarray(drawn.astype(out[name].dtype))
    for name, factor in factors.items():
        out[name] = (out[name] * factor).astype(out[name].dtype)
    return out
```

```python
from contextlib import ExitStack

import concourse.bass as bass
from concourse import mybir

F32 = mybir.dt.float32
F16 = mybir.dt.float16
U32 = mybir.dt.uint32
ALU = mybir.AluOpType
ACT = mybir.ActivationFunctionType
AX_X = mybir.AxisListType.X

P = 128
WS = 64.0
INV_WS = 1.0 / WS
PSHIFT = 6.93
LN_EPS = 1e-5
RMS_EPS = 1e-8


def decoder_layer(nc, x, ctx_in, ln_g, ln_b, q_gamma, k_gamma, w_q, w_k, w_v, w_o, b_o,
                  xw_q, xb_q, xw_k, xb_k, xw_v, xb_v, xw_o, xb_o, wr, br, w1, b1, w2, b2, out):
    B, N, D = x.shape
    DC = D // P
    DH = q_gamma.shape[0]
    H = D // DH
    TPC = 4
    CT = TPC * P
    CH = N // CT
    KB = N // P
    CTX = ctx_in.shape[1]
    XH = 16
    XD = D // XH
    E = wr.shape[1]
    XSCALE = float(XD) ** -0.5
    assert D == 512 and DH == 64 and CTX == P and N == 2048 and KB == 16

    x_rows = x.rearrange("b n d -> (b n) d")
    out_rows = out.rearrange("b n d -> (b n) d")
    ctx_rows = ctx_in.rearrange("b n d -> (b n) d")

    def by_rows(w):
        v = w.rearrange("(c p) n -> p c n", p=P)
        return [[v[0:64, 2 * i:2 * i + 2, :], v[64:128, 2 * i:2 * i + 2, :]] for i in range(2)]

    def by_head(w):
        v = w.rearrange("(h d) n -> d h n", d=DH)
        return [[v[:, 2 * i:2 * i + 2, :]] * 2 for i in range(4)]

    PIECES_P1 = [(n, i) for n in ("q", "k", "v") for i in range(2)]
    PIECES_P3 = [(n, i) for n in ("xk", "xv") for i in range(2)] + [("o", i) for i in range(4)] + \
                [(n, i) for n in ("xq", "xo") for i in range(2)]
    PIECES_P4 = [(n, i) for n in ("w10", "w11", "w20", "w21") for i in range(2)]
    PIECES = PIECES_P1 + PIECES_P3 + PIECES_P4
    NP = len(PIECES)
    source = {"q": by_rows(w_q), "k": by_rows(w_k), "v": by_rows(w_v), "xk": by_rows(xw_k), "xv": by_rows(xw_v),
              "o": by_head(w_o), "xq": by_rows(xw_q), "xo": by_rows(xw_o)}

    with ExitStack() as top:
        def sem(name):
            return top.enter_context(nc.semaphore(name))

        def sb(ctx, name, shape, dt):
            return ctx.enter_context(nc.sbuf_tensor(name, shape, dt))

        banks = [top.enter_context(nc.psum_tensor(f"bank{i}", [P, 512], F32)) for i in range(8)]

        ident = sb(top, "ident", [P, P], F32)
        ident16 = sb(top, "ident16", [P, P], F16)
        neg_half = sb(top, "neg_half", [P, 2 * H], F32)
        qg0 = sb(top, "qg0", [P, 1], F32)
        qg = sb(top, "qg", [P, 1], F32)
        kg = sb(top, "kg", [P, 1], F32)
        wr_sb = sb(top, "wr_sb", [P, DC, E], F32)
        br_sb = sb(top, "br_sb", [1, E], F32)
        q_hh = sb(top, "q_hh", [P, H, N], F16)

        s_const = sem("s_const")
        s_pool = sem("s_pool")
        s_setup = sem("s_setup")
        w_loaded = [sem("w_loaded0"), sem("w_loaded1")]
        wh_ready = sem("wh_ready")
        w_split = sem("w_split")

        def bcast(v):
            return v.rearrange("(a n) -> a n", a=1).broadcast_to([P, v.shape[0]])

        def load_pieces(sp, b, pieces, stage, src):
            for piece in pieces:
                w = PIECES.index(piece)
                sp.wait_ge(w_split, b * NP + w + 1)
                for half in range(2):
                    sp.dma_start(stage[w % 2][64 * half:64 * half + 64, :, :], src[piece[0]][piece[1]][half])\
                        .then_inc(w_loaded[w % 2], 16)

        def split_high(act, b, pieces, stage, wh):
            for piece in pieces:
                w = PIECES.index(piece)
                act.wait_ge(w_loaded[w % 2], b * (32 * NP // 2) + 32 * (w // 2 + 1))
                act.activation(wh[piece[0]][:, 2 * piece[1]:2 * piece[1] + 2, :], stage[w % 2][:, :, :], ACT.Copy,
                               scale=WS).then_inc(wh_ready, 1)

        def split_low(dve, b, pieces, stage, wh, wl):
            for piece in pieces:
                w = PIECES.index(piece)
                part = slice(2 * piece[1], 2 * piece[1] + 2)
                dve.wait_ge(wh_ready, b * NP + w + 1)
                dve.scalar_tensor_tensor(out=wl[piece[0]][:, part, :], in0=stage[w % 2][:, :, :], scalar=WS,
                                         in1=wh[piece[0]][:, part, :], op0=ALU.mult, op1=ALU.subtract)\
                    .then_inc(w_split, 1)

        def pieces_split(b, pieces):
            return b * NP + PIECES.index(pieces[-1]) + 3

        def mm3(pe, bank, xh, xl, wh, wl, last=None):
            for c in range(DC):
                pe.matmul(bank, xh(c), wh(c), start=(c == 0), stop=False)
                pe.matmul(bank, xh(c), wl(c), start=False, stop=False)
                mm = pe.matmul(bank, xl(c), wh(c), start=False, stop=(c == DC - 1))
            return mm

        a_const = sem("a_const")
        a_ones = sem("a_ones")
        a_x_in = [sem(f"a_x_in{i}") for i in range(2)]
        a_bn = sem("a_bn")
        a_stat = sem("a_stat")
        a_var = sem("a_var")
        a_rs = sem("a_rs")
        a_y = sem("a_y")
        a_xg = sem("a_xg")
        a_xn = sem("a_xn")
        a_t_done = sem("a_t_done")
        a_xh = sem("a_xh")
        a_xl = sem("a_xl")
        a_q_done = sem("a_q_done")
        a_k_done = sem("a_k_done")
        a_v_done = sem("a_v_done")
        a_sq = sem("a_sq")
        a_vh = sem("a_vh")
        a_v_ready = sem("a_v_ready")
        a_ssq = sem("a_ssq")
        a_ms = sem("a_ms")
        a_pow = sem("a_pow")
        a_rinv = sem("a_rinv")
        a_qk = sem("a_qk")
        a_ht_done = sem("a_ht_done")
        a_hh = sem("a_hh")
        a_ht_free = sem("a_ht_free")
        a_dup = sem("a_dup")
        s_ready = sem("s_ready")
        p_ready = sem("p_ready")
        ph_ready = sem("ph_ready")
        pl_ready = sem("pl_ready")
        p_free = sem("p_free")
        mx_ready = sem("mx_ready")
        mx_free = sem("mx_free")
        gm_ready = sem("gm_ready")
        nm_ready = sem("nm_ready")
        mrow_done = sem("mrow_done")
        m_ready = sem("m_ready")
        o_rec = sem("o_rec")
        o_norm = sem("o_norm")
        o_high = sem("o_high")
        o_free = sem("o_free")
        vs_ones = sem("vs_ones")
        vs_half = sem("vs_half")
        vs_ready = sem("vs_ready")
        c_in = sem("c_in")
        c_zero = sem("c_zero")
        c_t = sem("c_t")
        c_h = sem("c_h")
        c_l = sem("c_l")
        c_mm = sem("c_mm")
        c_tok = sem("c_tok")
        d_x_in = [sem(f"d_x_in{i}") for i in range(TPC)]
        d_xb = sem("d_xb")
        d_mm = sem("d_mm")
        d_x1 = sem("d_x1")
        d_x2 = sem("d_x2")
        d_xb2 = sem("d_xb2")
        d_bn = sem("d_bn")
        d_stat = sem("d_stat")
        d_var = sem("d_var")
        d_rs = sem("d_rs")
        d_tok = sem("d_tok")
        d_t_done = sem("d_t_done")
        d_th = sem("d_th")
        d_tl = sem("d_tl")
        d_s_done = sem("d_s_done")
        d_mx = sem("d_mx")
        d_nmx = sem("d_nmx")
        d_ex = sem("d_ex")
        d_pt_done = sem("d_pt_done")
        d_pth = sem("d_pth")
        d_ptl = sem("d_ptl")
        d_av_done = sem("d_av_done")
        d_rec = sem("d_rec")
        r_col = sem("r_col")
        r_mm = sem("r_mm")
        r_sc = sem("r_sc")
        r_top = sem("r_top")
        r_idx = sem("r_idx")
        f_b = sem("f_b")
        f_b2 = sem("f_b2")
        f_xb = sem("f_xb")
        f1_done = sem("f1_done")
        f_g = sem("f_g")
        f_gh = sem("f_gh")
        f_gl = sem("f_gl")
        f2_done = sem("f2_done")
        f_y = sem("f_y")
        y_out = [sem(f"y_out{i}") for i in range(2)]

        with nc.Block() as block:
            @block.sync
            def _(sp):
                for half in (0, DH):
                    sp.dma_start(qg0[half:half + DH, :], q_gamma.rearrange("(d a) -> d a", a=1)).then_inc(s_const, 16)
                    sp.dma_start(kg[half:half + DH, :], k_gamma.rearrange("(d a) -> d a", a=1)).then_inc(s_const, 16)
                sp.dma_start(wr_sb[:, :, :], wr.rearrange("(c p) e -> p c e", p=P)).then_inc(s_const, 16)
                sp.dma_start(br_sb[:, :], br.rearrange("(a e) -> a e", a=1)).then_inc(s_const, 16)
                sp.wait_ge(s_const, 16 * 6)

            @block.gpsimd
            def _(pool):
                pool.memset(ident[:, :], 0.0).then_inc(s_pool, 1)
                pool.memset(neg_half[:, :], -0.5).then_inc(s_pool, 1)
                pool.wait_ge(s_pool, 2)
                pool.affine_select(out=ident[:, :], in_=ident[:, :], compare_op=ALU.not_equal, fill=1.0, base=0,
                                   pattern=[[-1, P]], channel_multiplier=1).then_inc(s_pool, 1)
                for s, credits in ((w_split, 2), (a_y, 2), (a_v_ready, 1), (a_ht_free, 2), (p_free, 4), (mx_free, 4),
                                   (o_free, 8), (d_x2, 4), (d_tl, 2), (d_pt_done, 2), (d_ptl, 2),
                                   (f_g, 2), (f2_done, 4), (f_y, 2), (y_out[0], 16), (y_out[1], 16)):
                    pool.sem_inc(s, credits)

            @block.vector
            def _(dve):
                dve.wait_ge(s_pool, 3)
                dve.tensor_copy(ident16[:, :], ident[:, :]).then_inc(s_setup, 1)
                dve.wait_ge(s_const, 16 * 6)
                dve.tensor_scalar(qg[:, :], qg0[:, :], float(DH) ** -0.5, None, ALU.mult).then_inc(s_setup, 1)

        with nc.Fori(0, B) as b:
            with ExitStack() as attn:
                q_lm = sb(attn, "q_lm", [P, H, N], F16)
                k_h1 = sb(attn, "k_h1", [P, H, N], F16)
                k_hl = sb(attn, "k_hl", [P, H, N], F16)
                v_h = sb(attn, "v_h", [P, KB * D], F16)
                v_l = sb(attn, "v_l", [P, KB * D], F16)

                with ExitStack() as ph:
                    lng = sb(ph, "lng", [P, D], F32)
                    lnb = sb(ph, "lnb", [P, D], F32)
                    stage = [sb(ph, f"stage_a{i}", [P, 2, D], F32) for i in range(2)]
                    wh = {n: sb(ph, f"wh_{n}", [P, DC, D], F16) for n in ("q", "k", "v")}
                    wl = {n: sb(ph, f"wl_{n}", [P, DC, D], F16) for n in ("q", "k", "v")}
                    xt = stage[0]
                    yt = stage[1]
                    st = sb(ph, "st_a", [P, 2, 6], F32)
                    mv = sb(ph, "mv_a", [P, 2, 2], F32)
                    rs = sb(ph, "rs_a", [P, 2, 2], F32)
                    xth = sb(ph, "xth_a", [P, 2, D], F16)
                    xtl = sb(ph, "xtl_a", [P, 2, D], F16)
                    ssq = sb(ph, "ssq", [P, 2 * H], F32)
                    ms = sb(ph, "ms", [P, 2 * H], F32)
                    rp = sb(ph, "rp", [P, 2 * H], F32)
                    rinv = sb(ph, "rinv", [P, 2 * H], F32)
                    qkn = sb(ph, "qkn", [P, 2, D], F32)
                    HT = banks[0:2]
                    TB = banks[2]
                    QB = banks[3:5]
                    KBK = banks[5:7]
                    VB = banks[7]
                    block = ph.enter_context(nc.Block())

                    @block.sync
                    def _(sp):
                        load_pieces(sp, b, PIECES_P1, stage, source)
                        sp.dma_start(lng[:, :], bcast(ln_g)).then_inc(a_const, 16)
                        sp.dma_start(lnb[:, :], bcast(ln_b)).then_inc(a_const, 16)
                        sp.wait_ge(w_split, pieces_split(b, PIECES_P1))
                        sp.nop(nofuse=True)
                        with sp.Fori(0, CH) as c:
                            n = b * CH + c
                            for j in range(TPC):
                                sp.wait_ge(a_y, n * TPC + j + 1)
                                sp.dma_start(xt[:, j % 2, :], x_rows[bass.ds(n * CT + j * P, P), :])\
                                    .then_inc(a_x_in[j % 2], 16)

                    @block.gpsimd
                    def _(pool):
                        pool.memset(k_h1[DH:DH + 1, :, :], 1.0).then_inc(a_ones, 1)
                        pool.wait_ge(a_ones, b + 1)
                        pool.wait_ge(a_const, 32 * (b + 1))
                        pool.nop(nofuse=True)
                        with pool.Fori(0, CH) as c:
                            t0 = (b * CH + c) * TPC

                            def norm_scale(j):
                                pool.wait_ge(a_stat, t0 + j + 1)
                                pool.nop(nofuse=True)
                                pool.tensor_scalar(rs[:, 0, j % 2:j % 2 + 1], mv[:, j % 2, 1:2], 1.0 + LN_EPS,
                                                   LN_EPS * LN_EPS, ALU.mult, ALU.add).then_inc(a_var, 1)
                                pool.wait_ge(a_var, t0 + j + 1)
                                pool.tensor_tensor(rs[:, 1, j % 2:j % 2 + 1], rs[:, 0, j % 2:j % 2 + 1],
                                                   neg_half[:, 0:1], ALU.pow).then_inc(a_rs, 1)

                            def affine(j):
                                pool.wait_ge(a_y, t0 + j + 3)
                                pool.tensor_tensor(yt[:, j % 2, :], yt[:, j % 2, :], lng[:, :], ALU.mult)\
                                    .then_inc(a_xg, 1)
                                pool.wait_ge(a_xg, t0 + j + 1)
                                pool.tensor_tensor(yt[:, j % 2, :], yt[:, j % 2, :], lnb[:, :], ALU.add)\
                                    .then_inc(a_xn, 1)

                            def rms_scale(j):
                                pool.wait_ge(a_ssq, t0 + j + 1)
                                pool.nop(nofuse=True)
                                pool.tensor_scalar(ms[:, :], ssq[:, :], 1.0 / DH, RMS_EPS * RMS_EPS, ALU.mult, ALU.max)\
                                    .then_inc(a_ms, 1)
                                pool.wait_ge(a_ms, t0 + j + 1)
                                pool.tensor_tensor(rp[:, :], ms[:, :], neg_half[:, :], ALU.pow).then_inc(a_pow, 1)
                                pool.wait_ge(a_pow, t0 + j + 1)
                                pool.nop(nofuse=True)
                                pool.tensor_scalar(rinv[:, :], rp[:, :], INV_WS, None, ALU.mult).then_inc(a_rinv, 1)

                            norm_scale(0)
                            affine(0)
                            for j in range(TPC):
                                if j + 1 < TPC:
                                    norm_scale(j + 1)
                                    affine(j + 1)
                                rms_scale(j)

                    @block.tensor
                    def _(pe):
                        pe.wait_ge(w_split, pieces_split(b, PIECES_P1))
                        pe.nop(nofuse=True)
                        with pe.Fori(0, CH) as c:
                            t0 = (b * CH + c) * TPC

                            def transposes(j):
                                pe.wait_ge(a_xn, t0 + j + 1)
                                if j:
                                    pe.wait_ge(a_xl, t0 + j)
                                for d in range(DC):
                                    mm = pe.transpose(TB[:, d * P:(d + 1) * P], yt[:, j % 2, d * P:(d + 1) * P],
                                                      ident[:, :])
                                mm.then_inc(a_t_done, 1)

                            def project(j, name, bank, done):
                                mm3(pe, bank[:, :],
                                    lambda d: xth[:, j % 2, d * P:(d + 1) * P], lambda d: xtl[:, j % 2, d * P:(d + 1) * P],
                                    lambda d: wh[name][:, d, :], lambda d: wl[name][:, d, :]).then_inc(done, 1)

                            def head_transposes(j):
                                for which in range(2):
                                    pe.wait_ge(a_qk, 2 * (t0 + j) + which + 1)
                                    pe.wait_ge(a_ht_free, 2 * (t0 + j) + which + 1)
                                    for d in range(DC):
                                        mm = pe.transpose(HT[which][:, d * P:(d + 1) * P],
                                                          qkn[:, which, d * P:(d + 1) * P], ident[:, :])
                                    mm.then_inc(a_ht_done, 1)

                            transposes(0)
                            for j in range(TPC):
                                pe.wait_ge(a_xl, t0 + j + 1)
                                project(j, "q", QB[j % 2], a_q_done)
                                project(j, "k", KBK[j % 2], a_k_done)
                                if j:
                                    head_transposes(j - 1)
                                pe.wait_ge(a_v_ready, t0 + j + 1)
                                project(j, "v", VB, a_v_done)
                                if j + 1 < TPC:
                                    transposes(j + 1)
                            head_transposes(TPC - 1)

                    @block.scalar
                    def _(act):
                        split_high(act, b, PIECES_P1, stage, wh)
                        with act.Fori(0, CH) as c:
                            t0 = (b * CH + c) * TPC

                            def x_high(j):
                                act.wait_ge(a_t_done, t0 + j + 1)
                                act.activation(xth[:, j % 2, :], TB[:, :], ACT.Copy).then_inc(a_xh, 1)

                            def heads_high(j):
                                tok = bass.ds(c * CT + j * P, P)
                                for which, (dst, g) in enumerate(((q_hh, qg), (k_h1, kg))):
                                    act.wait_ge(a_ht_done, 2 * (t0 + j) + which + 1)
                                    for odd in range(2):
                                        src = HT[which][DH * odd:DH * odd + DH, :].rearrange("p (h n) -> p h n", h=DC)
                                        act.activation(dst[0:DH, odd::2, tok], src, ACT.Copy,
                                                       scale=g[DH * odd:DH * odd + DH, :]).then_inc(a_hh, 1)

                            x_high(0)
                            for j in range(TPC):
                                act.wait_ge(a_q_done, t0 + j + 1)
                                if j:
                                    act.wait_ge(a_ht_done, 2 * (t0 + j))
                                act.activation(qkn[:, 0, :], QB[j % 2][:, :], ACT.Square, scale=INV_WS).then_inc(a_sq, 1)
                                act.wait_ge(a_k_done, t0 + j + 1)
                                act.activation(qkn[:, 1, :], KBK[j % 2][:, :], ACT.Square, scale=INV_WS).then_inc(a_sq, 1)
                                if j:
                                    heads_high(j - 1)
                                act.wait_ge(a_v_done, t0 + j + 1)
                                act.activation(v_h[:, bass.ds(c * (TPC * D) + j * D, D)], VB[:, :], ACT.Copy,
                                               scale=INV_WS).then_inc(a_vh, 1)
                                if j + 1 < TPC:
                                    x_high(j + 1)
                            heads_high(TPC - 1)

                    @block.vector
                    def _(dve):
                        split_low(dve, b, PIECES_P1, stage, wh, wl)
                        with dve.Fori(0, CH) as c:
                            t0 = (b * CH + c) * TPC

                            def normalise(j):
                                s = j % 2
                                dve.wait_ge(a_x_in[s], 8 * t0 + 16 * (j // 2 + 1))
                                dve.nop(nofuse=True)
                                dve.bn_stats(st[:, s, :], xt[:, s, :]).then_inc(a_bn, 1)
                                dve.wait_ge(a_bn, t0 + j + 1)
                                dve.nop(nofuse=True)
                                dve.bn_aggr(mv[:, s, :], st[:, s, :]).then_inc(a_stat, 1)
                                dve.wait_ge(a_rs, t0 + j + 1)
                                if j >= 2:
                                    dve.wait_ge(a_t_done, t0 + j - 1)
                                dve.tensor_scalar(yt[:, s, :], xt[:, s, :], mv[:, s, 0:1], rs[:, 1, s:s + 1],
                                                  ALU.subtract, ALU.mult).then_inc(a_y, 1)

                            def x_low(j):
                                dve.wait_ge(a_xh, t0 + j + 1)
                                dve.tensor_tensor(xtl[:, j % 2, :], TB[:, :], xth[:, j % 2, :], ALU.subtract)\
                                    .then_inc(a_xl, 1)

                            def heads_low(j):
                                tok = bass.ds(c * CT + j * P, P)
                                for which, (high, low, row, g) in enumerate(((q_hh, q_lm, 0, qg), (k_h1, k_hl, DH, kg))):
                                    for odd in range(2):
                                        dve.wait_ge(a_hh, 4 * (t0 + j) + 2 * which + odd + 1)
                                        src = HT[which][DH * odd:DH * odd + DH, :].rearrange("p (h n) -> p h n", h=DC)
                                        low_part = dve.scalar_tensor_tensor(
                                            out=low[row:row + DH, odd::2, tok], in0=src,
                                            scalar=g[DH * odd:DH * odd + DH, :], in1=high[0:DH, odd::2, tok],
                                            op0=ALU.mult, op1=ALU.subtract)
                                    low_part.then_inc(a_ht_free, 1)
                                    if which == 0:
                                        dve.tensor_copy(q_hh[DH:P, :, tok], q_hh[0:DH, :, tok]).then_inc(a_dup, 1)
                                    else:
                                        dve.tensor_copy(k_hl[0:DH, :, tok], k_h1[0:DH, :, tok]).then_inc(a_dup, 1)

                            normalise(0)
                            x_low(0)
                            for j in range(TPC):
                                if j + 1 < TPC:
                                    normalise(j + 1)
                                dve.wait_ge(a_sq, 2 * (t0 + j) + 2)
                                dve.tensor_reduce(ssq[:, :], qkn[:, :, :].rearrange("p w (h d) -> p (w h) d", d=DH),
                                                  AX_X, ALU.add).then_inc(a_ssq, 1)
                                dve.wait_ge(a_rinv, t0 + j + 1)
                                for which, bank in enumerate((QB[j % 2], KBK[j % 2])):
                                    dve.tensor_tensor(
                                        qkn[:, which, :].rearrange("p (h d) -> p h d", d=DH),
                                        bank[:, :].rearrange("p (h d) -> p h d", d=DH),
                                        rinv[:, which * H:which * H + H].rearrange("p (h a) -> p h a", a=1)
                                        .broadcast_to([P, H, DH]), ALU.mult).then_inc(a_qk, 1)
                                if j + 1 < TPC:
                                    x_low(j + 1)
                                if j:
                                    heads_low(j - 1)
                                vcols = bass.ds(c * (TPC * D) + j * D, D)
                                dve.wait_ge(a_vh, t0 + j + 1)
                                dve.scalar_tensor_tensor(out=v_l[:, vcols], in0=VB[:, :], scalar=INV_WS,
                                                         in1=v_h[:, vcols], op0=ALU.mult, op1=ALU.subtract)\
                                    .then_inc(a_v_ready, 1)
                            heads_low(TPC - 1)

                with ExitStack() as ph:
                    vsh = sb(ph, "vsh", [P, 2 * KB * P], F16)
                    vsl = sb(ph, "vsl", [P, 2 * KB * P], F16)
                    probs = sb(ph, "probs", [P, 4, CT], F32)
                    probs_h = sb(ph, "probs_h", [P, 4, CT], F16)
                    probs_l = sb(ph, "probs_l", [P, 4, CT], F16)
                    pm = sb(ph, "pm", [P, 16], F32)
                    gm = sb(ph, "gm", [P, TPC], F32)
                    nm = sb(ph, "nm", [P, TPC], F16)
                    osb = sb(ph, "osb", [P, CT], F32)
                    rden = sb(ph, "rden", [DH, CT], F32)
                    onorm = sb(ph, "onorm", [DH, CT], F32)
                    SB = banks[0:2]
                    MB = banks[2:6]
                    OB = banks[7]
                    RB = banks[6]
                    qf = q_hh[:, :, :].rearrange("p h n -> p (h n)")
                    lf = q_lm[:, :, :].rearrange("p h n -> p (h n)")
                    k1 = k_hl[:, :, :].rearrange("p h n -> p (h n)")
                    k2 = k_h1[:, :, :].rearrange("p h n -> p (h n)")
                    UNITS = H * CH
                    U0 = b * UNITS
                    LA = 2
                    MAXED = UNITS - LA
                    block = ph.enter_context(nc.Block())

                    @block.gpsimd
                    def _(pool):
                        with pool.Fori(0, UNITS) as u:
                            step = (U0 + u) * KB
                            for kb in range(KB):
                                pool.wait_ge(ph_ready, step + kb + 1)
                                pool.wait_ge(p_free, step + kb + 1)
                                pool.tensor_tensor(probs_l[:, kb % 4, :], probs[:, kb % 4, :], probs_h[:, kb % 4, :],
                                                   ALU.subtract).then_inc(pl_ready, 1)

                    @block.tensor
                    def _(pe):
                        def max_scores(k, qcol, kcol, count):
                            pe.wait_ge(mx_free, count + 1)
                            pe.matmul(MB[k % 4][:, :], qf[:, qcol], k1[:, kcol], start=True, stop=True)\
                                .then_inc(mx_ready, 1)

                        def max_row(r):
                            pe.wait_ge(nm_ready, r + 1)
                            for a in range(TPC):
                                mm = pe.matmul(RB[DH:DH + 1, a * P:(a + 1) * P], nm[:, a:a + 1], ident16[:, :],
                                               start=True, stop=True)
                            mm.then_inc(mrow_done, 1)

                        def scores(u, kb):
                            kcols, qcols = bass.ds(u // CH * N + kb * P, P), bass.ds(u * CT, CT)
                            pe.matmul(SB[kb % 2][:, :], k1[:, kcols], qf[:, qcols], start=True, stop=False)
                            pe.matmul(SB[kb % 2][:, :], k2[0:DH + 1, kcols], lf[0:DH + 1, qcols], start=False,
                                      stop=True).then_inc(s_ready, 1)

                        def unit(u, maxed, last=False):
                            U = U0 + u
                            pe.wait_ge(vs_ready, U0 + u // CH * CH + CH)
                            for kb in range(KB):
                                pe.wait_ge(ph_ready, U * KB + kb + 1)
                                if kb + 2 < KB:
                                    scores(u, kb + 2)
                                elif not last:
                                    if kb + 2 == KB:
                                        pe.wait_ge(m_ready, U + 2)
                                    scores(u + 1, kb + 2 - KB)
                                if maxed:
                                    max_scores(kb, bass.ds((u + LA) * CT + kb // 4 * P, P),
                                               bass.ds((u + LA) // CH * N + kb % 4 * CT, CT), (U + LA) * 16 + kb)
                                if kb == 2 and (maxed or u == MAXED):
                                    max_row(U + LA - 1)
                                if kb == 0:
                                    pe.wait_ge(o_free, U + 8)
                                v0 = u // CH % 2 * (KB * P) + kb * P
                                pe.matmul(OB[:, :], vsl[:, bass.ds(v0, P)], probs_h[:, kb % 4, :],
                                          start=(kb == 0), stop=False)
                                pe.matmul(OB[0:DH, :], vsh[:, bass.ds(v0, DH)], probs_h[:, kb % 4, :],
                                          start=False, stop=False, skip_group_check=True)
                                pe.wait_ge(pl_ready, U * KB + kb + 1)
                                pe.matmul(OB[:, :], vsh[:, bass.ds(v0, P)], probs_l[:, kb % 4, :],
                                          start=False, stop=(kb == KB - 1)).then_inc(p_free, 1)

                        pe.wait_ge(a_ones, b + 1)
                        for g in range(LA):
                            for k in range(16):
                                max_scores(k, slice(g * CT + k // 4 * P, g * CT + k // 4 * P + P),
                                           slice(k % 4 * CT, k % 4 * CT + CT), U0 * 16 + g * 16 + k)
                            if g < LA - 1:
                                max_row(U0 + g)
                        pe.wait_ge(m_ready, U0 + 1)
                        scores(0, 0)
                        scores(0, 1)
                        with pe.Fori(0, MAXED) as u:
                            unit(u, True)
                        for u in range(MAXED, UNITS):
                            unit(u, False, last=(u == UNITS - 1))

                    @block.scalar
                    def _(act):
                        act.preload_act_table(ACT.Exp)
                        with act.Fori(0, UNITS) as u:
                            step = (U0 + u) * KB
                            for kb in range(KB):
                                act.wait_ge(s_ready, step + kb + 1)
                                act.wait_ge(p_free, step + kb + 1)
                                act.activation(probs[:, kb % 4, :], SB[kb % 2][:, :], ACT.Exp).then_inc(p_ready, 1)
                                act.activation(probs_h[:, kb % 4, :], SB[kb % 2][:, :], ACT.Exp).then_inc(ph_ready, 1)

                    @block.vector
                    def _(dve):
                        def reduce_max(k, count):
                            dve.wait_ge(mx_ready, count + 1)
                            dve.tensor_reduce(pm[:, k:k + 1], MB[k % 4][:, :], AX_X, ALU.max).then_inc(mx_free, 1)

                        def negate_max(r):
                            dve.wait_ge(mx_free, r * 16 + 20)
                            dve.tensor_reduce(gm[:, :], pm[:, :].rearrange("p (a k) -> p a k", k=4), AX_X, ALU.max)\
                                .then_inc(gm_ready, 1)
                            dve.wait_ge(gm_ready, r + 1)
                            dve.tensor_scalar(nm[:, :], gm[:, :], -1.0, PSHIFT, ALU.mult, ALU.add).then_inc(nm_ready, 1)

                        def copy_row(r, cols):
                            dve.wait_ge(mrow_done, r + 1)
                            dve.tensor_copy(lf[DH:DH + 1, cols], RB[DH:DH + 1, :]).then_inc(m_ready, 1)

                        def copy_v(t):
                            cols = bass.ds(t * (KB // CH * P) % (2 * KB * P), KB // CH * P)
                            rows = bass.ds(t % CH * (KB // CH * D), KB // CH * D)
                            for i, (dst, src) in enumerate(((vsh, v_h), (vsl, v_l))):
                                dve.tensor_copy(dst[:, cols].rearrange("p (k n) -> p k n", n=P)[:, :, 0:DH],
                                                src[:, rows].rearrange("p (k d) -> p k d", d=D)
                                                [:, :, bass.ds(t // CH * DH, DH)])\
                                    .then_inc((vs_half, vs_ready)[i], 1)

                        AHEAD = 4
                        for i, v in enumerate((vsh, vsl)):
                            dve.memset(v[:, :].rearrange("p (k n) -> p k n", n=P)[:, :, DH:P], 1.0).then_inc(vs_ones, 1)
                        for t in range(CH):
                            copy_v(t)
                        for g in range(LA):
                            for k in range(16):
                                reduce_max(k, U0 * 16 + g * 16 + k)
                            negate_max(U0 + g)
                            if g < LA - 1:
                                copy_row(U0 + g, slice(g * CT, g * CT + CT))

                        def unit(u, maxed, next_maxed, next_v):
                            U = U0 + u
                            for k in range(AHEAD, 16):
                                if maxed:
                                    reduce_max(k, (U + LA) * 16 + k)
                                if k == 4 and (maxed or u == MAXED):
                                    copy_row(U + LA - 1, bass.ds((u + LA - 1) * CT, CT))
                                if k == 8 and next_v:
                                    copy_v(u + CH)
                            if maxed:
                                negate_max(U + LA)
                            dve.wait_ge(p_free, (U + 1) * KB + 4)
                            dve.tensor_copy(osb[:, :], OB[:, :]).then_inc(o_free, 1)
                            if next_maxed:
                                reduce_max(0, (U + LA + 1) * 16)
                            dve.wait_ge(o_free, U + 9)
                            dve.reciprocal(rden[:, 0:CT // 2], osb[DH:P, 0:CT // 2]).then_inc(o_rec, 1)
                            if next_maxed:
                                reduce_max(1, (U + LA + 1) * 16 + 1)
                            dve.reciprocal(rden[:, CT // 2:CT], osb[DH:P, CT // 2:CT]).then_inc(o_rec, 1)
                            if next_maxed:
                                reduce_max(2, (U + LA + 1) * 16 + 2)
                            dve.wait_ge(o_rec, 2 * U + 2)
                            dve.tensor_tensor(onorm[:, :], osb[0:DH, :], rden[:, :], ALU.mult).then_inc(o_norm, 1)
                            if next_maxed:
                                reduce_max(3, (U + LA + 1) * 16 + 3)
                            dve.wait_ge(o_norm, U + 1)
                            cols = bass.ds(u * CT, CT)
                            dve.tensor_copy(qf[0:DH, cols], onorm[:, :]).then_inc(o_high, 1)
                            dve.wait_ge(o_high, U + 1)
                            dve.tensor_tensor(qf[DH:P, cols], onorm[:, :], qf[0:DH, cols], ALU.subtract)

                        for k in range(AHEAD):
                            reduce_max(k, (U0 + LA) * 16 + k)
                        with dve.Fori(0, UNITS - CH) as u:
                            unit(u, True, True, True)
                        for u in range(UNITS - CH, UNITS):
                            unit(u, u < MAXED, u + 1 < MAXED, False)

            with ExitStack() as mlp:
                x2 = sb(mlp, "x2", [P, KB * D], F32)
                x2th = sb(mlp, "x2th", [P, DC, N], F16)
                x2tl = sb(mlp, "x2tl", [P, DC, N], F16)

                with ExitStack() as ph:
                    wh = {n: sb(ph, f"dwh_{n}", [P, DC, D], F16) for n in ("xq", "xo")}
                    wl = {n: sb(ph, f"dwl_{n}", [P, DC, D], F16) for n in ("xq", "xo")}
                    wh["o"] = sb(ph, "dwh_o", [P, H, D], F16)
                    wl["o"] = sb(ph, "dwl_o", [P, H, D], F16)
                    kbh = sb(ph, "kbh", [P, DC, 4 * CTX], F16)
                    kbl = sb(ph, "kbl", [P, DC, 4 * CTX], F16)
                    vxh = sb(ph, "vxh", [P, D], F16)
                    vxl = sb(ph, "vxl", [P, D], F16)
                    bo_b = sb(ph, "bo_b", [P, D], F32)
                    xbq_b = sb(ph, "xbq_b", [P, D], F32)
                    xbo_b = sb(ph, "xbo_b", [P, D], F32)

                    with ExitStack() as cp:
                        stage = [sb(cp, f"stage_c{i}", [P, 2, D], F32) for i in range(2)]
                        for n_ in ("xk", "xv"):
                            wh[n_] = sb(cp, f"cwh_{n_}", [P, DC, D], F16)
                            wl[n_] = sb(cp, f"cwl_{n_}", [P, DC, D], F16)
                        cx = sb(cp, "cx", [P, D], F32)
                        cth = sb(cp, "cth", [P, D], F16)
                        ctl = sb(cp, "ctl", [P, D], F16)
                        kx = sb(cp, "kx", [P, D], F32)
                        vx = sb(cp, "vx", [P, D], F32)
                        xbk_b = sb(cp, "xbk_b", [P, D], F32)
                        xbv_b = sb(cp, "xbv_b", [P, D], F32)
                        block = cp.enter_context(nc.Block())

                        @block.sync
                        def _(sp):
                            sp.dma_start(cx[:, :], ctx_rows[bass.ds(b * CTX, CTX), :]).then_inc(c_in, 16)
                            load_pieces(sp, b, PIECES_P3[:4], stage, source)
                            for dst, src in ((xbk_b, xb_k), (xbv_b, xb_v), (bo_b, b_o), (xbq_b, xb_q), (xbo_b, xb_o)):
                                sp.dma_start(dst[:, :], bcast(src)).then_inc(c_in, 16)
                            load_pieces(sp, b, PIECES_P3[4:], stage, source)
                            sp.wait_ge(c_in, b * 96 + 96)
                            sp.nop(nofuse=True)

                        @block.gpsimd
                        def _(pool):
                            pool.memset(kbh[:, :, :], 0.0).then_inc(c_zero, 1)
                            pool.memset(kbl[:, :, :], 0.0).then_inc(c_zero, 1)

                        @block.tensor
                        def _(pe):
                            def transposes(src):
                                for d in range(DC):
                                    mm = pe.transpose(banks[0][:, d * P:(d + 1) * P], src[:, d * P:(d + 1) * P],
                                                      ident[:, :])
                                mm.then_inc(c_t, 1)

                            def project(name, bank):
                                mm3(pe, bank[:, :], lambda d: cth[:, d * P:(d + 1) * P],
                                    lambda d: ctl[:, d * P:(d + 1) * P], lambda d: wh[name][:, d, :],
                                    lambda d: wl[name][:, d, :]).then_inc(c_mm, 1)

                            pe.wait_ge(c_in, b * 96 + 96)
                            transposes(cx)
                            pe.wait_ge(c_l, b * 6 + 1)
                            pe.wait_ge(w_split, pieces_split(b, PIECES_P3[:4]))
                            project("xk", banks[1])
                            project("xv", banks[2])
                            pe.wait_ge(c_tok, b * 2 + 1)
                            transposes(kx)

                        @block.scalar
                        def _(act):
                            split_high(act, b, PIECES_P3[:4], stage, wh)
                            act.wait_ge(c_t, b * 2 + 1)
                            act.activation(cth[:, :], banks[0][:, :], ACT.Copy).then_inc(c_h, 1)
                            act.wait_ge(c_zero, b * 2 + 2)
                            act.wait_ge(c_t, b * 2 + 2)
                            for a in range(4):
                                act.activation(kbh[32 * a:32 * a + 32, :, a * CTX:(a + 1) * CTX],
                                               banks[0][32 * a:32 * a + 32, :].rearrange("p (c n) -> p c n", c=DC),
                                               ACT.Copy).then_inc(c_h, 1)
                            act.wait_ge(c_tok, b * 2 + 2)
                            act.activation(vxh[:, :], vx[:, :], ACT.Copy).then_inc(c_h, 1)
                            split_high(act, b, PIECES_P3[4:], stage, wh)

                        @block.vector
                        def _(dve):
                            split_low(dve, b, PIECES_P3[:4], stage, wh, wl)
                            dve.wait_ge(c_h, b * 6 + 1)
                            dve.tensor_tensor(ctl[:, :], banks[0][:, :], cth[:, :], ALU.subtract).then_inc(c_l, 1)
                            for i, (dst, bias) in enumerate(((kx, xbk_b), (vx, xbv_b))):
                                dve.wait_ge(c_mm, b * 2 + i + 1)
                                dve.wait_ge(c_in, b * 96 + 96)
                                dve.scalar_tensor_tensor(out=dst[:, :], in0=banks[1 + i][:, :], scalar=INV_WS,
                                                         in1=bias[:, :], op0=ALU.mult, op1=ALU.add).then_inc(c_tok, 1)
                            for a in range(4):
                                dve.wait_ge(c_h, b * 6 + 2 + a)
                                part = slice(32 * a, 32 * a + 32)
                                dve.tensor_tensor(kbl[part, :, a * CTX:(a + 1) * CTX],
                                                  banks[0][part, :].rearrange("p (c n) -> p c n", c=DC),
                                                  kbh[part, :, a * CTX:(a + 1) * CTX], ALU.subtract).then_inc(c_l, 1)
                            dve.wait_ge(c_h, b * 6 + 6)
                            dve.tensor_tensor(vxl[:, :], vx[:, :], vxh[:, :], ALU.subtract).then_inc(c_l, 1)
                            split_low(dve, b, PIECES_P3[4:], stage, wh, wl)

                    with ExitStack() as tp:
                        xr = sb(tp, "xr", [P, TPC, D], F32)
                        tok = sb(tp, "tok", [P, TPC, D], F32)
                        th = sb(tp, "th", [P, TPC, D], F16)
                        tl = sb(tp, "tl", [P, TPC, D], F16)
                        px = sb(tp, "px", [P, 2, 8 * CTX], F32)
                        pth = sb(tp, "pth", [P, 2, 8 * CTX], F16)
                        ptl = sb(tp, "ptl", [P, 2, 8 * CTX], F16)
                        mx = sb(tp, "mx", [P, 2, 8], F32)
                        nmx = sb(tp, "nmx", [P, 2, 8], F32)
                        sm = sb(tp, "sm", [P, TPC, XH], F32)
                        rsm = sb(tp, "rsm", [P, TPC, XH], F32)
                        st = sb(tp, "st_d", [P, TPC, 6], F32)
                        mv = sb(tp, "mv_d", [P, TPC, 2], F32)
                        rs = sb(tp, "rs_d", [P, 2, TPC], F32)
                        TB = banks[0:2]
                        PB = banks[2:4]
                        SU = [banks[4:6], banks[6:8]]
                        block = tp.enter_context(nc.Block())

                        @block.sync
                        def _(sp):
                            with sp.Fori(0, CH) as c:
                                n = b * CH + c
                                for j in range(TPC):
                                    sp.wait_ge(d_x2, n * TPC + j + 1)
                                    sp.dma_start(xr[:, j, :], x_rows[bass.ds(n * CT + j * P, P), :])\
                                        .then_inc(d_x_in[j], 16)

                        @block.gpsimd
                        def _(pool):
                            with pool.Fori(0, CH) as c:
                                n = b * CH + c

                                def norm_scale(s, j):
                                    i = n * 8 + s * TPC + j
                                    pool.wait_ge(d_stat, i + 1)
                                    pool.nop(nofuse=True)
                                    pool.tensor_scalar(rs[:, 0, j:j + 1], mv[:, j, 1:2], LN_EPS, None, ALU.add)\
                                        .then_inc(d_var, 1)
                                    pool.wait_ge(d_var, i + 1)
                                    pool.tensor_tensor(rs[:, 1, j:j + 1], rs[:, 0, j:j + 1], neg_half[:, 0:1], ALU.pow)\
                                        .then_inc(d_rs, 1)

                                for j in range(TPC):
                                    pool.wait_ge(d_x_in[j], n * 16 + 16)
                                    pool.tensor_tensor(xr[:, j, :], xr[:, j, :], bo_b[:, :], ALU.add).then_inc(d_xb, 1)
                                for j in range(TPC):
                                    norm_scale(0, j)
                                for j in range(TPC):
                                    pool.wait_ge(d_tok, n * 16 + j + 1)
                                    pool.tensor_tensor(xr[:, j, :], xr[:, j, :], xbo_b[:, :], ALU.add)\
                                        .then_inc(d_xb2, 1)
                                for j in range(TPC):
                                    norm_scale(1, j)

                        @block.tensor
                        def _(pe):
                            with pe.Fori(0, CH) as c:
                                n = b * CH + c

                                def transposes(s, j):
                                    i = n * 16 + s * TPC + j
                                    pe.wait_ge(d_tok, i + 1)
                                    pe.wait_ge(d_tl, i + 1)
                                    for d in range(DC):
                                        mm = pe.transpose(TB[j % 2][:, d * P:(d + 1) * P], tok[:, j, d * P:(d + 1) * P],
                                                          ident[:, :])
                                    mm.then_inc(d_t_done, 1)

                                def project(s, j, name):
                                    pe.wait_ge(d_tl, n * 16 + s * TPC + j + 3)
                                    mm3(pe, PB[j % 2][:, :], lambda d: th[:, j, d * P:(d + 1) * P],
                                        lambda d: tl[:, j, d * P:(d + 1) * P], lambda d: wh[name][:, d, :],
                                        lambda d: wl[name][:, d, :]).then_inc(d_mm, 1)

                                pe.wait_ge(d_x2, n * TPC + TPC)
                                for j in range(TPC):
                                    if j >= 2:
                                        pe.wait_ge(d_x1, n * TPC + j - 1)
                                    o_cols = bass.ds(c * CT + j * P, P)
                                    for h in range(H):
                                        pe.matmul(PB[j % 2][:, :], q_hh[:, h, o_cols], wh["o"][:, h, :],
                                                  start=(h == 0), stop=False)
                                        mm = pe.matmul(PB[j % 2][:, :], q_hh[:, h, o_cols], wl["o"][:, h, :],
                                                       start=False, stop=(h == H - 1))
                                    mm.then_inc(d_mm, 1)
                                transposes(0, 0)
                                for j in range(TPC):
                                    if j + 1 < TPC:
                                        transposes(0, j + 1)
                                    if j < 2:
                                        pe.wait_ge(d_x1, n * TPC + j + 3)
                                    else:
                                        pe.wait_ge(d_tok, n * 16 + TPC + j - 1)
                                    project(0, j, "xq")
                                for j in range(TPC):
                                    transposes(1, j)

                                def cross_scores(v):
                                    j, half = v // 2, v % 2
                                    pe.wait_ge(d_tl, n * 16 + TPC + j + 3)
                                    if v >= 2:
                                        pe.wait_ge(d_ex, n * 8 + v - 1)
                                    for i in range(2):
                                        d = 2 * half + i
                                        bank = SU[v % 2][i][:, :]
                                        qh, ql = th[:, j, d * P:(d + 1) * P], tl[:, j, d * P:(d + 1) * P]
                                        pe.matmul(bank, qh, kbh[:, d, :], start=True, stop=False)
                                        pe.matmul(bank, qh, kbl[:, d, :], start=False, stop=False)
                                        mm = pe.matmul(bank, ql, kbh[:, d, :], start=False, stop=True)
                                    mm.then_inc(d_s_done, 1)

                                def transpose_probs(v):
                                    pe.wait_ge(d_ex, n * 8 + v + 1)
                                    pe.wait_ge(d_ptl, (n * 8 + v) * 2 + 2)
                                    for hh in range(8):
                                        mm = pe.transpose(PB[hh // 4][:, hh % 4 * P:hh % 4 * P + P],
                                                          px[:, v % 2, hh * CTX:(hh + 1) * CTX], ident[:, :])
                                    mm.then_inc(d_pt_done, 1)

                                def cross_values(v):
                                    j, half = v // 2, v % 2
                                    pe.wait_ge(d_ptl, (n * 8 + v) * 2 + 4)
                                    if j >= 2 and half == 0:
                                        pe.wait_ge(d_tok, n * 16 + 2 * TPC + j - 1)
                                    for hh in range(8):
                                        cols = slice((8 * half + hh) * XD, (8 * half + hh + 1) * XD)
                                        ph_, pl_ = (t[:, v % 2, hh * CTX:(hh + 1) * CTX] for t in (pth, ptl))
                                        pe.matmul(TB[j % 2][:, cols], ph_, vxh[:, cols], start=True, stop=False)
                                        pe.matmul(TB[j % 2][:, cols], ph_, vxl[:, cols], start=False, stop=False)
                                        mm = pe.matmul(TB[j % 2][:, cols], pl_, vxh[:, cols], start=False, stop=True)
                                    mm.then_inc(d_av_done, 1)

                                cross_scores(0)
                                pe.wait_ge(d_tl, n * 16 + 2 * TPC + 2)
                                for v in range(8):
                                    if v + 1 < 8:
                                        cross_scores(v + 1)
                                    transpose_probs(v)
                                    if v:
                                        cross_values(v - 1)
                                cross_values(7)
                                pe.wait_ge(d_tok, n * 16 + 2 * TPC + 3)
                                transposes(2, 0)
                                pe.wait_ge(d_tok, n * 16 + 2 * TPC + 4)
                                for j in range(TPC):
                                    if j + 1 < TPC:
                                        transposes(2, j + 1)
                                    if j >= 2:
                                        pe.wait_ge(d_x2, n * TPC + j + 3)
                                    project(2, j, "xo")
                                for j in range(TPC):
                                    transposes(3, j)

                        @block.scalar
                        def _(act):
                            with act.Fori(0, CH) as c:
                                n = b * CH + c

                                def high(s, j, dst):
                                    act.wait_ge(d_t_done, n * 16 + s * TPC + j + 1)
                                    act.activation(dst, TB[j % 2][:, :], ACT.Copy).then_inc(d_th, 1)

                                for s in range(2):
                                    for j in range(TPC):
                                        high(s, j, th[:, j, :])

                                def exponentials(v):
                                    act.wait_ge(d_nmx, n * 8 + v + 1)
                                    act.wait_ge(d_pt_done, n * 8 + v + 1)
                                    for hh in range(8):
                                        ex = act.activation(
                                            px[:, v % 2, hh * CTX:(hh + 1) * CTX],
                                            SU[v % 2][hh // 4][:, hh % 4 * CTX:(hh % 4 + 1) * CTX], ACT.Exp,
                                            bias=nmx[:, v % 2, hh:hh + 1], scale=XSCALE,
                                            accum_out=sm[:, v // 2, 8 * (v % 2) + hh:8 * (v % 2) + hh + 1])
                                    ex.then_inc(d_ex, 1)

                                def probs_high(v):
                                    act.wait_ge(d_pt_done, n * 8 + v + 3)
                                    for i in range(2):
                                        act.activation(pth[:, v % 2, i * 512:i * 512 + 512], PB[i][:, :], ACT.Copy)\
                                            .then_inc(d_pth, 1)

                                exponentials(0)
                                for v in range(8):
                                    if v + 1 < 8:
                                        exponentials(v + 1)
                                    probs_high(v)
                                for j in range(TPC):
                                    high(2, j, th[:, j, :])
                                for j in range(TPC):
                                    high(3, j, x2th[:, :, bass.ds(c * CT + j * P, P)])

                        @block.vector
                        def _(dve):
                            with dve.Fori(0, CH) as c:
                                n = b * CH + c

                                def low(s, j, dst, high):
                                    dve.wait_ge(d_th, n * 16 + s * TPC + j + 1)
                                    dve.tensor_tensor(dst, TB[j % 2][:, :], high, ALU.subtract).then_inc(d_tl, 1)

                                def stats(s, j, src):
                                    i = n * 8 + s * TPC + j
                                    dve.bn_stats(st[:, j, :], src).then_inc(d_bn, 1)
                                    dve.wait_ge(d_bn, i + 1)
                                    dve.nop(nofuse=True)
                                    dve.bn_aggr(mv[:, j, :], st[:, j, :]).then_inc(d_stat, 1)

                                def norm(s, j, src):
                                    dve.wait_ge(d_rs, n * 8 + s * TPC + j + 1)
                                    dve.tensor_scalar(tok[:, j, :], src, mv[:, j, 0:1], rs[:, 1, j:j + 1],
                                                      ALU.subtract, ALU.mult).then_inc(d_tok, 1)

                                for j in range(TPC):
                                    dve.wait_ge(d_xb, n * TPC + j + 1)
                                    dve.wait_ge(d_mm, n * 12 + j + 1)
                                    dve.scalar_tensor_tensor(out=xr[:, j, :], in0=PB[j % 2][:, :], scalar=INV_WS,
                                                             in1=xr[:, j, :], op0=ALU.mult, op1=ALU.add)\
                                        .then_inc(d_x1, 1)
                                    dve.wait_ge(d_x1, n * TPC + j + 1)
                                    dve.nop(nofuse=True)
                                    stats(0, j, xr[:, j, :])
                                    if j:
                                        norm(0, j - 1, xr[:, j - 1, :])
                                norm(0, TPC - 1, xr[:, TPC - 1, :])
                                low(0, 0, tl[:, 0, :], th[:, 0, :])
                                for j in range(TPC):
                                    if j + 1 < TPC:
                                        low(0, j + 1, tl[:, j + 1, :], th[:, j + 1, :])
                                    dve.wait_ge(d_mm, n * 12 + TPC + j + 1)
                                    dve.scalar_tensor_tensor(out=tok[:, j, :], in0=PB[j % 2][:, :], scalar=INV_WS,
                                                             in1=xbq_b[:, :], op0=ALU.mult, op1=ALU.add)\
                                        .then_inc(d_tok, 1)
                                for j in range(TPC):
                                    low(1, j, tl[:, j, :], th[:, j, :])

                                def cross_max(v):
                                    u = n * 8 + v
                                    dve.wait_ge(d_s_done, u + 1)
                                    for i in range(2):
                                        dve.tensor_reduce(mx[:, v % 2, 4 * i:4 * i + 4],
                                                          SU[v % 2][i][:, :].rearrange("p (h k) -> p h k", k=CTX),
                                                          AX_X, ALU.max).then_inc(d_mx, 1)
                                    dve.wait_ge(d_mx, u * 2 + 2)
                                    dve.tensor_scalar(nmx[:, v % 2, :], mx[:, v % 2, :], -XSCALE, None, ALU.mult)\
                                        .then_inc(d_nmx, 1)

                                def probs_low(v):
                                    for i in range(2):
                                        dve.wait_ge(d_pth, (n * 8 + v) * 2 + i + 1)
                                        dve.tensor_tensor(ptl[:, v % 2, i * 512:i * 512 + 512], PB[i][:, :],
                                                          pth[:, v % 2, i * 512:i * 512 + 512], ALU.subtract)\
                                            .then_inc(d_ptl, 1)

                                def output(j):
                                    dve.wait_ge(d_ex, n * 8 + 2 * j + 2)
                                    dve.reciprocal(rsm[:, j, :], sm[:, j, :]).then_inc(d_rec, 1)
                                    dve.wait_ge(d_rec, n * TPC + j + 1)
                                    dve.wait_ge(d_av_done, n * 8 + 2 * j + 2)
                                    dve.tensor_tensor(tok[:, j, :].rearrange("p (h d) -> p h d", d=XD),
                                                      TB[j % 2][:, :].rearrange("p (h d) -> p h d", d=XD),
                                                      rsm[:, j, :].rearrange("p (h a) -> p h a", a=1)
                                                      .broadcast_to([P, XH, XD]), ALU.mult).then_inc(d_tok, 1)

                                cross_max(0)
                                for v in range(8):
                                    if v + 1 < 8:
                                        cross_max(v + 1)
                                    probs_low(v)
                                    if v >= 2 and v % 2 == 0:
                                        output(v // 2 - 1)
                                output(TPC - 1)
                                low(2, 0, tl[:, 0, :], th[:, 0, :])
                                for j in range(TPC):
                                    cols = bass.ds(c * (TPC * D) + j * D, D)
                                    if j + 1 < TPC:
                                        low(2, j + 1, tl[:, j + 1, :], th[:, j + 1, :])
                                    dve.wait_ge(d_xb2, n * TPC + j + 1)
                                    dve.wait_ge(d_mm, n * 12 + 2 * TPC + j + 1)
                                    dve.scalar_tensor_tensor(out=x2[:, cols], in0=PB[j % 2][:, :], scalar=INV_WS,
                                                             in1=xr[:, j, :], op0=ALU.mult, op1=ALU.add)\
                                        .then_inc(d_x2, 1)
                                    dve.wait_ge(d_x2, n * TPC + j + 5)
                                    dve.nop(nofuse=True)
                                    stats(1, j, x2[:, cols])
                                for j in range(TPC):
                                    norm(1, j, x2[:, bass.ds(c * (TPC * D) + j * D, D)])
                                for j in range(TPC):
                                    toks = bass.ds(c * CT + j * P, P)
                                    low(3, j, x2tl[:, :, toks], x2th[:, :, toks])

                with ExitStack() as ph:
                    stage = [sb(ph, f"stage_f{i}", [P, 2, D], F32) for i in range(2)]
                    names = ("w10", "w11", "w20", "w21")
                    wh = {n_: sb(ph, f"fwh_{n_}", [P, DC, D], F16) for n_ in names}
                    wl = {n_: sb(ph, f"fwl_{n_}", [P, DC, D], F16) for n_ in names}
                    col = sb(ph, "col", [P, DC], F32)
                    sc = sb(ph, "sc", [1, E], F32)
                    best = sb(ph, "best", [1, 8], F32)
                    idx = sb(ph, "idx", [1, 8], U32)
                    b1c = sb(ph, "b1c", [P, 2, DC], F32)
                    b2r = sb(ph, "b2r", [P, 2, D], F32)
                    b2s = sb(ph, "b2s", [P, 2, D], F32)
                    g32 = sb(ph, "g32", [P, 2, CT], F32)
                    gh = sb(ph, "gh", [P, 2, DC, CT], F16)
                    gl = sb(ph, "gl", [P, 2, DC, CT], F16)
                    yt = sb(ph, "yt_f", [P, 2, D], F32)
                    F1 = banks[0:2]
                    F2 = banks[2:4]
                    block = ph.enter_context(nc.Block())

                    @block.sync
                    def _(sp):
                        sp.wait_ge(r_idx, b + 1)
                        sp.nop(nofuse=True)
                        expert = [sp.value_load(idx[0:1, k:k + 1], min_val=0, max_val=E - 1) for k in range(2)]

                        def rows_of(w, e):
                            v = w[bass.ds(e, 1), :, :].rearrange("a (c p) n -> p (a c) n", p=P)
                            return [[v[64 * half:64 * half + 64, 2 * i:2 * i + 2, :] for half in range(2)]
                                    for i in range(2)]

                        src = {"w10": rows_of(w1, expert[0]), "w11": rows_of(w1, expert[1]),
                               "w20": rows_of(w2, expert[0]), "w21": rows_of(w2, expert[1])}
                        for k in range(2):
                            sp.dma_start(b1c[:, k, :], b1[bass.ds(expert[k], 1), :, :].rearrange("a p c -> p (a c)"))\
                                .then_inc(f_b, 16)
                            sp.dma_start(b2r[:, k, :], b2[bass.ds(expert[k], 1), :].broadcast_to([P, D])).then_inc(f_b, 16)
                        load_pieces(sp, b, PIECES_P4, stage, src)
                        with sp.Fori(0, CH) as c:
                            n = b * CH + c
                            for j in range(TPC):
                                sp.wait_ge(f_y, n * TPC + j + 3)
                                sp.dma_start(out_rows[bass.ds(n * CT + j * P, P), :], yt[:, j % 2, :])\
                                    .then_inc(y_out[j % 2], 16)
                        for s in range(2):
                            sp.wait_ge(y_out[s], (b + 1) * (CH * 32) + 16)
                        sp.nop(nofuse=True)

                    @block.gpsimd
                    def _(pool):
                        pool.wait_ge(f_b2, 2 * b + 2)
                        pool.nop(nofuse=True)
                        with pool.Fori(0, CH) as c:
                            n = b * CH + c
                            for j in range(TPC):
                                cols = bass.ds(c * (TPC * D) + j * D, D)
                                pool.tensor_tensor(x2[:, cols], x2[:, cols], b2s[:, 1, :], ALU.add).then_inc(f_xb, 1)

                    @block.tensor
                    def _(pe):
                        pe.wait_ge(r_col, b + 1)
                        for d in range(DC):
                            mm = pe.matmul(F1[0][0:1, 0:E], col[:, d:d + 1], wr_sb[:, d, :], start=(d == 0),
                                           stop=(d == DC - 1))
                        mm.then_inc(r_mm, 1)
                        pe.wait_ge(r_sc, b + 1)
                        pe.wait_ge(w_split, pieces_split(b, PIECES_P4))
                        pe.nop(nofuse=True)
                        with pe.Fori(0, CH) as c:
                            n = b * CH + c
                            toks = bass.ds(c * CT, CT)
                            for w in range(8):
                                k, ec = w // DC, w % DC
                                pe.wait_ge(f_g, n * 8 + w + 1)
                                ecols = slice(ec * P, ec * P + P)
                                mm3(pe, F1[w % 2][:, :], lambda d: wh[f"w1{k}"][:, d, ecols],
                                    lambda d: wl[f"w1{k}"][:, d, ecols], lambda d: x2th[:, d, toks],
                                    lambda d: x2tl[:, d, toks]).then_inc(f1_done, 1)
                            for j in range(TPC):
                                pe.wait_ge(f_y, n * TPC + j + 1)
                                cols = slice(j * P, j * P + P)
                                for w in range(8):
                                    k, ec = w // DC, w % DC
                                    if j == 0:
                                        pe.wait_ge(f_gl, n * 8 + w + 1)
                                    bank = F2[j % 2][:, :]
                                    pe.matmul(bank, gh[:, k, ec, cols], wh[f"w2{k}"][:, ec, :], start=(w == 0),
                                              stop=False)
                                    pe.matmul(bank, gh[:, k, ec, cols], wl[f"w2{k}"][:, ec, :], start=False,
                                              stop=False)
                                    mm = pe.matmul(bank, gl[:, k, ec, cols], wh[f"w2{k}"][:, ec, :], start=False,
                                                   stop=(w == 7))
                                mm.then_inc(f2_done, 1)

                    @block.scalar
                    def _(act):
                        split_high(act, b, PIECES_P4, stage, wh)
                        act.wait_ge(f_b, b * 64 + 64)
                        act.nop(nofuse=True)
                        act.preload_act_table(ACT.Gelu)
                        with act.Fori(0, CH) as c:
                            n = b * CH + c
                            for w in range(8):
                                k, ec = w // DC, w % DC
                                act.wait_ge(f1_done, n * 8 + w + 1)
                                if w >= 2:
                                    act.wait_ge(f_gl, n * 8 + w - 1)
                                act.activation(g32[:, w % 2, :], F1[w % 2][:, :], ACT.Gelu, bias=b1c[:, k, ec:ec + 1],
                                               scale=INV_WS).then_inc(f_g, 1)

                    @block.vector
                    def _(dve):
                        dve.tensor_tensor(col[:, :], x2th[:, :, 0], x2tl[:, :, 0], ALU.add).then_inc(r_col, 1)
                        dve.wait_ge(r_mm, b + 1)
                        dve.tensor_tensor(sc[:, :], F1[0][0:1, 0:E], br_sb[:, :], ALU.add).then_inc(r_sc, 1)
                        dve.wait_ge(r_sc, b + 1)
                        dve.nop(nofuse=True)
                        dve.max(best[:, :], sc[:, :]).then_inc(r_top, 1)
                        dve.wait_ge(r_top, b + 1)
                        dve.nop(nofuse=True)
                        dve.max_index(idx[:, :], best[:, :], sc[:, :]).then_inc(r_idx, 1)
                        split_low(dve, b, PIECES_P4, stage, wh, wl)
                        dve.wait_ge(f_b, b * 64 + 64)
                        dve.tensor_tensor(b2s[:, 0, :], b2r[:, 0, :], b2r[:, 1, :], ALU.add).then_inc(f_b2, 1)
                        dve.wait_ge(f_b2, 2 * b + 1)
                        dve.tensor_scalar(b2s[:, 1, :], b2s[:, 0, :], 0.5, None, ALU.mult).then_inc(f_b2, 1)
                        with dve.Fori(0, CH) as c:
                            n = b * CH + c
                            dve.wait_ge(f2_done, n * TPC + 4)
                            for w in range(8):
                                k, ec = w // DC, w % DC
                                dve.wait_ge(f_g, n * 8 + w + 3)
                                dve.tensor_copy(gh[:, k, ec, :], g32[:, w % 2, :]).then_inc(f_gh, 1)
                                dve.wait_ge(f_gh, n * 8 + w + 1)
                                dve.tensor_tensor(gl[:, k, ec, :], g32[:, w % 2, :], gh[:, k, ec, :], ALU.subtract)\
                                    .then_inc(f_gl, 1)
                            for j in range(TPC):
                                cols = bass.ds(c * (TPC * D) + j * D, D)
                                dve.wait_ge(f2_done, n * TPC + j + 5)
                                dve.wait_ge(f_xb, n * TPC + j + 1)
                                dve.wait_ge(y_out[j % 2], n * 32 + 16 * (j // 2) + 16)
                                dve.scalar_tensor_tensor(out=yt[:, j % 2, :], in0=F2[j % 2][:, :], scalar=0.5 * INV_WS,
                                                         in1=x2[:, cols], op0=ALU.mult, op1=ALU.add).then_inc(f_y, 1)


_INS = ["x", "ctx_1024", "L0_attn_ln_gamma", "L0_attn_ln_beta", "L0_attn_q_gamma", "L0_attn_k_gamma", "L0_attn_w_q",
        "L0_attn_w_k", "L0_attn_w_v", "L0_attn_w_o", "L0_attn_b_o", "L0_xattn_Wq", "L0_xattn_bq", "L0_xattn_Wk",
        "L0_xattn_bk", "L0_xattn_Wv", "L0_xattn_bv", "L0_xattn_Wo", "L0_xattn_bo", "L0_ffn_Wr", "L0_ffn_br",
        "L0_ffn_W1", "L0_ffn_b1", "L0_ffn_W2", "L0_ffn_b2"]
_TRANSPOSED = ("L0_attn_w_q", "L0_attn_w_k", "L0_attn_w_v", "L0_attn_w_o")


def kernel(**inputs):
    import numpy as _np
    import concourse.bacc as _bacc
    from concourse import mybir as _mybir
    from concourse.bass_utils import run_bass_kernel_spmd as _run

    nc = _bacc.Bacc("TRN2", target_bir_lowering=False, num_devices=1)
    arrays, args = {}, []
    for name in _INS:
        a = _np.asarray(inputs[name])
        if name == "L0_ffn_b1":
            a = a.reshape(a.shape[0], -1, P).transpose(0, 2, 1)
        a = _np.ascontiguousarray(a.T if name in _TRANSPOSED else a)
        arrays[f"in_{name}"] = a
        args.append(nc.dram_tensor(f"in_{name}", a.shape, _mybir.dt.from_np(a.dtype), kind="ExternalInput").ap())
    shape = inputs["x"].shape
    y = nc.dram_tensor("out_0", shape, _mybir.dt.from_np(_np.dtype("float32")), kind="ExternalOutput").ap()
    decoder_layer(nc, *args, y)
    r = _run(nc, [arrays], core_ids=[0])
    return r.results[0]["out_0"]
```

```python
from contextlib import ExitStack

import concourse.bass as bass
from concourse import mybir

F32 = mybir.dt.float32
F16 = mybir.dt.float16
U32 = mybir.dt.uint32
ALU = mybir.AluOpType
ACT = mybir.ActivationFunctionType
AX_X = mybir.AxisListType.X

P = 128
WS = 64.0
INV_WS = 1.0 / WS
PSHIFT = 6.93
LN_EPS = 1e-5
RMS_EPS = 1e-8


def decoder_layer(nc, x, ctx_in, ln_g, ln_b, q_gamma, k_gamma, w_q, w_k, w_v, w_o, b_o,
                  xw_q, xb_q, xw_k, xb_k, xw_v, xb_v, xw_o, xb_o, wr, br, w1, b1, w2, b2, out):
    B, N, D = x.shape
    DC = D // P
    DH = q_gamma.shape[0]
    H = D // DH
    TPC = 4
    CT = TPC * P
    CH = N // CT
    KB = N // P
    CTX = ctx_in.shape[1]
    XH = 16
    XD = D // XH
    E = wr.shape[1]
    XSCALE = float(XD) ** -0.5
    assert D == 512 and DH == 64 and CTX == P and N == 2048 and KB == 16

    x_rows = x.rearrange("b n d -> (b n) d")
    out_rows = out.rearrange("b n d -> (b n) d")
    ctx_rows = ctx_in.rearrange("b n d -> (b n) d")

    def by_rows(w):
        v = w.rearrange("(c p) n -> p c n", p=P)
        return [[v[0:64, 2 * i:2 * i + 2, :], v[64:128, 2 * i:2 * i + 2, :]] for i in range(2)]

    def by_head(w):
        v = w.rearrange("(h d) n -> d h n", d=DH)
        return [[v[:, 2 * i:2 * i + 2, :]] * 2 for i in range(4)]

    PIECES_P1 = [(n, i) for n in ("q", "k", "v") for i in range(2)]
    PIECES_P3 = [("o", i) for i in range(4)] + [(n, i) for n in ("xk", "xv", "xq", "xo") for i in range(2)]
    PIECES_P4 = [(n, i) for n in ("w10", "w11", "w20", "w21") for i in range(2)]
    PIECES = PIECES_P1 + PIECES_P3 + PIECES_P4
    NP = len(PIECES)
    PHASES = ((PIECES_P1, 6), (PIECES_P3, 4), (PIECES_P4, 4))
    use, taken = [], [0] * 6
    for pieces_, slots in PHASES:
        for k_ in range(len(pieces_)):
            taken[k_ % slots] += 1
            use.append((k_ % slots, taken[k_ % slots], slots))
    source = {"q": by_rows(w_q), "k": by_rows(w_k), "v": by_rows(w_v), "xk": by_rows(xw_k), "xv": by_rows(xw_v),
              "o": by_head(w_o), "xq": by_rows(xw_q), "xo": by_rows(xw_o)}

    with ExitStack() as top:
        def sem(name):
            return top.enter_context(nc.semaphore(name))

        def sb(ctx, name, shape, dt):
            return ctx.enter_context(nc.sbuf_tensor(name, shape, dt))

        banks = [top.enter_context(nc.psum_tensor(f"bank{i}", [P, 512], F32)) for i in range(8)]

        ident = sb(top, "ident", [P, P], F32)
        ident16 = sb(top, "ident16", [P, P], F16)
        neg_half = sb(top, "neg_half", [P, 2 * H], F32)
        qg0 = sb(top, "qg0", [P, 1], F32)
        qg = sb(top, "qg", [P, 1], F32)
        kg = sb(top, "kg", [P, 1], F32)
        wr_sb = sb(top, "wr_sb", [P, DC, E], F32)
        br_sb = sb(top, "br_sb", [1, E], F32)
        q_hh = sb(top, "q_hh", [P, H, N], F16)

        s_const = sem("s_const")
        s_pool = sem("s_pool")
        s_setup = sem("s_setup")
        w_loaded = [sem(f"w_loaded{i}") for i in range(6)]
        wh_ready = sem("wh_ready")
        w_split = sem("w_split")

        def bcast(v):
            return v.rearrange("(a n) -> a n", a=1).broadcast_to([P, v.shape[0]])

        def load_pieces(sp, b, pieces, stage, src):
            for piece in pieces:
                w = PIECES.index(piece)
                slot, _, slots = use[w]
                sp.wait_ge(w_split, b * NP + w + 7 - slots)
                for half in range(2):
                    sp.dma_start(stage[slot][64 * half:64 * half + 64, :, :], src[piece[0]][piece[1]][half])\
                        .then_inc(w_loaded[slot], 16)

        def split_high(act, b, pieces, stage, wh):
            for piece in pieces:
                w = PIECES.index(piece)
                slot, nth, _ = use[w]
                act.wait_ge(w_loaded[slot], b * (32 * taken[slot]) + 32 * nth)
                act.activation(wh[piece[0]][:, 2 * piece[1]:2 * piece[1] + 2, :], stage[slot][:, :, :], ACT.Copy,
                               scale=WS).then_inc(wh_ready, 1)

        def split_low(dve, b, pieces, stage, wh, wl):
            for piece in pieces:
                w = PIECES.index(piece)
                part = slice(2 * piece[1], 2 * piece[1] + 2)
                dve.wait_ge(wh_ready, b * NP + w + 1)
                dve.scalar_tensor_tensor(out=wl[piece[0]][:, part, :], in0=stage[use[w][0]][:, :, :], scalar=WS,
                                         in1=wh[piece[0]][:, part, :], op0=ALU.mult, op1=ALU.subtract)\
                    .then_inc(w_split, 1)

        def pieces_split(b, pieces):
            return b * NP + PIECES.index(pieces[-1]) + 7

        def mm3(pe, bank, xh, xl, wh, wl, last=None):
            for c in range(DC):
                pe.matmul(bank, xh(c), wh(c), start=(c == 0), stop=False)
                pe.matmul(bank, xh(c), wl(c), start=False, stop=False)
                mm = pe.matmul(bank, xl(c), wh(c), start=False, stop=(c == DC - 1))
            return mm

        a_const = sem("a_const")
        a_ones = sem("a_ones")
        a_x_in = [sem(f"a_x_in{i}") for i in range(2)]
        a_bn = sem("a_bn")
        a_stat = sem("a_stat")
        a_var = sem("a_var")
        a_rs = sem("a_rs")
        a_y = sem("a_y")
        a_xg = sem("a_xg")
        a_xn = sem("a_xn")
        a_t_done = sem("a_t_done")
        a_xh = sem("a_xh")
        a_xl = sem("a_xl")
        a_q_done = sem("a_q_done")
        a_k_done = sem("a_k_done")
        a_v_done = sem("a_v_done")
        a_sq = sem("a_sq")
        a_vh = sem("a_vh")
        a_v_ready = sem("a_v_ready")
        a_ssq = sem("a_ssq")
        a_ms = sem("a_ms")
        a_pow = sem("a_pow")
        a_rinv = sem("a_rinv")
        a_qk = sem("a_qk")
        a_ht_done = sem("a_ht_done")
        a_hh = sem("a_hh")
        a_ht_free = sem("a_ht_free")
        a_dup = sem("a_dup")
        s_ready = sem("s_ready")
        p_ready = sem("p_ready")
        ph_ready = sem("ph_ready")
        pl_ready = sem("pl_ready")
        p_free = sem("p_free")
        mx_ready = sem("mx_ready")
        mx_free = sem("mx_free")
        gm_ready = sem("gm_ready")
        nm_ready = sem("nm_ready")
        mrow_done = sem("mrow_done")
        m_ready = sem("m_ready")
        o_rec = sem("o_rec")
        o_norm = sem("o_norm")
        o_high = sem("o_high")
        o_free = sem("o_free")
        vs_ones = sem("vs_ones")
        vs_half = sem("vs_half")
        vs_ready = sem("vs_ready")
        c_ctx = sem("c_ctx")
        c_in = sem("c_in")
        c_zero = sem("c_zero")
        c_t = sem("c_t")
        c_h = sem("c_h")
        c_l = sem("c_l")
        c_mm = sem("c_mm")
        c_tok = sem("c_tok")
        d_x_in = [sem(f"d_x_in{i}") for i in range(TPC)]
        d_xb = sem("d_xb")
        d_o_done = sem("d_o_done")
        d_q_done = sem("d_q_done")
        d_xo_done = sem("d_xo_done")
        d_x1 = sem("d_x1")
        d_x2 = sem("d_x2")
        d_xb2 = sem("d_xb2")
        d_bn, d_stat, d_var, d_rs = ([sem(f"{name}{s}") for s in range(2)] for name in ("d_bn", "d_stat", "d_var", "d_rs"))
        d_n0 = sem("d_n0")
        d_n1 = sem("d_n1")
        d_q = sem("d_q")
        d_o = sem("d_o")
        d_t_done = sem("d_t_done")
        d_th = sem("d_th")
        d_tl = sem("d_tl")
        d_s_done = sem("d_s_done")
        d_mx = sem("d_mx")
        d_nmx = sem("d_nmx")
        d_ex = sem("d_ex")
        d_pt_done = sem("d_pt_done")
        d_pth = [sem(f"d_pth{i}") for i in range(2)]
        d_ptl = sem("d_ptl")
        d_av_done = sem("d_av_done")
        d_rec = sem("d_rec")
        r_col = sem("r_col")
        r_mm = sem("r_mm")
        r_sc = sem("r_sc")
        r_top = sem("r_top")
        r_idx = sem("r_idx")
        f_b = sem("f_b")
        f_b2 = sem("f_b2")
        f_xb = sem("f_xb")
        f1_done = sem("f1_done")
        f_g = sem("f_g")
        f_gh = sem("f_gh")
        f_gl = sem("f_gl")
        f2_done = sem("f2_done")
        f_y = sem("f_y")
        y_out = [sem(f"y_out{i}") for i in range(2)]

        with nc.Block() as block:
            @block.sync
            def _(sp):
                for half in (0, DH):
                    sp.dma_start(qg0[half:half + DH, :], q_gamma.rearrange("(d a) -> d a", a=1)).then_inc(s_const, 16)
                    sp.dma_start(kg[half:half + DH, :], k_gamma.rearrange("(d a) -> d a", a=1)).then_inc(s_const, 16)
                sp.dma_start(wr_sb[:, :, :], wr.rearrange("(c p) e -> p c e", p=P)).then_inc(s_const, 16)
                sp.dma_start(br_sb[:, :], br.rearrange("(a e) -> a e", a=1)).then_inc(s_const, 16)
                sp.wait_ge(s_const, 16 * 6)

            @block.gpsimd
            def _(pool):
                pool.memset(ident[:, :], 0.0).then_inc(s_pool, 1)
                pool.memset(neg_half[:, :], -0.5).then_inc(s_pool, 1)
                pool.wait_ge(s_pool, 2)
                pool.affine_select(out=ident[:, :], in_=ident[:, :], compare_op=ALU.not_equal, fill=1.0, base=0,
                                   pattern=[[-1, P]], channel_multiplier=1).then_inc(s_pool, 1)
                for s, credits in ((w_split, 6), (a_y, 2), (a_v_ready, 1), (a_ssq, 1), (a_ht_free, 2), (p_free, 4), (mx_free, 4),
                                   (o_free, 8), (d_x1, 4), (d_tl, 2), (d_pt_done, 2), (d_ptl, 2),
                                   (f_g, 2), (f2_done, 4), (f_y, 2), (y_out[0], 16), (y_out[1], 16)):
                    pool.sem_inc(s, credits)

            @block.vector
            def _(dve):
                dve.wait_ge(s_pool, 3)
                dve.tensor_copy(ident16[:, :], ident[:, :]).then_inc(s_setup, 1)
                dve.wait_ge(s_const, 16 * 6)
                dve.tensor_scalar(qg[:, :], qg0[:, :], float(DH) ** -0.5, None, ALU.mult).then_inc(s_setup, 1)

        with nc.Fori(0, B) as b:
            with ExitStack() as attn:
                q_lm = sb(attn, "q_lm", [P, H, N], F16)
                k_h1 = sb(attn, "k_h1", [P, H, N], F16)
                k_hl = sb(attn, "k_hl", [P, H, N], F16)
                v_h = sb(attn, "v_h", [P, KB * D], F16)
                v_l = sb(attn, "v_l", [P, KB * D], F16)

                with ExitStack() as ph:
                    lng = sb(ph, "lng", [P, D], F32)
                    lnb = sb(ph, "lnb", [P, D], F32)
                    stage = [v[:, :].bitcast(F32).rearrange("p (s c n) -> p s c n", c=2, n=D)[:, i] for v, i in
                             [(v_h, i) for i in range(4)] + [(v_l, i) for i in range(2)]]
                    wh = {n: sb(ph, f"wh_{n}", [P, DC, D], F16) for n in ("q", "k", "v")}
                    wl = {n: sb(ph, f"wl_{n}", [P, DC, D], F16) for n in ("q", "k", "v")}
                    xt = sb(ph, "xt_a", [P, 2, D], F32)
                    yt = sb(ph, "yt_a", [P, 2, D], F32)
                    st = sb(ph, "st_a", [P, 2, 6], F32)
                    mv = sb(ph, "mv_a", [P, 2, 2], F32)
                    rs = sb(ph, "rs_a", [P, 2, 2], F32)
                    xth = sb(ph, "xth_a", [P, 2, D], F16)
                    xtl = sb(ph, "xtl_a", [P, 2, D], F16)
                    ssq = sb(ph, "ssq", [P, 2 * H], F32)
                    ms = sb(ph, "ms", [P, 2 * H], F32)
                    rp = sb(ph, "rp", [P, 2 * H], F32)
                    rinv = sb(ph, "rinv", [P, 2 * H], F32)
                    sq = sb(ph, "sq", [P, D], F32)
                    qkn = sb(ph, "qkn", [P, 2, D], F32)
                    HT = banks[0:2]
                    TB = banks[2]
                    QB = banks[3:5]
                    KBK = banks[5:7]
                    VB = banks[7]
                    block = ph.enter_context(nc.Block())

                    T0 = b * KB

                    def over_tiles(eng, step):
                        step(0, 0, False, True, True)
                        with eng.Fori(0, KB // 2 - 2) as pair:
                            step(pair * 2 + 1, 1, True, True, True)
                            step(pair * 2 + 2, 0, True, True, True)
                        step(KB - 3, 1, True, True, True)
                        step(KB - 2, 0, True, True, False)
                        step(KB - 1, 1, True, False, False)

                    @block.sync
                    def _(sp):
                        def load_x(t, s):
                            sp.wait_ge(a_y, T0 + t + 1)
                            sp.dma_start(xt[:, s, :], x_rows[bass.ds((T0 + t) * P, P), :]).then_inc(a_x_in[s], 16)

                        for t in range(2):
                            load_x(t, t)
                        sp.dma_start(lng[:, :], bcast(ln_g)).then_inc(a_const, 16)
                        sp.dma_start(lnb[:, :], bcast(ln_b)).then_inc(a_const, 16)
                        load_pieces(sp, b, PIECES_P1, stage, source)
                        with sp.Fori(1, KB // 2) as pair:
                            for s in range(2):
                                load_x(pair * 2 + s, s)

                    @block.gpsimd
                    def _(pool):
                        def norm_scale(t, s):
                            pool.wait_ge(a_stat, T0 + t + 1)
                            pool.nop(nofuse=True)
                            pool.tensor_scalar(rs[:, 0, s:s + 1], mv[:, s, 1:2], 1.0 + LN_EPS,
                                               LN_EPS * LN_EPS, ALU.mult, ALU.add).then_inc(a_var, 1)
                            pool.wait_ge(a_var, T0 + t + 1)
                            pool.tensor_tensor(rs[:, 1, s:s + 1], rs[:, 0, s:s + 1], neg_half[:, 0:1], ALU.pow)\
                                .then_inc(a_rs, 1)

                        def affine(t, s):
                            pool.wait_ge(a_y, T0 + t + 3)
                            pool.tensor_tensor(yt[:, s, :], yt[:, s, :], lng[:, :], ALU.mult).then_inc(a_xg, 1)
                            pool.wait_ge(a_xg, T0 + t + 1)
                            pool.tensor_tensor(yt[:, s, :], yt[:, s, :], lnb[:, :], ALU.add).then_inc(a_xn, 1)

                        def rms_scale(t, which):
                            i = (T0 + t) * 2 + which + 1
                            part = slice(which * H, which * H + H)
                            pool.wait_ge(a_ssq, i + 1)
                            pool.nop(nofuse=True)
                            pool.tensor_scalar(ms[:, part], ssq[:, part], 1.0 / DH, RMS_EPS * RMS_EPS, ALU.mult, ALU.max)\
                                .then_inc(a_ms, 1)
                            pool.wait_ge(a_ms, i)
                            pool.tensor_tensor(rp[:, part], ms[:, part], neg_half[:, part], ALU.pow).then_inc(a_pow, 1)
                            pool.wait_ge(a_pow, i)
                            pool.nop(nofuse=True)
                            pool.tensor_scalar(rinv[:, part], rp[:, part], INV_WS, None, ALU.mult).then_inc(a_rinv, 1)

                        def step(t, s, before, next1, next2):
                            if next2:
                                norm_scale(t + 2, s)
                            rms_scale(t, 0)
                            if next2:
                                affine(t + 2, s)
                            rms_scale(t, 1)

                        pool.wait_ge(a_const, 32 * (b + 1))
                        pool.nop(nofuse=True)
                        for t in range(2):
                            norm_scale(t, t)
                            affine(t, t)
                        over_tiles(pool, step)

                    @block.tensor
                    def _(pe):
                        def transposes(t, s, first=False):
                            pe.wait_ge(a_xn, T0 + t + 1)
                            if not first:
                                pe.wait_ge(a_xl, T0 + t)
                            for d in range(DC):
                                mm = pe.transpose(TB[:, d * P:(d + 1) * P], yt[:, s, d * P:(d + 1) * P], ident[:, :])
                            mm.then_inc(a_t_done, 1)

                        def project(s, name, bank, done):
                            mm3(pe, bank[:, :],
                                lambda d: xth[:, s, d * P:(d + 1) * P], lambda d: xtl[:, s, d * P:(d + 1) * P],
                                lambda d: wh[name][:, d, :], lambda d: wl[name][:, d, :]).then_inc(done, 1)

                        def head_transposes(t):
                            for which in range(2):
                                pe.wait_ge(a_qk, (T0 + t) * 2 + which + 1)
                                pe.wait_ge(a_ht_free, (T0 + t) * 2 + which + 1)
                                for d in range(DC):
                                    mm = pe.transpose(HT[which][:, d * P:(d + 1) * P],
                                                      qkn[:, which, d * P:(d + 1) * P], ident[:, :])
                                mm.then_inc(a_ht_done, 1)

                        def step(t, s, before, next1, next2):
                            pe.wait_ge(a_xl, T0 + t + 1)
                            if not before:
                                pe.wait_ge(w_split, pieces_split(b, PIECES_P1[:2]))
                            project(s, "q", QB[s], a_q_done)
                            if next1:
                                transposes(t + 1, 1 - s)
                            if not before:
                                pe.wait_ge(w_split, pieces_split(b, PIECES_P1[:4]))
                            project(s, "k", KBK[s], a_k_done)
                            if before:
                                head_transposes(t - 1)
                            pe.wait_ge(a_v_ready, T0 + t + 1)
                            if not before:
                                pe.wait_ge(w_split, pieces_split(b, PIECES_P1))
                            project(s, "v", VB, a_v_done)

                        transposes(0, 0, first=True)
                        over_tiles(pe, step)
                        head_transposes(KB - 1)

                    @block.scalar
                    def _(act):
                        def x_high(t, s):
                            act.wait_ge(a_t_done, T0 + t + 1)
                            act.activation(xth[:, s, :], TB[:, :], ACT.Copy).then_inc(a_xh, 1)

                        def square(t, which, bank, done):
                            act.wait_ge(done, T0 + t + 1)
                            act.wait_ge(a_ssq, (T0 + t) * 2 + which + 1)
                            act.activation(sq[:, :], bank[:, :], ACT.Square, scale=INV_WS).then_inc(a_sq, 1)

                        def heads_high(t):
                            tok = bass.ds(t * P, P)
                            for which, (dst, g) in enumerate(((q_hh, qg), (k_h1, kg))):
                                act.wait_ge(a_ht_done, (T0 + t) * 2 + which + 1)
                                for odd in range(2):
                                    src = HT[which][DH * odd:DH * odd + DH, :].rearrange("p (h n) -> p h n", h=DC)
                                    act.activation(dst[0:DH, odd::2, tok], src, ACT.Copy,
                                                   scale=g[DH * odd:DH * odd + DH, :]).then_inc(a_hh, 1)

                        def step(t, s, before, next1, next2):
                            square(t, 0, QB[s], a_q_done)
                            if next1:
                                x_high(t + 1, 1 - s)
                            square(t, 1, KBK[s], a_k_done)
                            if before:
                                heads_high(t - 1)
                            act.wait_ge(a_v_done, T0 + t + 1)
                            act.activation(v_h[:, bass.ds(t * D, D)], VB[:, :], ACT.Copy, scale=INV_WS).then_inc(a_vh, 1)

                        split_high(act, b, PIECES_P1[:2], stage, wh)
                        x_high(0, 0)
                        split_high(act, b, PIECES_P1[2:], stage, wh)
                        over_tiles(act, step)
                        heads_high(KB - 1)

                    @block.vector
                    def _(dve):
                        def stats(t, s):
                            dve.wait_ge(a_x_in[s], T0 * 8 + (t // 2) * 16 + 16)
                            dve.nop(nofuse=True)
                            dve.bn_stats(st[:, s, :], xt[:, s, :]).then_inc(a_bn, 1)
                            dve.wait_ge(a_bn, T0 + t + 1)
                            dve.nop(nofuse=True)
                            dve.bn_aggr(mv[:, s, :], st[:, s, :]).then_inc(a_stat, 1)

                        def normalise(t, s, first=False):
                            dve.wait_ge(a_rs, T0 + t + 1)
                            if not first:
                                dve.wait_ge(a_t_done, T0 + t - 1)
                            dve.tensor_scalar(yt[:, s, :], xt[:, s, :], mv[:, s, 0:1], rs[:, 1, s:s + 1],
                                              ALU.subtract, ALU.mult).then_inc(a_y, 1)

                        def x_low(t, s):
                            dve.wait_ge(a_xh, T0 + t + 1)
                            dve.tensor_tensor(xtl[:, s, :], TB[:, :], xth[:, s, :], ALU.subtract).then_inc(a_xl, 1)

                        def sum_squares(t, which):
                            dve.wait_ge(a_sq, (T0 + t) * 2 + which + 1)
                            dve.tensor_reduce(ssq[:, which * H:which * H + H],
                                              sq[:, :].rearrange("p (h d) -> p h d", d=DH), AX_X, ALU.add)\
                                .then_inc(a_ssq, 1)

                        def heads_low(t):
                            tok = bass.ds(t * P, P)
                            for which, (high, low, row, g) in enumerate(((q_hh, q_lm, 0, qg), (k_h1, k_hl, DH, kg))):
                                for odd in range(2):
                                    dve.wait_ge(a_hh, (T0 + t) * 4 + 2 * which + odd + 1)
                                    src = HT[which][DH * odd:DH * odd + DH, :].rearrange("p (h n) -> p h n", h=DC)
                                    low_part = dve.scalar_tensor_tensor(
                                        out=low[row:row + DH, odd::2, tok], in0=src,
                                        scalar=g[DH * odd:DH * odd + DH, :], in1=high[0:DH, odd::2, tok],
                                        op0=ALU.mult, op1=ALU.subtract)
                                low_part.then_inc(a_ht_free, 1)
                                if which == 0:
                                    dve.tensor_copy(q_hh[DH:P, :, tok], q_hh[0:DH, :, tok]).then_inc(a_dup, 1)
                                else:
                                    dve.tensor_copy(k_hl[0:DH, :, tok], k_h1[0:DH, :, tok]).then_inc(a_dup, 1)

                        def scale_heads(t, s, before):
                            if before:
                                dve.wait_ge(a_ht_done, (T0 + t) * 2)
                            for which, bank in enumerate((QB[s], KBK[s])):
                                dve.wait_ge(a_rinv, (T0 + t) * 2 + which + 1)
                                dve.tensor_tensor(
                                    qkn[:, which, :].rearrange("p (h d) -> p h d", d=DH),
                                    bank[:, :].rearrange("p (h d) -> p h d", d=DH),
                                    rinv[:, which * H:which * H + H].rearrange("p (h a) -> p h a", a=1)
                                    .broadcast_to([P, H, DH]), ALU.mult).then_inc(a_qk, 1)

                        def v_low(t):
                            vcols = bass.ds(t * D, D)
                            dve.wait_ge(a_vh, T0 + t + 1)
                            dve.scalar_tensor_tensor(out=v_l[:, vcols], in0=VB[:, :], scalar=INV_WS,
                                                     in1=v_h[:, vcols], op0=ALU.mult, op1=ALU.subtract)\
                                .then_inc(a_v_ready, 1)

                        def step(t, s, before, next1, next2):
                            if next2:
                                stats(t + 2, s)
                            sum_squares(t, 0)
                            if next1:
                                x_low(t + 1, 1 - s)
                            if next2:
                                normalise(t + 2, s)
                            sum_squares(t, 1)
                            if before:
                                heads_low(t - 1)
                            v_low(t)
                            scale_heads(t, s, before)

                        for t in range(2):
                            stats(t, t)
                            normalise(t, t, first=True)
                        split_low(dve, b, PIECES_P1[:2], stage, wh, wl)
                        x_low(0, 0)
                        split_low(dve, b, PIECES_P1[2:], stage, wh, wl)
                        over_tiles(dve, step)
                        heads_low(KB - 1)

                with ExitStack() as ph:
                    vsh = sb(ph, "vsh", [P, 2 * KB * P], F16)
                    vsl = sb(ph, "vsl", [P, 2 * KB * P], F16)
                    probs = sb(ph, "probs", [P, 4, CT], F32)
                    probs_h = sb(ph, "probs_h", [P, 4, CT], F16)
                    probs_l = sb(ph, "probs_l", [P, 4, CT], F16)
                    pm = sb(ph, "pm", [P, 16], F32)
                    gm = sb(ph, "gm", [P, TPC], F32)
                    nm = sb(ph, "nm", [P, TPC], F16)
                    osb = sb(ph, "osb", [P, CT], F32)
                    rden = sb(ph, "rden", [DH, CT], F32)
                    onorm = sb(ph, "onorm", [DH, CT], F32)
                    SB = banks[0:2]
                    MB = banks[2:6]
                    OB = banks[7]
                    RB = banks[6]
                    qf = q_hh[:, :, :].rearrange("p h n -> p (h n)")
                    lf = q_lm[:, :, :].rearrange("p h n -> p (h n)")
                    k1 = k_hl[:, :, :].rearrange("p h n -> p (h n)")
                    k2 = k_h1[:, :, :].rearrange("p h n -> p (h n)")
                    UNITS = H * CH
                    U0 = b * UNITS
                    LA = 2
                    MAXED = UNITS - LA
                    block = ph.enter_context(nc.Block())

                    @block.gpsimd
                    def _(pool):
                        pool.memset(k_h1[DH:DH + 1, :, :], 1.0).then_inc(a_ones, 1)
                        pool.wait_ge(a_ones, b + 1)
                        pool.nop(nofuse=True)
                        with pool.Fori(0, UNITS) as u:
                            step = (U0 + u) * KB
                            for kb in range(KB):
                                pool.wait_ge(ph_ready, step + kb + 1)
                                pool.wait_ge(p_free, step + kb + 1)
                                pool.tensor_tensor(probs_l[:, kb % 4, :], probs[:, kb % 4, :], probs_h[:, kb % 4, :],
                                                   ALU.subtract).then_inc(pl_ready, 1)

                    @block.tensor
                    def _(pe):
                        def max_scores(k, qcol, kcol, count):
                            pe.wait_ge(mx_free, count + 1)
                            pe.matmul(MB[k % 4][:, :], qf[:, qcol], k1[:, kcol], start=True, stop=True)\
                                .then_inc(mx_ready, 1)

                        def max_row(r):
                            pe.wait_ge(nm_ready, r + 1)
                            for a in range(TPC):
                                mm = pe.matmul(RB[DH:DH + 1, a * P:(a + 1) * P], nm[:, a:a + 1], ident16[:, :],
                                               start=True, stop=True)
                            mm.then_inc(mrow_done, 1)

                        def scores(u, kb):
                            kcols, qcols = bass.ds(u // CH * N + kb * P, P), bass.ds(u * CT, CT)
                            pe.matmul(SB[kb % 2][:, :], k1[:, kcols], qf[:, qcols], start=True, stop=False)
                            pe.matmul(SB[kb % 2][:, :], k2[0:DH + 1, kcols], lf[0:DH + 1, qcols], start=False,
                                      stop=True).then_inc(s_ready, 1)

                        def unit(u, maxed, last=False):
                            U = U0 + u
                            pe.wait_ge(vs_ready, U0 + u // CH * CH + CH)
                            for kb in range(KB):
                                pe.wait_ge(ph_ready, U * KB + kb + 1)
                                if kb + 2 < KB:
                                    scores(u, kb + 2)
                                elif not last:
                                    if kb + 2 == KB:
                                        pe.wait_ge(m_ready, U + 2)
                                    scores(u + 1, kb + 2 - KB)
                                if maxed:
                                    max_scores(kb, bass.ds((u + LA) * CT + kb // 4 * P, P),
                                               bass.ds((u + LA) // CH * N + kb % 4 * CT, CT), (U + LA) * 16 + kb)
                                if kb == 2 and (maxed or u == MAXED):
                                    max_row(U + LA - 1)
                                if kb == 0:
                                    pe.wait_ge(o_free, U + 8)
                                v0 = u // CH % 2 * (KB * P) + kb * P
                                pe.matmul(OB[:, :], vsl[:, bass.ds(v0, P)], probs_h[:, kb % 4, :],
                                          start=(kb == 0), stop=False)
                                pe.matmul(OB[0:DH, :], vsh[:, bass.ds(v0, DH)], probs_h[:, kb % 4, :],
                                          start=False, stop=False, skip_group_check=True)
                                pe.wait_ge(pl_ready, U * KB + kb + 1)
                                pe.matmul(OB[:, :], vsh[:, bass.ds(v0, P)], probs_l[:, kb % 4, :],
                                          start=False, stop=(kb == KB - 1)).then_inc(p_free, 1)

                        for g in range(LA):
                            for k in range(16):
                                max_scores(k, slice(g * CT + k // 4 * P, g * CT + k // 4 * P + P),
                                           slice(k % 4 * CT, k % 4 * CT + CT), U0 * 16 + g * 16 + k)
                            if g < LA - 1:
                                max_row(U0 + g)
                        pe.wait_ge(m_ready, U0 + 1)
                        pe.wait_ge(a_ones, b + 1)
                        scores(0, 0)
                        scores(0, 1)
                        with pe.Fori(0, MAXED) as u:
                            unit(u, True)
                        for u in range(MAXED, UNITS):
                            unit(u, False, last=(u == UNITS - 1))

                    @block.scalar
                    def _(act):
                        act.preload_act_table(ACT.Exp)
                        with act.Fori(0, UNITS) as u:
                            step = (U0 + u) * KB
                            for kb in range(KB):
                                act.wait_ge(s_ready, step + kb + 1)
                                act.wait_ge(p_free, step + kb + 1)
                                act.activation(probs[:, kb % 4, :], SB[kb % 2][:, :], ACT.Exp).then_inc(p_ready, 1)
                                act.activation(probs_h[:, kb % 4, :], SB[kb % 2][:, :], ACT.Exp).then_inc(ph_ready, 1)

                    @block.vector
                    def _(dve):
                        def reduce_max(k, count):
                            dve.wait_ge(mx_ready, count + 1)
                            dve.tensor_reduce(pm[:, k:k + 1], MB[k % 4][:, :], AX_X, ALU.max).then_inc(mx_free, 1)

                        def negate_max(r):
                            dve.wait_ge(mx_free, r * 16 + 20)
                            dve.tensor_reduce(gm[:, :], pm[:, :].rearrange("p (a k) -> p a k", k=4), AX_X, ALU.max)\
                                .then_inc(gm_ready, 1)
                            dve.wait_ge(gm_ready, r + 1)
                            dve.tensor_scalar(nm[:, :], gm[:, :], -1.0, PSHIFT, ALU.mult, ALU.add).then_inc(nm_ready, 1)

                        def copy_row(r, cols):
                            dve.wait_ge(mrow_done, r + 1)
                            dve.tensor_copy(lf[DH:DH + 1, cols], RB[DH:DH + 1, :]).then_inc(m_ready, 1)

                        def copy_v(t):
                            cols = bass.ds(t * (KB // CH * P) % (2 * KB * P), KB // CH * P)
                            rows = bass.ds(t % CH * (KB // CH * D), KB // CH * D)
                            for i, (dst, src) in enumerate(((vsh, v_h), (vsl, v_l))):
                                dve.tensor_copy(dst[:, cols].rearrange("p (k n) -> p k n", n=P)[:, :, 0:DH],
                                                src[:, rows].rearrange("p (k d) -> p k d", d=D)
                                                [:, :, bass.ds(t // CH * DH, DH)])\
                                    .then_inc((vs_half, vs_ready)[i], 1)

                        AHEAD = 4
                        for i, v in enumerate((vsh, vsl)):
                            dve.memset(v[:, :].rearrange("p (k n) -> p k n", n=P)[:, :, DH:P], 1.0).then_inc(vs_ones, 1)
                        for t in range(CH):
                            copy_v(t)
                        for g in range(LA):
                            for k in range(16):
                                reduce_max(k, U0 * 16 + g * 16 + k)
                            negate_max(U0 + g)
                            if g < LA - 1:
                                copy_row(U0 + g, slice(g * CT, g * CT + CT))

                        def unit(u, maxed, next_maxed, next_v):
                            U = U0 + u
                            for k in range(AHEAD, 16):
                                if maxed:
                                    reduce_max(k, (U + LA) * 16 + k)
                                if k == 4 and (maxed or u == MAXED):
                                    copy_row(U + LA - 1, bass.ds((u + LA - 1) * CT, CT))
                                if k == 8 and next_v:
                                    copy_v(u + CH)
                            if maxed:
                                negate_max(U + LA)
                            dve.wait_ge(p_free, (U + 1) * KB + 4)
                            dve.tensor_copy(osb[:, :], OB[:, :]).then_inc(o_free, 1)
                            if next_maxed:
                                reduce_max(0, (U + LA + 1) * 16)
                            dve.wait_ge(o_free, U + 9)
                            dve.reciprocal(rden[:, 0:CT // 2], osb[DH:P, 0:CT // 2]).then_inc(o_rec, 1)
                            if next_maxed:
                                reduce_max(1, (U + LA + 1) * 16 + 1)
                            dve.reciprocal(rden[:, CT // 2:CT], osb[DH:P, CT // 2:CT]).then_inc(o_rec, 1)
                            if next_maxed:
                                reduce_max(2, (U + LA + 1) * 16 + 2)
                            dve.wait_ge(o_rec, 2 * U + 2)
                            dve.tensor_tensor(onorm[:, :], osb[0:DH, :], rden[:, :], ALU.mult).then_inc(o_norm, 1)
                            if next_maxed:
                                reduce_max(3, (U + LA + 1) * 16 + 3)
                            dve.wait_ge(o_norm, U + 1)
                            cols = bass.ds(u * CT, CT)
                            dve.tensor_copy(qf[0:DH, cols], onorm[:, :]).then_inc(o_high, 1)
                            dve.wait_ge(o_high, U + 1)
                            dve.tensor_tensor(qf[DH:P, cols], onorm[:, :], qf[0:DH, cols], ALU.subtract)

                        for k in range(AHEAD):
                            reduce_max(k, (U0 + LA) * 16 + k)
                        with dve.Fori(0, UNITS - CH) as u:
                            unit(u, True, True, True)
                        for u in range(UNITS - CH, UNITS):
                            unit(u, u < MAXED, u + 1 < MAXED, False)

            with ExitStack() as mlp:
                x2 = sb(mlp, "x2", [P, KB * D], F32)
                x2th = sb(mlp, "x2th", [P, DC, N], F16)
                x2tl = sb(mlp, "x2tl", [P, DC, N], F16)

                with ExitStack() as ph:
                    wh = {n: sb(ph, f"dwh_{n}", [P, DC, D], F16) for n in ("xq", "xo")}
                    wl = {n: sb(ph, f"dwl_{n}", [P, DC, D], F16) for n in ("xq", "xo")}
                    wh["o"] = sb(ph, "dwh_o", [P, H, D], F16)
                    wl["o"] = sb(ph, "dwl_o", [P, H, D], F16)
                    kbh = sb(ph, "kbh", [P, DC, 4 * CTX], F16)
                    kbl = sb(ph, "kbl", [P, DC, 4 * CTX], F16)
                    vxh = sb(ph, "vxh", [P, D], F16)
                    vxl = sb(ph, "vxl", [P, D], F16)
                    bo_b = sb(ph, "bo_b", [P, D], F32)
                    xbq_b = sb(ph, "xbq_b", [P, D], F32)
                    xbo_b = sb(ph, "xbo_b", [P, D], F32)

                    OB4 = banks[4:8]

                    def out_project(pe, c, j):
                        o_cols = bass.ds(c * CT + j * P, P)
                        for h in range(H):
                            pe.matmul(OB4[j][:, :], q_hh[:, h, o_cols], wh["o"][:, h, :], start=(h == 0), stop=False)
                            mm = pe.matmul(OB4[j][:, :], q_hh[:, h, o_cols], wl["o"][:, h, :], start=False,
                                           stop=(h == H - 1))
                        mm.then_inc(d_o_done, 1)

                    xr = sb(ph, "xr", [P, TPC, D], F32)

                    def load_x(sp, n):
                        for j in range(TPC):
                            sp.wait_ge(d_x1, n * TPC + j + 1)
                            sp.dma_start(xr[:, j, :], x_rows[bass.ds(n * CT + j * P, P), :]).then_inc(d_x_in[j], 16)

                    def add_bo(pool, n, j):
                        pool.wait_ge(d_x_in[j], n * 16 + 16)
                        pool.tensor_tensor(xr[:, j, :], xr[:, j, :], bo_b[:, :], ALU.add).then_inc(d_xb, 1)

                    with ExitStack() as cp:
                        stage = [sb(cp, f"stage_c{i}", [P, 2, D], F32) for i in range(4)]
                        for n_ in ("xk", "xv"):
                            wh[n_] = sb(cp, f"cwh_{n_}", [P, DC, D], F16)
                            wl[n_] = sb(cp, f"cwl_{n_}", [P, DC, D], F16)
                        cx = sb(cp, "cx", [P, D], F32)
                        cth = sb(cp, "cth", [P, D], F16)
                        ctl = sb(cp, "ctl", [P, D], F16)
                        kx = sb(cp, "kx", [P, D], F32)
                        vx = sb(cp, "vx", [P, D], F32)
                        xbk_b = sb(cp, "xbk_b", [P, D], F32)
                        xbv_b = sb(cp, "xbv_b", [P, D], F32)
                        block = cp.enter_context(nc.Block())

                        @block.sync
                        def _(sp):
                            sp.dma_start(cx[:, :], ctx_rows[bass.ds(b * CTX, CTX), :]).then_inc(c_ctx, 16)
                            load_pieces(sp, b, PIECES_P3[:8], stage, source)
                            load_x(sp, b * CH)
                            for dst, src in ((bo_b, b_o), (xbk_b, xb_k), (xbv_b, xb_v), (xbq_b, xb_q), (xbo_b, xb_o)):
                                sp.dma_start(dst[:, :], bcast(src)).then_inc(c_in, 16)
                            load_pieces(sp, b, PIECES_P3[8:], stage, source)
                            sp.wait_ge(c_in, b * 80 + 80)
                            sp.nop(nofuse=True)

                        @block.gpsimd
                        def _(pool):
                            pool.memset(kbh[:, :, :], 0.0).then_inc(c_zero, 1)
                            pool.memset(kbl[:, :, :], 0.0).then_inc(c_zero, 1)
                            pool.wait_ge(c_in, b * 80 + 80)
                            for j in range(TPC):
                                add_bo(pool, b * CH, j)

                        @block.tensor
                        def _(pe):
                            def transposes(src):
                                for d in range(DC):
                                    mm = pe.transpose(banks[0][:, d * P:(d + 1) * P], src[:, d * P:(d + 1) * P],
                                                      ident[:, :])
                                mm.then_inc(c_t, 1)

                            def project(name, bank):
                                mm3(pe, bank[:, :], lambda d: cth[:, d * P:(d + 1) * P],
                                    lambda d: ctl[:, d * P:(d + 1) * P], lambda d: wh[name][:, d, :],
                                    lambda d: wl[name][:, d, :]).then_inc(c_mm, 1)

                            pe.wait_ge(c_ctx, b * 16 + 16)
                            transposes(cx)
                            pe.wait_ge(w_split, pieces_split(b, PIECES_P3[:4]))
                            for j in range(TPC):
                                out_project(pe, 0, j)
                            pe.wait_ge(c_l, b * 6 + 1)
                            pe.wait_ge(w_split, pieces_split(b, PIECES_P3[:6]))
                            project("xk", banks[1])
                            pe.wait_ge(w_split, pieces_split(b, PIECES_P3[:8]))
                            project("xv", banks[2])
                            pe.wait_ge(c_tok, b * 2 + 1)
                            transposes(kx)

                        @block.scalar
                        def _(act):
                            act.wait_ge(c_t, b * 2 + 1)
                            act.activation(cth[:, :], banks[0][:, :], ACT.Copy).then_inc(c_h, 1)
                            split_high(act, b, PIECES_P3, stage, wh)
                            act.wait_ge(c_zero, b * 2 + 2)
                            act.wait_ge(c_t, b * 2 + 2)
                            for a in range(4):
                                act.activation(kbh[32 * a:32 * a + 32, :, a * CTX:(a + 1) * CTX],
                                               banks[0][32 * a:32 * a + 32, :].rearrange("p (c n) -> p c n", c=DC),
                                               ACT.Copy).then_inc(c_h, 1)
                            act.wait_ge(c_tok, b * 2 + 2)
                            act.activation(vxh[:, :], vx[:, :], ACT.Copy).then_inc(c_h, 1)

                        @block.vector
                        def _(dve):
                            dve.wait_ge(c_h, b * 6 + 1)
                            dve.tensor_tensor(ctl[:, :], banks[0][:, :], cth[:, :], ALU.subtract).then_inc(c_l, 1)
                            split_low(dve, b, PIECES_P3, stage, wh, wl)
                            for i, (dst, bias) in enumerate(((kx, xbk_b), (vx, xbv_b))):
                                dve.wait_ge(c_mm, b * 2 + i + 1)
                                dve.wait_ge(c_in, b * 80 + 80)
                                dve.scalar_tensor_tensor(out=dst[:, :], in0=banks[1 + i][:, :], scalar=INV_WS,
                                                         in1=bias[:, :], op0=ALU.mult, op1=ALU.add).then_inc(c_tok, 1)
                            for a in range(4):
                                dve.wait_ge(c_h, b * 6 + 2 + a)
                                part = slice(32 * a, 32 * a + 32)
                                dve.tensor_tensor(kbl[part, :, a * CTX:(a + 1) * CTX],
                                                  banks[0][part, :].rearrange("p (c n) -> p c n", c=DC),
                                                  kbh[part, :, a * CTX:(a + 1) * CTX], ALU.subtract).then_inc(c_l, 1)
                            dve.wait_ge(c_h, b * 6 + 6)
                            dve.tensor_tensor(vxl[:, :], vx[:, :], vxh[:, :], ALU.subtract).then_inc(c_l, 1)

                    with ExitStack() as tp:
                        tok0 = sb(tp, "tok0", [P, TPC, D], F32)
                        tok = sb(tp, "tok", [P, TPC, D], F32)
                        th = sb(tp, "th", [P, TPC, D], F16)
                        tl = sb(tp, "tl", [P, TPC, D], F16)
                        px = sb(tp, "px", [P, 2, 8 * CTX], F32)
                        pth = sb(tp, "pth", [P, 2, 8 * CTX], F16)
                        ptl = sb(tp, "ptl", [P, 2, 8 * CTX], F16)
                        mx = sb(tp, "mx", [P, 2, 8], F32)
                        nmx = sb(tp, "nmx", [P, 2, 8], F32)
                        sm = sb(tp, "sm", [P, TPC, XH], F32)
                        rsm = sb(tp, "rsm", [P, TPC, XH], F32)
                        st = sb(tp, "st_d", [P, 2 * TPC, 6], F32)
                        mv = sb(tp, "mv_d", [P, 2 * TPC, 2], F32)
                        rs = sb(tp, "rs_d", [P, 2, 2 * TPC], F32)
                        TB = banks[0:2]
                        PB = banks[2:4]
                        SU = [banks[4:6], banks[6:8]]
                        block = tp.enter_context(nc.Block())

                        TURNS = [(0, 0), (0, 1), (3, 0), (0, 2), (3, 1), (0, 3), (3, 2), (1, 0), (3, 3), (1, 1), (1, 2),
                                 (1, 3)] + [(2, j) for j in range(TPC)]

                        def turns(c, first):
                            if first:
                                return b * (CH * 16), [t for t in TURNS if t[0] != 3]
                            return b * (CH * 16) + c * 16 - TPC, TURNS

                        def bodies(eng, body):
                            body(0, True, False)
                            with eng.Fori(1, CH - 1) as c:
                                body(c, False, False)
                            body(CH - 1, False, True)

                        LAST = [(3, j) for j in range(TPC)]
                        LAST0 = (b + 1) * (CH * 16) - TPC

                        @block.sync
                        def _(sp):
                            with sp.Fori(1, CH) as c:
                                load_x(sp, b * CH + c)

                        @block.gpsimd
                        def _(pool):
                            def norm_scale(s, n, j):
                                k = s * TPC + j
                                pool.wait_ge(d_stat[s], n * TPC + j + 1)
                                pool.nop(nofuse=True)
                                pool.tensor_scalar(rs[:, 0, k:k + 1], mv[:, k, 1:2], LN_EPS, None, ALU.add)\
                                    .then_inc(d_var[s], 1)
                                pool.wait_ge(d_var[s], n * TPC + j + 1)
                                pool.tensor_tensor(rs[:, 1, k:k + 1], rs[:, 0, k:k + 1], neg_half[:, 0:1], ALU.pow)\
                                    .then_inc(d_rs[s], 1)

                            def add_xbo(n, c, j):
                                cols = bass.ds(c * (TPC * D) + j * D, D)
                                pool.wait_ge(d_n0, n * TPC + j + 1)
                                pool.tensor_tensor(x2[:, cols], x2[:, cols], xbo_b[:, :], ALU.add).then_inc(d_xb2, 1)

                            def body(c, first, last):
                                n = b * CH + c
                                if not last:
                                    for j in range(TPC):
                                        add_bo(pool, n + 1, j)
                                for s, j in NORMS:
                                    if s == 1 or not last:
                                        norm_scale(s, n + 1 - s, j)
                                if not last:
                                    for j in range(TPC):
                                        add_xbo(n + 1, c + 1, j)

                            NORMS = [(0, 0), (0, 1), (0, 2), (1, 0), (0, 3), (1, 1), (1, 2), (1, 3)]
                            for j in range(TPC):
                                norm_scale(0, b * CH, j)
                            for j in range(TPC):
                                add_xbo(b * CH, 0, j)
                            bodies(pool, body)

                        @block.tensor
                        def _(pe):
                            def transposes(before, i, src, j):
                                pe.wait_ge(d_tl, before + i + 1)
                                for d in range(DC):
                                    mm = pe.transpose(TB[i % 2][:, d * P:(d + 1) * P], src[:, j, d * P:(d + 1) * P],
                                                      ident[:, :])
                                mm.then_inc(d_t_done, 1)

                            def body(c, first, last):
                                n = b * CH + c
                                before, order = turns(c, first)

                                def turn(s, j):
                                    if s == 0:
                                        pe.wait_ge(d_n0, n * TPC + j + 1)
                                    elif s == 1:
                                        pe.wait_ge(d_q, n * TPC + j + 1)
                                    elif s == 2:
                                        pe.wait_ge(d_o, n * TPC + max(j + 1, min(j + 3, TPC)))
                                    else:
                                        pe.wait_ge(d_n1, (n - 1) * TPC + j + 1)
                                    transposes(before, order.index((s, j)), tok if s else tok0, j)

                                def split(s, j):
                                    return before + order.index((s, j)) + 3

                                def project(s, j, name, done):
                                    pe.wait_ge(d_tl, split(s, j))
                                    mm3(pe, PB[j % 2][:, :], lambda d: th[:, j, d * P:(d + 1) * P],
                                        lambda d: tl[:, j, d * P:(d + 1) * P], lambda d: wh[name][:, d, :],
                                        lambda d: wl[name][:, d, :]).then_inc(done, 1)

                                turn(0, 0)
                                turn(0, 1)
                                for j in range(TPC):
                                    if not first:
                                        turn(3, j)
                                    if j >= 2:
                                        pe.wait_ge(d_q, n * TPC + j - 1)
                                    elif not first:
                                        pe.wait_ge(d_x2, (n - 1) * TPC + j + 3)
                                    project(0, j, "xq", d_q_done)
                                    if j + 2 < TPC:
                                        turn(0, j + 2)
                                    else:
                                        turn(1, j - 2)

                                def cross_scores(v):
                                    j, half = v // 2, v % 2
                                    pe.wait_ge(d_tl, split(1, j))
                                    if v >= 2:
                                        pe.wait_ge(d_ex, n * 8 + v - 1)
                                    for i in range(2):
                                        d = 2 * half + i
                                        bank = SU[v % 2][i][:, :]
                                        qh, ql = th[:, j, d * P:(d + 1) * P], tl[:, j, d * P:(d + 1) * P]
                                        pe.matmul(bank, qh, kbh[:, d, :], start=True, stop=False)
                                        pe.matmul(bank, qh, kbl[:, d, :], start=False, stop=False)
                                        mm = pe.matmul(bank, ql, kbh[:, d, :], start=False, stop=True)
                                    mm.then_inc(d_s_done, 1)

                                def transpose_probs(v):
                                    pe.wait_ge(d_ex, n * 8 + v + 1)
                                    pe.wait_ge(d_ptl, (n * 8 + v) * 2 + 2)
                                    for hh in range(8):
                                        mm = pe.transpose(PB[hh // 4][:, hh % 4 * P:hh % 4 * P + P],
                                                          px[:, v % 2, hh * CTX:(hh + 1) * CTX], ident[:, :])
                                    mm.then_inc(d_pt_done, 1)

                                def cross_values(v):
                                    j, half = v // 2, v % 2
                                    pe.wait_ge(d_ptl, (n * 8 + v) * 2 + 4)
                                    if half == 0 and j >= 2:
                                        pe.wait_ge(d_o, n * TPC + j - 1)
                                    elif half == 0:
                                        pe.wait_ge(d_tl, split(1, TPC - 1))
                                    for hh in range(8):
                                        cols = slice((8 * half + hh) * XD, (8 * half + hh + 1) * XD)
                                        ph_, pl_ = (t[:, v % 2, hh * CTX:(hh + 1) * CTX] for t in (pth, ptl))
                                        pe.matmul(TB[j % 2][:, cols], ph_, vxh[:, cols], start=True, stop=False)
                                        pe.matmul(TB[j % 2][:, cols], ph_, vxl[:, cols], start=False, stop=False)
                                        mm = pe.matmul(TB[j % 2][:, cols], pl_, vxh[:, cols], start=False, stop=True)
                                    mm.then_inc(d_av_done, 1)

                                pe.wait_ge(d_x1, n * TPC + 2 * TPC)
                                cross_scores(0)
                                cross_scores(1)
                                turn(1, 2)
                                turn(1, 3)
                                for v in range(8):
                                    if v + 2 < 8:
                                        cross_scores(v + 2)
                                    transpose_probs(v)
                                    if v:
                                        cross_values(v - 1)
                                    if v == 6 and not last:
                                        out_project(pe, c + 1, 0)
                                        out_project(pe, c + 1, 1)
                                    if v == 7 and not last:
                                        out_project(pe, c + 1, 2)
                                cross_values(7)
                                turn(2, 0)
                                if not last:
                                    out_project(pe, c + 1, 3)
                                pe.wait_ge(d_ptl, n * 16 + 18)
                                for j in range(TPC):
                                    if j + 1 < TPC:
                                        turn(2, j + 1)
                                    if j >= 2:
                                        pe.wait_ge(d_x2, n * TPC + j - 1)
                                    project(2, j, "xo", d_xo_done)

                            bodies(pe, body)
                            for i, (_, j) in enumerate(LAST):
                                pe.wait_ge(d_n1, (b + 1) * (CH * TPC) - TPC + j + 1)
                                transposes(LAST0, i, tok, j)

                        @block.scalar
                        def _(act):
                            def high(before, i, dst):
                                act.wait_ge(d_t_done, before + i + 1)
                                act.activation(dst, TB[i % 2][:, :], ACT.Copy).then_inc(d_th, 1)

                            def body(c, first, last):
                                n = b * CH + c
                                before, order = turns(c, first)

                                def high_of(i):
                                    s, j = order[i]
                                    high(before, i, x2th[:, :, bass.ds((c - 1) * CT + j * P, P)] if s == 3
                                         else th[:, j, :])

                                def exponentials(v):
                                    act.wait_ge(d_nmx, n * 8 + v + 1)
                                    act.wait_ge(d_pt_done, n * 8 + v + 1)
                                    for hh in range(8):
                                        ex = act.activation(
                                            px[:, v % 2, hh * CTX:(hh + 1) * CTX],
                                            SU[v % 2][hh // 4][:, hh % 4 * CTX:(hh % 4 + 1) * CTX], ACT.Exp,
                                            bias=nmx[:, v % 2, hh:hh + 1], scale=XSCALE,
                                            accum_out=sm[:, v // 2, 8 * (v % 2) + hh:8 * (v % 2) + hh + 1])
                                    ex.then_inc(d_ex, 1)

                                def probs_high(v):
                                    act.wait_ge(d_pt_done, n * 8 + v + 3)
                                    act.activation(pth[:, v % 2, 0:512], PB[0][:, :], ACT.Copy).then_inc(d_pth[0], 1)

                                queries = len(order) - TPC
                                for i in range(queries - 2):
                                    high_of(i)
                                exponentials(0)
                                for i in range(queries - 2, queries):
                                    high_of(i)
                                for v in range(8):
                                    if v + 1 < 8:
                                        exponentials(v + 1)
                                    probs_high(v)
                                for i in range(queries, len(order)):
                                    high_of(i)

                            bodies(act, body)
                            for i, (_, j) in enumerate(LAST):
                                high(LAST0, i, x2th[:, :, (CH - 1) * CT + j * P:(CH - 1) * CT + j * P + P])

                        @block.vector
                        def _(dve):
                            def low(before, i, dst, high):
                                dve.wait_ge(d_th, before + i + 1)
                                dve.tensor_tensor(dst, TB[i % 2][:, :], high, ALU.subtract).then_inc(d_tl, 1)

                            def stats(s, n, j, src):
                                k = s * TPC + j
                                dve.bn_stats(st[:, k, :], src).then_inc(d_bn[s], 1)
                                dve.wait_ge(d_bn[s], n * TPC + j + 1)
                                dve.nop(nofuse=True)
                                dve.bn_aggr(mv[:, k, :], st[:, k, :]).then_inc(d_stat[s], 1)

                            def norm(s, n, c, j):
                                k = s * TPC + j
                                dve.wait_ge(d_rs[s], n * TPC + j + 1)
                                dve.tensor_scalar((tok if s else tok0)[:, j, :],
                                                  x2[:, bass.ds(c * (TPC * D) + j * D, D)], mv[:, k, 0:1],
                                                  rs[:, 1, k:k + 1], ALU.subtract, ALU.mult)\
                                    .then_inc(d_n1 if s else d_n0, 1)

                            def residual1(n, c, j):
                                cols = bass.ds(c * (TPC * D) + j * D, D)
                                dve.wait_ge(d_xb, n * TPC + j + 1)
                                dve.wait_ge(d_o_done, n * TPC + j + 1)
                                dve.scalar_tensor_tensor(out=x2[:, cols], in0=OB4[j][:, :], scalar=INV_WS,
                                                         in1=xr[:, j, :], op0=ALU.mult, op1=ALU.add)\
                                    .then_inc(d_x1, 1)
                                dve.wait_ge(d_x1, n * TPC + j + 5)
                                dve.nop(nofuse=True)
                                stats(0, n, j, x2[:, cols])

                            def residual2(n, c, j):
                                cols = bass.ds(c * (TPC * D) + j * D, D)
                                dve.wait_ge(d_xb2, n * TPC + j + 1)
                                dve.wait_ge(d_xo_done, n * TPC + j + 1)
                                dve.scalar_tensor_tensor(out=x2[:, cols], in0=PB[j % 2][:, :], scalar=INV_WS,
                                                         in1=x2[:, cols], op0=ALU.mult, op1=ALU.add)\
                                    .then_inc(d_x2, 1)
                                dve.wait_ge(d_x2, n * TPC + j + 1)
                                dve.nop(nofuse=True)
                                stats(1, n, j, x2[:, cols])

                            def body(c, first, last):
                                n = b * CH + c
                                before, order = turns(c, first)

                                def low_of(s, j):
                                    if s == 3:
                                        toks = bass.ds((c - 1) * CT + j * P, P)
                                        dst, high = x2tl[:, :, toks], x2th[:, :, toks]
                                    else:
                                        dst, high = tl[:, j, :], th[:, j, :]
                                    low(before, order.index((s, j)), dst, high)

                                def query(j):
                                    dve.wait_ge(d_q_done, n * TPC + j + 1)
                                    dve.scalar_tensor_tensor(out=tok[:, j, :], in0=PB[j % 2][:, :], scalar=INV_WS,
                                                             in1=xbq_b[:, :], op0=ALU.mult, op1=ALU.add)\
                                        .then_inc(d_q, 1)

                                def cross_max(v):
                                    u = n * 8 + v
                                    dve.wait_ge(d_s_done, u + 1)
                                    for i in range(2):
                                        dve.tensor_reduce(mx[:, v % 2, 4 * i:4 * i + 4],
                                                          SU[v % 2][i][:, :].rearrange("p (h k) -> p h k", k=CTX),
                                                          AX_X, ALU.max).then_inc(d_mx, 1)
                                    dve.wait_ge(d_mx, u * 2 + 2)
                                    dve.tensor_scalar(nmx[:, v % 2, :], mx[:, v % 2, :], -XSCALE, None, ALU.mult)\
                                        .then_inc(d_nmx, 1)

                                def probs_low(v):
                                    dve.wait_ge(d_pt_done, n * 8 + v + 3)
                                    dve.tensor_copy(pth[:, v % 2, 512:1024], PB[1][:, :]).then_inc(d_pth[1], 1)
                                    for i in range(2):
                                        dve.wait_ge(d_pth[i], n * 8 + v + 1)
                                        dve.tensor_tensor(ptl[:, v % 2, i * 512:i * 512 + 512], PB[i][:, :],
                                                          pth[:, v % 2, i * 512:i * 512 + 512], ALU.subtract)\
                                            .then_inc(d_ptl, 1)

                                def output(j):
                                    dve.wait_ge(d_ex, n * 8 + 2 * j + 2)
                                    dve.reciprocal(rsm[:, j, :], sm[:, j, :]).then_inc(d_rec, 1)
                                    dve.wait_ge(d_rec, n * TPC + j + 1)
                                    dve.wait_ge(d_av_done, n * 8 + 2 * j + 2)
                                    dve.tensor_tensor(tok[:, j, :].rearrange("p (h d) -> p h d", d=XD),
                                                      TB[j % 2][:, :].rearrange("p (h d) -> p h d", d=XD),
                                                      rsm[:, j, :].rearrange("p (h a) -> p h a", a=1)
                                                      .broadcast_to([P, XH, XD]), ALU.mult).then_inc(d_o, 1)

                                low_of(0, 0)
                                low_of(0, 1)
                                for j in range(TPC):
                                    if j == 3:
                                        low_of(1, 0)
                                    if not first:
                                        low_of(3, j)
                                    if j + 2 < TPC:
                                        low_of(0, j + 2)
                                    query(j)
                                low_of(1, 1)
                                cross_max(0)
                                low_of(1, 2)
                                cross_max(1)
                                low_of(1, 3)
                                for v in range(8):
                                    if v + 2 < 8:
                                        cross_max(v + 2)
                                    probs_low(v)
                                    if v >= 2 and v % 2 == 0:
                                        output(v // 2 - 1)
                                if not last:
                                    residual1(n + 1, c + 1, 0)
                                    residual1(n + 1, c + 1, 1)
                                output(TPC - 1)
                                low_of(2, 0)
                                if not last:
                                    residual1(n + 1, c + 1, 2)
                                low_of(2, 1)
                                if not last:
                                    norm(0, n + 1, c + 1, 0)
                                    norm(0, n + 1, c + 1, 1)
                                residual2(n, c, 0)
                                if not last:
                                    residual1(n + 1, c + 1, 3)
                                low_of(2, 2)
                                if not last:
                                    norm(0, n + 1, c + 1, 2)
                                residual2(n, c, 1)
                                if not last:
                                    norm(0, n + 1, c + 1, 3)
                                low_of(2, 3)
                                residual2(n, c, 2)
                                norm(1, n, c, 0)
                                residual2(n, c, 3)
                                for j in range(1, TPC):
                                    norm(1, n, c, j)

                            for j in range(TPC):
                                residual1(b * CH, 0, j)
                                if j:
                                    norm(0, b * CH, 0, j - 1)
                            norm(0, b * CH, 0, TPC - 1)
                            bodies(dve, body)
                            for i, (_, j) in enumerate(LAST):
                                toks = slice((CH - 1) * CT + j * P, (CH - 1) * CT + j * P + P)
                                low(LAST0, i, x2tl[:, :, toks], x2th[:, :, toks])

                with ExitStack() as ph:
                    stage = [sb(ph, f"stage_f{i}", [P, 2, D], F32) for i in range(4)]
                    names = ("w10", "w11", "w20", "w21")
                    wh = {n_: sb(ph, f"fwh_{n_}", [P, DC, D], F16) for n_ in names}
                    wl = {n_: sb(ph, f"fwl_{n_}", [P, DC, D], F16) for n_ in names}
                    col = sb(ph, "col", [P, DC], F32)
                    sc = sb(ph, "sc", [1, E], F32)
                    best = sb(ph, "best", [1, 8], F32)
                    idx = sb(ph, "idx", [1, 8], U32)
                    b1c = sb(ph, "b1c", [P, 2, DC], F32)
                    b2r = sb(ph, "b2r", [P, 2, D], F32)
                    b2s = sb(ph, "b2s", [P, 2, D], F32)
                    g32 = sb(ph, "g32", [P, 2, CT], F32)
                    gh = sb(ph, "gh", [P, 2, DC, CT], F16)
                    gl = sb(ph, "gl", [P, 2, DC, CT], F16)
                    yt = sb(ph, "yt_f", [P, 2, D], F32)
                    F1 = banks[0:2]
                    F2 = banks[2:4]
                    block = ph.enter_context(nc.Block())

                    @block.sync
                    def _(sp):
                        sp.wait_ge(r_idx, b + 1)
                        sp.nop(nofuse=True)
                        expert = [sp.value_load(idx[0:1, k:k + 1], min_val=0, max_val=E - 1) for k in range(2)]

                        def rows_of(w, e):
                            v = w[bass.ds(e, 1), :, :].rearrange("a (c p) n -> p (a c) n", p=P)
                            return [[v[64 * half:64 * half + 64, 2 * i:2 * i + 2, :] for half in range(2)]
                                    for i in range(2)]

                        src = {"w10": rows_of(w1, expert[0]), "w11": rows_of(w1, expert[1]),
                               "w20": rows_of(w2, expert[0]), "w21": rows_of(w2, expert[1])}
                        for k in range(2):
                            sp.dma_start(b1c[:, k, :], b1[bass.ds(expert[k], 1), :, :].rearrange("a p c -> p (a c)"))\
                                .then_inc(f_b, 16)
                            sp.dma_start(b2r[:, k, :], b2[bass.ds(expert[k], 1), :].broadcast_to([P, D])).then_inc(f_b, 16)
                        load_pieces(sp, b, PIECES_P4, stage, src)
                        with sp.Fori(0, CH) as c:
                            n = b * CH + c
                            for j in range(TPC):
                                sp.wait_ge(f_y, n * TPC + j + 3)
                                sp.dma_start(out_rows[bass.ds(n * CT + j * P, P), :], yt[:, j % 2, :])\
                                    .then_inc(y_out[j % 2], 16)
                        for s in range(2):
                            sp.wait_ge(y_out[s], (b + 1) * (CH * 32) + 16)
                        sp.nop(nofuse=True)

                    @block.gpsimd
                    def _(pool):
                        pool.wait_ge(f_b2, 2 * b + 2)
                        pool.nop(nofuse=True)
                        with pool.Fori(0, CH) as c:
                            n = b * CH + c
                            for j in range(TPC):
                                cols = bass.ds(c * (TPC * D) + j * D, D)
                                pool.tensor_tensor(x2[:, cols], x2[:, cols], b2s[:, 1, :], ALU.add).then_inc(f_xb, 1)

                    @block.tensor
                    def _(pe):
                        pe.wait_ge(r_col, b + 1)
                        for d in range(DC):
                            mm = pe.matmul(F1[0][0:1, 0:E], col[:, d:d + 1], wr_sb[:, d, :], start=(d == 0),
                                           stop=(d == DC - 1))
                        mm.then_inc(r_mm, 1)
                        pe.wait_ge(r_sc, b + 1)
                        pe.nop(nofuse=True)
                        with pe.Fori(0, CH) as c:
                            n = b * CH + c
                            toks = bass.ds(c * CT, CT)
                            for w in range(8):
                                k, ec = w // DC, w % DC
                                pe.wait_ge(f_g, n * 8 + w + 1)
                                if ec == 0:
                                    pe.wait_ge(w_split, pieces_split(b, PIECES_P4[:2 * k + 2]))
                                ecols = slice(ec * P, ec * P + P)
                                mm3(pe, F1[w % 2][:, :], lambda d: wh[f"w1{k}"][:, d, ecols],
                                    lambda d: wl[f"w1{k}"][:, d, ecols], lambda d: x2th[:, d, toks],
                                    lambda d: x2tl[:, d, toks]).then_inc(f1_done, 1)
                            pe.wait_ge(w_split, pieces_split(b, PIECES_P4))
                            for j in range(TPC):
                                pe.wait_ge(f_y, n * TPC + j + 1)
                                cols = slice(j * P, j * P + P)
                                for w in range(8):
                                    k, ec = w // DC, w % DC
                                    if j == 0:
                                        pe.wait_ge(f_gl, n * 8 + w + 1)
                                    bank = F2[j % 2][:, :]
                                    pe.matmul(bank, gh[:, k, ec, cols], wh[f"w2{k}"][:, ec, :], start=(w == 0),
                                              stop=False)
                                    pe.matmul(bank, gh[:, k, ec, cols], wl[f"w2{k}"][:, ec, :], start=False,
                                              stop=False)
                                    mm = pe.matmul(bank, gl[:, k, ec, cols], wh[f"w2{k}"][:, ec, :], start=False,
                                                   stop=(w == 7))
                                mm.then_inc(f2_done, 1)

                    @block.scalar
                    def _(act):
                        split_high(act, b, PIECES_P4[:4], stage, wh)
                        act.wait_ge(f_b, b * 64 + 64)
                        act.nop(nofuse=True)
                        act.preload_act_table(ACT.Gelu)

                        def chunk(c, splits):
                            n = b * CH + c
                            for w in range(8):
                                k, ec = w // DC, w % DC
                                act.wait_ge(f1_done, n * 8 + w + 1)
                                if w >= 2:
                                    act.wait_ge(f_gl, n * 8 + w - 1)
                                act.activation(g32[:, w % 2, :], F1[w % 2][:, :], ACT.Gelu, bias=b1c[:, k, ec:ec + 1],
                                               scale=INV_WS).then_inc(f_g, 1)
                                if splits and w < 4:
                                    split_high(act, b, PIECES_P4[4 + w:5 + w], stage, wh)

                        chunk(0, True)
                        with act.Fori(1, CH) as c:
                            chunk(c, False)

                    @block.vector
                    def _(dve):
                        dve.tensor_tensor(col[:, :], x2th[:, :, 0], x2tl[:, :, 0], ALU.add).then_inc(r_col, 1)
                        dve.wait_ge(r_mm, b + 1)
                        dve.tensor_tensor(sc[:, :], F1[0][0:1, 0:E], br_sb[:, :], ALU.add).then_inc(r_sc, 1)
                        dve.wait_ge(r_sc, b + 1)
                        dve.nop(nofuse=True)
                        dve.max(best[:, :], sc[:, :]).then_inc(r_top, 1)
                        dve.wait_ge(r_top, b + 1)
                        dve.nop(nofuse=True)
                        dve.max_index(idx[:, :], best[:, :], sc[:, :]).then_inc(r_idx, 1)
                        split_low(dve, b, PIECES_P4[:4], stage, wh, wl)
                        dve.wait_ge(f_b, b * 64 + 64)
                        dve.tensor_tensor(b2s[:, 0, :], b2r[:, 0, :], b2r[:, 1, :], ALU.add).then_inc(f_b2, 1)
                        dve.wait_ge(f_b2, 2 * b + 1)
                        dve.tensor_scalar(b2s[:, 1, :], b2s[:, 0, :], 0.5, None, ALU.mult).then_inc(f_b2, 1)

                        def chunk(c, splits):
                            n = b * CH + c
                            dve.wait_ge(f2_done, n * TPC + 4)
                            for w in range(8):
                                k, ec = w // DC, w % DC
                                dve.wait_ge(f_g, n * 8 + w + 3)
                                dve.tensor_copy(gh[:, k, ec, :], g32[:, w % 2, :]).then_inc(f_gh, 1)
                                dve.wait_ge(f_gh, n * 8 + w + 1)
                                dve.tensor_tensor(gl[:, k, ec, :], g32[:, w % 2, :], gh[:, k, ec, :], ALU.subtract)\
                                    .then_inc(f_gl, 1)
                                if splits and w < 4:
                                    split_low(dve, b, PIECES_P4[4 + w:5 + w], stage, wh, wl)
                            for j in range(TPC):
                                cols = bass.ds(c * (TPC * D) + j * D, D)
                                dve.wait_ge(f2_done, n * TPC + j + 5)
                                dve.wait_ge(f_xb, n * TPC + j + 1)
                                dve.wait_ge(y_out[j % 2], n * 32 + 16 * (j // 2) + 16)
                                dve.scalar_tensor_tensor(out=yt[:, j % 2, :], in0=F2[j % 2][:, :], scalar=0.5 * INV_WS,
                                                         in1=x2[:, cols], op0=ALU.mult, op1=ALU.add).then_inc(f_y, 1)

                        chunk(0, True)
                        with dve.Fori(1, CH) as c:
                            chunk(c, False)


_INS = ["x", "ctx_1024", "L0_attn_ln_gamma", "L0_attn_ln_beta", "L0_attn_q_gamma", "L0_attn_k_gamma", "L0_attn_w_q",
        "L0_attn_w_k", "L0_attn_w_v", "L0_attn_w_o", "L0_attn_b_o", "L0_xattn_Wq", "L0_xattn_bq", "L0_xattn_Wk",
        "L0_xattn_bk", "L0_xattn_Wv", "L0_xattn_bv", "L0_xattn_Wo", "L0_xattn_bo", "L0_ffn_Wr", "L0_ffn_br",
        "L0_ffn_W1", "L0_ffn_b1", "L0_ffn_W2", "L0_ffn_b2"]
_TRANSPOSED = ("L0_attn_w_q", "L0_attn_w_k", "L0_attn_w_v", "L0_attn_w_o")


def kernel(**inputs):
    import numpy as _np
    import concourse.bacc as _bacc
    from concourse import mybir as _mybir
    from concourse.bass_utils import run_bass_kernel_spmd as _run

    nc = _bacc.Bacc("TRN2", target_bir_lowering=False, num_devices=1)
    arrays, args = {}, []
    for name in _INS:
        a = _np.asarray(inputs[name])
        if name == "L0_ffn_b1":
            a = a.reshape(a.shape[0], -1, P).transpose(0, 2, 1)
        a = _np.ascontiguousarray(a.T if name in _TRANSPOSED else a)
        arrays[f"in_{name}"] = a
        args.append(nc.dram_tensor(f"in_{name}", a.shape, _mybir.dt.from_np(a.dtype), kind="ExternalInput").ap())
    shape = inputs["x"].shape
    y = nc.dram_tensor("out_0", shape, _mybir.dt.from_np(_np.dtype("float32")), kind="ExternalOutput").ap()
    decoder_layer(nc, *args, y)
    r = _run(nc, [arrays], core_ids=[0])
    return r.results[0]["out_0"]
```

```python
from contextlib import ExitStack

import concourse.bass as bass
from concourse import mybir

F32 = mybir.dt.float32
F16 = mybir.dt.float16
U32 = mybir.dt.uint32
ALU = mybir.AluOpType
ACT = mybir.ActivationFunctionType
AX_X = mybir.AxisListType.X

P = 128
WS = 64.0
INV_WS = 1.0 / WS
PSHIFT = 6.93
LN_EPS = 1e-5
RMS_EPS = 1e-8


def decoder_layer(nc, x, ctx_in, ln_g, ln_b, q_gamma, k_gamma, w_q, w_k, w_v, w_o, b_o,
                  xw_q, xb_q, xw_k, xb_k, xw_v, xb_v, xw_o, xb_o, wr, br, w1, b1, w2, b2, out):
    B, N, D = x.shape
    DC = D // P
    DH = q_gamma.shape[0]
    H = D // DH
    TPC = 4
    CT = TPC * P
    CH = N // CT
    KB = N // P
    CTX = ctx_in.shape[1]
    XH = 16
    XD = D // XH
    E = wr.shape[1]
    XSCALE = float(XD) ** -0.5
    assert D == 512 and DH == 64 and CTX == P and N == 2048 and KB == 16

    x_rows = x.rearrange("b n d -> (b n) d")
    out_rows = out.rearrange("b n d -> (b n) d")
    ctx_rows = ctx_in.rearrange("b n d -> (b n) d")

    def by_rows(w):
        v = w.rearrange("(c p) n -> p c n", p=P)
        return [[v[0:64, 2 * i:2 * i + 2, :], v[64:128, 2 * i:2 * i + 2, :]] for i in range(2)]

    PIECES_P1 = [(n, i) for n in ("q", "k", "v") for i in range(2)]
    PIECES_P3 = [(n, i) for n in ("xk", "xv", "o", "xq", "xo") for i in range(2)]
    PIECES_P4 = [(n, i) for n in ("w10", "w11", "w20", "w21") for i in range(2)]
    PIECES = PIECES_P1 + PIECES_P3 + PIECES_P4
    NP = len(PIECES)
    PHASES = ((PIECES_P1, range(6)), (PIECES_P3, [*range(H), 2, 3]), (PIECES_P4, [*range(4)] * 2))
    use, taken = [], [0] * H
    for pieces_, slots in PHASES:
        first_piece = len(use)
        for slot in slots:
            taken[slot] += 1
            same = [w for w in range(first_piece, len(use)) if use[w][0] == slot]
            use.append((slot, taken[slot], same[-1] if same else None))
    assert len(use) == NP
    source = {"q": by_rows(w_q), "k": by_rows(w_k), "v": by_rows(w_v), "xk": by_rows(xw_k), "xv": by_rows(xw_v),
              "o": by_rows(w_o), "xq": by_rows(xw_q), "xo": by_rows(xw_o)}

    with ExitStack() as top:
        def sem(name):
            return top.enter_context(nc.semaphore(name))

        def sb(ctx, name, shape, dt):
            return ctx.enter_context(nc.sbuf_tensor(name, shape, dt))

        banks = [top.enter_context(nc.psum_tensor(f"bank{i}", [P, 512], F32)) for i in range(8)]

        ident = sb(top, "ident", [P, P], F32)
        ident16 = sb(top, "ident16", [P, P], F16)
        neg_half = sb(top, "neg_half", [P, 2 * H], F32)
        qg0 = sb(top, "qg0", [P, 1], F32)
        qg = sb(top, "qg", [P, 1], F32)
        kg = sb(top, "kg", [P, 1], F32)
        wr_sb = sb(top, "wr_sb", [P, DC, E], F32)
        br_sb = sb(top, "br_sb", [1, E], F32)
        q_hh = sb(top, "q_hh", [P, H, N], F16)

        q_lm = sb(top, "q_lm", [P, H, N], F16)
        x2 = q_lm[:, :, :].rearrange("p h n -> p (h n)").bitcast(F32)
        stage3 = [x2[:, h * 2 * D:(h + 1) * 2 * D].rearrange("p (c n) -> p c n", c=2) for h in range(H)]

        s_const = sem("s_const")
        s_pool = sem("s_pool")
        s_setup = sem("s_setup")
        w_loaded = [sem(f"w_loaded{i}") for i in range(H)]
        wh_ready = sem("wh_ready")
        w_split = sem("w_split")

        def bcast(v):
            return v.rearrange("(a n) -> a n", a=1).broadcast_to([P, v.shape[0]])

        def load_pieces(sp, b, pieces, stage, src):
            for piece in pieces:
                w = PIECES.index(piece)
                slot, _, before = use[w]
                if before is not None:
                    sp.wait_ge(w_split, b * NP + before + 1)
                for half in range(2):
                    sp.dma_start(stage[slot][64 * half:64 * half + 64, :, :], src[piece[0]][piece[1]][half])\
                        .then_inc(w_loaded[slot], 16)

        def split_high(act, b, pieces, stage, wh):
            for piece in pieces:
                w = PIECES.index(piece)
                slot, nth, _ = use[w]
                act.wait_ge(w_loaded[slot], b * (32 * taken[slot]) + 32 * nth)
                act.activation(wh[piece[0]][:, 2 * piece[1]:2 * piece[1] + 2, :], stage[slot][:, :, :], ACT.Copy,
                               scale=WS).then_inc(wh_ready, 1)

        def split_low(dve, b, pieces, stage, wh, wl):
            for piece in pieces:
                w = PIECES.index(piece)
                part = slice(2 * piece[1], 2 * piece[1] + 2)
                dve.wait_ge(wh_ready, b * NP + w + 1)
                dve.scalar_tensor_tensor(out=wl[piece[0]][:, part, :], in0=stage[use[w][0]][:, :, :], scalar=WS,
                                         in1=wh[piece[0]][:, part, :], op0=ALU.mult, op1=ALU.subtract)\
                    .then_inc(w_split, 1)

        def pieces_split(b, pieces):
            return b * NP + PIECES.index(pieces[-1]) + 1

        def mm3(pe, bank, xh, xl, wh, wl, last=None):
            for c in range(DC):
                pe.matmul(bank, xh(c), wh(c), start=(c == 0), stop=False)
                pe.matmul(bank, xh(c), wl(c), start=False, stop=False)
                mm = pe.matmul(bank, xl(c), wh(c), start=False, stop=(c == DC - 1))
            return mm

        a_const = sem("a_const")
        a_ones = sem("a_ones")
        a_x_in = [sem(f"a_x_in{i}") for i in range(2)]
        a_bn = sem("a_bn")
        a_stat = sem("a_stat")
        a_var = sem("a_var")
        a_rs = sem("a_rs")
        a_y = sem("a_y")
        a_xg = sem("a_xg")
        a_xn = sem("a_xn")
        a_t_done = sem("a_t_done")
        a_xh = sem("a_xh")
        a_xl = sem("a_xl")
        a_q_done = sem("a_q_done")
        a_k_done = sem("a_k_done")
        a_v_done = sem("a_v_done")
        a_sq = sem("a_sq")
        a_vh = sem("a_vh")
        a_v_ready = sem("a_v_ready")
        a_ssq = sem("a_ssq")
        a_ms = sem("a_ms")
        a_pow = sem("a_pow")
        a_rinv = sem("a_rinv")
        a_qk = sem("a_qk")
        a_ht_done = sem("a_ht_done")
        a_hh = sem("a_hh")
        a_ht_free = sem("a_ht_free")
        a_dup = sem("a_dup")
        s_ready = sem("s_ready")
        p_ready = sem("p_ready")
        ph_ready = sem("ph_ready")
        pl_ready = sem("pl_ready")
        p_free = sem("p_free")
        mx_ready = sem("mx_ready")
        mx_free = sem("mx_free")
        gm_ready = sem("gm_ready")
        nm_ready = sem("nm_ready")
        mrow_done = sem("mrow_done")
        m_ready = sem("m_ready")
        o_rec = sem("o_rec")
        o_norm = sem("o_norm")
        o_moved = sem("o_moved")
        o_high = sem("o_high")
        o_low = sem("o_low")
        o_free = sem("o_free")
        vs_ones = sem("vs_ones")
        vs_half = sem("vs_half")
        vs_ready = sem("vs_ready")
        c_ctx = sem("c_ctx")
        c_in = sem("c_in")
        c_zero = sem("c_zero")
        c_t = sem("c_t")
        c_h = sem("c_h")
        c_l = sem("c_l")
        c_mm = sem("c_mm")
        c_tok = sem("c_tok")
        d_x_in = [sem(f"d_x_in{i}") for i in range(TPC)]
        d_xb = sem("d_xb")
        d_o_done = sem("d_o_done")
        d_q_done = sem("d_q_done")
        d_xo_done = sem("d_xo_done")
        d_x1 = sem("d_x1")
        d_x2 = sem("d_x2")
        d_xb2 = sem("d_xb2")
        d_bn, d_stat, d_var, d_rs = ([sem(f"{name}{s}") for s in range(2)] for name in ("d_bn", "d_stat", "d_var", "d_rs"))
        d_n0 = sem("d_n0")
        d_n1 = sem("d_n1")
        d_q = sem("d_q")
        d_o = sem("d_o")
        d_t_done = sem("d_t_done")
        d_th = sem("d_th")
        d_tl = sem("d_tl")
        d_s_done = sem("d_s_done")
        d_nmx = sem("d_nmx")
        d_ex = sem("d_ex")
        d_pt_done = sem("d_pt_done")
        d_pth = [sem(f"d_pth{i}") for i in range(2)]
        d_ptl = sem("d_ptl")
        d_av_done = sem("d_av_done")
        d_rec = sem("d_rec")
        r_col = sem("r_col")
        r_mm = sem("r_mm")
        r_sc = sem("r_sc")
        r_top = sem("r_top")
        r_idx = sem("r_idx")
        f_b = sem("f_b")
        f_b2 = sem("f_b2")
        f_xb = sem("f_xb")
        f1_done = sem("f1_done")
        f_g = sem("f_g")
        f_gh = sem("f_gh")
        f_gl = sem("f_gl")
        f2_done = sem("f2_done")
        f_y = sem("f_y")
        y_out = [sem(f"y_out{i}") for i in range(2)]

        with nc.Block() as block:
            @block.sync
            def _(sp):
                for half in (0, DH):
                    sp.dma_start(qg0[half:half + DH, :], q_gamma.rearrange("(d a) -> d a", a=1)).then_inc(s_const, 16)
                    sp.dma_start(kg[half:half + DH, :], k_gamma.rearrange("(d a) -> d a", a=1)).then_inc(s_const, 16)
                sp.dma_start(wr_sb[:, :, :], wr.rearrange("(c p) e -> p c e", p=P)).then_inc(s_const, 16)
                sp.dma_start(br_sb[:, :], br.rearrange("(a e) -> a e", a=1)).then_inc(s_const, 16)
                sp.wait_ge(s_const, 16 * 6)

            @block.gpsimd
            def _(pool):
                pool.memset(ident[:, :], 0.0).then_inc(s_pool, 1)
                pool.memset(neg_half[:, :], -0.5).then_inc(s_pool, 1)
                pool.wait_ge(s_pool, 2)
                pool.affine_select(out=ident[:, :], in_=ident[:, :], compare_op=ALU.not_equal, fill=1.0, base=0,
                                   pattern=[[-1, P]], channel_multiplier=1).then_inc(s_pool, 1)
                for s, credits in ((a_y, 2), (a_v_ready, 1), (a_ssq, 1), (a_ht_free, 2), (p_free, 4), (mx_free, 4),
                                   (o_free, 8), (d_x1, 4), (d_tl, 2), (d_pt_done, 2), (d_ptl, 2),
                                   (f_g, 2), (f2_done, 4), (f_y, 2), (y_out[0], 16), (y_out[1], 16)):
                    pool.sem_inc(s, credits)

            @block.vector
            def _(dve):
                dve.wait_ge(s_pool, 3)
                dve.tensor_copy(ident16[:, :], ident[:, :]).then_inc(s_setup, 1)
                dve.wait_ge(s_const, 16 * 6)
                dve.tensor_scalar(qg[:, :], qg0[:, :], float(DH) ** -0.5, None, ALU.mult).then_inc(s_setup, 1)

        with nc.Fori(0, B) as b:
            with ExitStack() as attn:
                k_h1 = sb(attn, "k_h1", [P, H, N], F16)
                k_hl = sb(attn, "k_hl", [P, H, N], F16)
                v_h = sb(attn, "v_h", [P, KB * D], F16)
                v_l = sb(attn, "v_l", [P, KB * D], F16)

                with ExitStack() as ph:
                    lng = sb(ph, "lng", [P, D], F32)
                    lnb = sb(ph, "lnb", [P, D], F32)
                    stage = [v[:, :].bitcast(F32).rearrange("p (s c n) -> p s c n", c=2, n=D)[:, i] for v, i in
                             [(v_h, i) for i in range(4)] + [(v_l, i) for i in range(2)]]
                    wh = {n: sb(ph, f"wh_{n}", [P, DC, D], F16) for n in ("q", "k", "v")}
                    wl = {n: sb(ph, f"wl_{n}", [P, DC, D], F16) for n in ("q", "k", "v")}
                    xt = sb(ph, "xt_a", [P, 2, D], F32)
                    yt = sb(ph, "yt_a", [P, 2, D], F32)
                    st = sb(ph, "st_a", [P, 2, 6], F32)
                    mv = sb(ph, "mv_a", [P, 2, 2], F32)
                    rs = sb(ph, "rs_a", [P, 2, 2], F32)
                    xth = sb(ph, "xth_a", [P, 2, D], F16)
                    xtl = sb(ph, "xtl_a", [P, 2, D], F16)
                    ssq = sb(ph, "ssq", [P, 2 * H], F32)
                    ms = sb(ph, "ms", [P, 2 * H], F32)
                    rp = sb(ph, "rp", [P, 2 * H], F32)
                    rinv = sb(ph, "rinv", [P, 2 * H], F32)
                    sq = sb(ph, "sq", [P, D], F32)
                    qkn = sb(ph, "qkn", [P, 2, D], F32)
                    HT = banks[0:2]
                    TB = banks[2]
                    QB = banks[3:5]
                    KBK = banks[5:7]
                    VB = banks[7]
                    block = ph.enter_context(nc.Block())

                    T0 = b * KB

                    def over_tiles(eng, step):
                        step(0, 0, False, True, True)
                        with eng.Fori(0, KB // 2 - 2) as pair:
                            step(pair * 2 + 1, 1, True, True, True)
                            step(pair * 2 + 2, 0, True, True, True)
                        step(KB - 3, 1, True, True, True)
                        step(KB - 2, 0, True, True, False)
                        step(KB - 1, 1, True, False, False)

                    @block.sync
                    def _(sp):
                        def load_x(t, s):
                            sp.wait_ge(a_y, T0 + t + 1)
                            sp.dma_start(xt[:, s, :], x_rows[bass.ds((T0 + t) * P, P), :]).then_inc(a_x_in[s], 16)

                        for t in range(2):
                            load_x(t, t)
                        sp.dma_start(lng[:, :], bcast(ln_g)).then_inc(a_const, 16)
                        sp.dma_start(lnb[:, :], bcast(ln_b)).then_inc(a_const, 16)
                        load_pieces(sp, b, PIECES_P1, stage, source)
                        with sp.Fori(1, KB // 2) as pair:
                            for s in range(2):
                                load_x(pair * 2 + s, s)

                    @block.gpsimd
                    def _(pool):
                        def norm_scale(t, s):
                            pool.wait_ge(a_stat, T0 + t + 1)
                            pool.nop(nofuse=True)
                            pool.tensor_scalar(rs[:, 0, s:s + 1], mv[:, s, 1:2], 1.0 + LN_EPS,
                                               LN_EPS * LN_EPS, ALU.mult, ALU.add).then_inc(a_var, 1)
                            pool.wait_ge(a_var, T0 + t + 1)
                            pool.tensor_tensor(rs[:, 1, s:s + 1], rs[:, 0, s:s + 1], neg_half[:, 0:1], ALU.pow)\
                                .then_inc(a_rs, 1)

                        def affine(t, s):
                            pool.wait_ge(a_y, T0 + t + 3)
                            pool.tensor_tensor(yt[:, s, :], yt[:, s, :], lng[:, :], ALU.mult).then_inc(a_xg, 1)
                            pool.wait_ge(a_xg, T0 + t + 1)
                            pool.tensor_tensor(yt[:, s, :], yt[:, s, :], lnb[:, :], ALU.add).then_inc(a_xn, 1)

                        def rms_scale(t, which):
                            i = (T0 + t) * 2 + which + 1
                            part = slice(which * H, which * H + H)
                            pool.wait_ge(a_ssq, i + 1)
                            pool.nop(nofuse=True)
                            pool.tensor_scalar(ms[:, part], ssq[:, part], 1.0 / DH, RMS_EPS * RMS_EPS, ALU.mult, ALU.max)\
                                .then_inc(a_ms, 1)
                            pool.wait_ge(a_ms, i)
                            pool.tensor_tensor(rp[:, part], ms[:, part], neg_half[:, part], ALU.pow).then_inc(a_pow, 1)
                            pool.wait_ge(a_pow, i)
                            pool.nop(nofuse=True)
                            pool.tensor_scalar(rinv[:, part], rp[:, part], INV_WS, None, ALU.mult).then_inc(a_rinv, 1)

                        def step(t, s, before, next1, next2):
                            if next2:
                                norm_scale(t + 2, s)
                            rms_scale(t, 0)
                            if next2:
                                affine(t + 2, s)
                            rms_scale(t, 1)

                        pool.wait_ge(a_const, 32 * (b + 1))
                        pool.nop(nofuse=True)
                        for t in range(2):
                            norm_scale(t, t)
                            affine(t, t)
                        over_tiles(pool, step)

                    @block.tensor
                    def _(pe):
                        def transposes(t, s, first=False):
                            pe.wait_ge(a_xn, T0 + t + 1)
                            if not first:
                                pe.wait_ge(a_xl, T0 + t)
                            for d in range(DC):
                                mm = pe.transpose(TB[:, d * P:(d + 1) * P], yt[:, s, d * P:(d + 1) * P], ident[:, :])
                            mm.then_inc(a_t_done, 1)

                        def project(s, name, bank, done):
                            mm3(pe, bank[:, :],
                                lambda d: xth[:, s, d * P:(d + 1) * P], lambda d: xtl[:, s, d * P:(d + 1) * P],
                                lambda d: wh[name][:, d, :], lambda d: wl[name][:, d, :]).then_inc(done, 1)

                        def head_transposes(t):
                            for which in range(2):
                                pe.wait_ge(a_qk, (T0 + t) * 2 + which + 1)
                                pe.wait_ge(a_ht_free, (T0 + t) * 2 + which + 1)
                                for d in range(DC):
                                    mm = pe.transpose(HT[which][:, d * P:(d + 1) * P],
                                                      qkn[:, which, d * P:(d + 1) * P], ident[:, :])
                                mm.then_inc(a_ht_done, 1)

                        def step(t, s, before, next1, next2):
                            pe.wait_ge(a_xl, T0 + t + 1)
                            if not before:
                                pe.wait_ge(w_split, pieces_split(b, PIECES_P1[:2]))
                            project(s, "q", QB[s], a_q_done)
                            if next1:
                                transposes(t + 1, 1 - s)
                            if not before:
                                pe.wait_ge(w_split, pieces_split(b, PIECES_P1[:4]))
                            project(s, "k", KBK[s], a_k_done)
                            if before:
                                head_transposes(t - 1)
                            pe.wait_ge(a_v_ready, T0 + t + 1)
                            if not before:
                                pe.wait_ge(w_split, pieces_split(b, PIECES_P1))
                            project(s, "v", VB, a_v_done)

                        transposes(0, 0, first=True)
                        over_tiles(pe, step)
                        head_transposes(KB - 1)

                    @block.scalar
                    def _(act):
                        def x_high(t, s):
                            act.wait_ge(a_t_done, T0 + t + 1)
                            act.activation(xth[:, s, :], TB[:, :], ACT.Copy).then_inc(a_xh, 1)

                        def square(t, which, bank, done):
                            act.wait_ge(done, T0 + t + 1)
                            act.wait_ge(a_ssq, (T0 + t) * 2 + which + 1)
                            act.activation(sq[:, :], bank[:, :], ACT.Square, scale=INV_WS).then_inc(a_sq, 1)

                        def heads_high(t):
                            tok = bass.ds(t * P, P)
                            for which, (dst, g) in enumerate(((q_hh, qg), (k_h1, kg))):
                                act.wait_ge(a_ht_done, (T0 + t) * 2 + which + 1)
                                for odd in range(2):
                                    src = HT[which][DH * odd:DH * odd + DH, :].rearrange("p (h n) -> p h n", h=DC)
                                    act.activation(dst[0:DH, odd::2, tok], src, ACT.Copy,
                                                   scale=g[DH * odd:DH * odd + DH, :]).then_inc(a_hh, 1)

                        def step(t, s, before, next1, next2):
                            square(t, 0, QB[s], a_q_done)
                            if next1:
                                x_high(t + 1, 1 - s)
                            square(t, 1, KBK[s], a_k_done)
                            if before:
                                heads_high(t - 1)
                            act.wait_ge(a_v_done, T0 + t + 1)
                            act.activation(v_h[:, bass.ds(t * D, D)], VB[:, :], ACT.Copy, scale=INV_WS).then_inc(a_vh, 1)

                        split_high(act, b, PIECES_P1[:2], stage, wh)
                        x_high(0, 0)
                        split_high(act, b, PIECES_P1[2:], stage, wh)
                        over_tiles(act, step)
                        heads_high(KB - 1)

                    @block.vector
                    def _(dve):
                        def stats(t, s):
                            dve.wait_ge(a_x_in[s], T0 * 8 + (t // 2) * 16 + 16)
                            dve.nop(nofuse=True)
                            dve.bn_stats(st[:, s, :], xt[:, s, :]).then_inc(a_bn, 1)
                            dve.wait_ge(a_bn, T0 + t + 1)
                            dve.nop(nofuse=True)
                            dve.bn_aggr(mv[:, s, :], st[:, s, :]).then_inc(a_stat, 1)

                        def normalise(t, s, first=False):
                            dve.wait_ge(a_rs, T0 + t + 1)
                            if not first:
                                dve.wait_ge(a_t_done, T0 + t - 1)
                            dve.tensor_scalar(yt[:, s, :], xt[:, s, :], mv[:, s, 0:1], rs[:, 1, s:s + 1],
                                              ALU.subtract, ALU.mult).then_inc(a_y, 1)

                        def x_low(t, s):
                            dve.wait_ge(a_xh, T0 + t + 1)
                            dve.tensor_tensor(xtl[:, s, :], TB[:, :], xth[:, s, :], ALU.subtract).then_inc(a_xl, 1)

                        def sum_squares(t, which):
                            dve.wait_ge(a_sq, (T0 + t) * 2 + which + 1)
                            dve.tensor_reduce(ssq[:, which * H:which * H + H],
                                              sq[:, :].rearrange("p (h d) -> p h d", d=DH), AX_X, ALU.add)\
                                .then_inc(a_ssq, 1)

                        def heads_low(t):
                            tok = bass.ds(t * P, P)
                            for which, (high, low, row, g) in enumerate(((q_hh, q_lm, 0, qg), (k_h1, k_hl, DH, kg))):
                                for odd in range(2):
                                    dve.wait_ge(a_hh, (T0 + t) * 4 + 2 * which + odd + 1)
                                    src = HT[which][DH * odd:DH * odd + DH, :].rearrange("p (h n) -> p h n", h=DC)
                                    low_part = dve.scalar_tensor_tensor(
                                        out=low[row:row + DH, odd::2, tok], in0=src,
                                        scalar=g[DH * odd:DH * odd + DH, :], in1=high[0:DH, odd::2, tok],
                                        op0=ALU.mult, op1=ALU.subtract)
                                low_part.then_inc(a_ht_free, 1)
                                if which == 0:
                                    dve.tensor_copy(q_hh[DH:P, :, tok], q_hh[0:DH, :, tok]).then_inc(a_dup, 1)
                                else:
                                    dve.tensor_copy(k_hl[0:DH, :, tok], k_h1[0:DH, :, tok]).then_inc(a_dup, 1)

                        def scale_heads(t, s, before):
                            if before:
                                dve.wait_ge(a_ht_done, (T0 + t) * 2)
                            for which, bank in enumerate((QB[s], KBK[s])):
                                dve.wait_ge(a_rinv, (T0 + t) * 2 + which + 1)
                                dve.tensor_tensor(
                                    qkn[:, which, :].rearrange("p (h d) -> p h d", d=DH),
                                    bank[:, :].rearrange("p (h d) -> p h d", d=DH),
                                    rinv[:, which * H:which * H + H].rearrange("p (h a) -> p h a", a=1)
                                    .broadcast_to([P, H, DH]), ALU.mult).then_inc(a_qk, 1)

                        def v_low(t):
                            vcols = bass.ds(t * D, D)
                            dve.wait_ge(a_vh, T0 + t + 1)
                            dve.scalar_tensor_tensor(out=v_l[:, vcols], in0=VB[:, :], scalar=INV_WS,
                                                     in1=v_h[:, vcols], op0=ALU.mult, op1=ALU.subtract)\
                                .then_inc(a_v_ready, 1)

                        def step(t, s, before, next1, next2):
                            if next2:
                                stats(t + 2, s)
                            sum_squares(t, 0)
                            if next1:
                                x_low(t + 1, 1 - s)
                            if next2:
                                normalise(t + 2, s)
                            sum_squares(t, 1)
                            if before:
                                heads_low(t - 1)
                            v_low(t)
                            scale_heads(t, s, before)

                        for t in range(2):
                            stats(t, t)
                            normalise(t, t, first=True)
                        split_low(dve, b, PIECES_P1[:2], stage, wh, wl)
                        x_low(0, 0)
                        split_low(dve, b, PIECES_P1[2:], stage, wh, wl)
                        over_tiles(dve, step)
                        heads_low(KB - 1)

                with ExitStack() as ph:
                    vsh = sb(ph, "vsh", [P, 2 * KB * P], F16)
                    vsl = sb(ph, "vsl", [P, 2 * KB * P], F16)
                    probs = sb(ph, "probs", [P, 4, CT], F32)
                    probs_h = sb(ph, "probs_h", [P, 4, CT], F16)
                    probs_l = sb(ph, "probs_l", [P, 4, CT], F16)
                    pm = sb(ph, "pm", [P, 16], F32)
                    gm = sb(ph, "gm", [P, TPC], F32)
                    nm = sb(ph, "nm", [P, TPC], F16)
                    osb = sb(ph, "osb", [P, CT], F32)
                    rden = sb(ph, "rden", [DH, CT], F32)
                    onorm = sb(ph, "onorm", [P, CT], F32)
                    SB = banks[0:2]
                    MB = banks[2:6]
                    OB = banks[7]
                    RB = banks[6]
                    qf = q_hh[:, :, :].rearrange("p h n -> p (h n)")
                    lf = q_lm[:, :, :].rearrange("p h n -> p (h n)")
                    k1 = k_hl[:, :, :].rearrange("p h n -> p (h n)")
                    k2 = k_h1[:, :, :].rearrange("p h n -> p (h n)")
                    UNITS = H * CH
                    U0 = b * UNITS
                    LA = 2
                    MAXED = UNITS - LA
                    block = ph.enter_context(nc.Block())

                    @block.sync
                    def _(sp):
                        for h in range(H - 1):
                            sp.wait_ge(p_free, (U0 + (h + 1) * CH) * KB + 4)
                            sp.nop(nofuse=True)
                            load_pieces(sp, b, PIECES_P3[h:h + 1], stage3, source)
                        sp.nop(nofuse=True)

                    @block.gpsimd
                    def _(pool):
                        pool.memset(k_h1[DH:DH + 1, :, :], 1.0).then_inc(a_ones, 1)
                        pool.wait_ge(a_ones, b + 1)
                        pool.nop(nofuse=True)
                        with pool.Fori(0, UNITS) as u:
                            step = (U0 + u) * KB
                            for kb in range(KB):
                                pool.wait_ge(ph_ready, step + kb + 1)
                                pool.wait_ge(p_free, step + kb + 1)
                                pool.tensor_tensor(probs_l[:, kb % 4, :], probs[:, kb % 4, :], probs_h[:, kb % 4, :],
                                                   ALU.subtract).then_inc(pl_ready, 1)

                    @block.tensor
                    def _(pe):
                        def max_scores(k, qcol, kcol, count):
                            pe.wait_ge(mx_free, count + 1)
                            pe.matmul(MB[k % 4][:, :], qf[:, qcol], k1[:, kcol], start=True, stop=True)\
                                .then_inc(mx_ready, 1)

                        def max_row(r):
                            pe.wait_ge(nm_ready, r + 1)
                            for a in range(TPC):
                                mm = pe.matmul(RB[DH:DH + 1, a * P:(a + 1) * P], nm[:, a:a + 1], ident16[:, :],
                                               start=True, stop=True)
                            mm.then_inc(mrow_done, 1)

                        def scores(u, kb):
                            kcols, qcols = bass.ds(u // CH * N + kb * P, P), bass.ds(u * CT, CT)
                            pe.matmul(SB[kb % 2][:, :], k1[:, kcols], qf[:, qcols], start=True, stop=False)
                            pe.matmul(SB[kb % 2][:, :], k2[0:DH + 1, kcols], lf[0:DH + 1, qcols], start=False,
                                      stop=True).then_inc(s_ready, 1)

                        def unit_max(r, k):
                            max_scores(k, bass.ds(r * CT + k // 4 * P, P), bass.ds(r // CH * N + k % 4 * CT, CT),
                                       (U0 + r) * 16 + k)

                        def unit(u, maxed, first=False, last=False):
                            U = U0 + u
                            pe.wait_ge(vs_ready, U0 + u // CH * CH + CH)
                            for kb in range(KB):
                                pe.wait_ge(ph_ready, U * KB + kb + 1)
                                if kb + 2 < KB:
                                    scores(u, kb + 2)
                                elif not last:
                                    if kb + 2 == KB:
                                        pe.wait_ge(m_ready, U + 2)
                                    scores(u + 1, kb + 2 - KB)
                                if first:
                                    for k in range(2):
                                        unit_max(1 + kb // 8, kb % 8 * 2 + k)
                                elif maxed:
                                    unit_max(u + LA, kb)
                                if kb == (11 if first else 2) and (maxed or u == MAXED):
                                    max_row(U + LA - 1)
                                if kb == 0:
                                    pe.wait_ge(o_free, U + 8)
                                v0 = u // CH % 2 * (KB * P) + kb * P
                                pe.matmul(OB[:, :], vsl[:, bass.ds(v0, P)], probs_h[:, kb % 4, :],
                                          start=(kb == 0), stop=False)
                                pe.matmul(OB[0:DH, :], vsh[:, bass.ds(v0, DH)], probs_h[:, kb % 4, :],
                                          start=False, stop=False, skip_group_check=True)
                                pe.wait_ge(pl_ready, U * KB + kb + 1)
                                pe.matmul(OB[:, :], vsh[:, bass.ds(v0, P)], probs_l[:, kb % 4, :],
                                          start=False, stop=(kb == KB - 1)).then_inc(p_free, 1)

                        for k in range(16):
                            unit_max(0, k)
                        max_row(U0)
                        pe.wait_ge(m_ready, U0 + 1)
                        pe.wait_ge(a_ones, b + 1)
                        scores(0, 0)
                        scores(0, 1)
                        unit(0, True, first=True)
                        with pe.Fori(1, MAXED) as u:
                            unit(u, True)
                        for u in range(MAXED, UNITS):
                            unit(u, False, last=(u == UNITS - 1))

                    @block.scalar
                    def _(act):
                        act.preload_act_table(ACT.Exp)
                        with act.Fori(0, UNITS) as u:
                            step = (U0 + u) * KB
                            for kb in range(KB):
                                act.wait_ge(s_ready, step + kb + 1)
                                act.wait_ge(p_free, step + kb + 1)
                                act.activation(probs[:, kb % 4, :], SB[kb % 2][:, :], ACT.Exp).then_inc(p_ready, 1)
                                act.activation(probs_h[:, kb % 4, :], SB[kb % 2][:, :], ACT.Exp).then_inc(ph_ready, 1)

                    @block.vector
                    def _(dve):
                        def reduce_max(k, count):
                            dve.wait_ge(mx_ready, count + 1)
                            dve.tensor_reduce(pm[:, k:k + 1], MB[k % 4][:, :], AX_X, ALU.max).then_inc(mx_free, 1)

                        def negate_max(r):
                            dve.wait_ge(mx_free, r * 16 + 20)
                            dve.tensor_reduce(gm[:, :], pm[:, :].rearrange("p (a k) -> p a k", k=4), AX_X, ALU.max)\
                                .then_inc(gm_ready, 1)
                            dve.wait_ge(gm_ready, r + 1)
                            dve.tensor_scalar(nm[:, :], gm[:, :], -1.0, PSHIFT, ALU.mult, ALU.add).then_inc(nm_ready, 1)

                        def copy_row(r, cols):
                            dve.wait_ge(mrow_done, r + 1)
                            dve.tensor_copy(lf[DH:DH + 1, cols], RB[DH:DH + 1, :]).then_inc(m_ready, 1)

                        def copy_v(t):
                            cols = bass.ds(t * (KB // CH * P) % (2 * KB * P), KB // CH * P)
                            rows = bass.ds(t % CH * (KB // CH * D), KB // CH * D)
                            for i, (dst, src) in enumerate(((vsh, v_h), (vsl, v_l))):
                                dve.tensor_copy(dst[:, cols].rearrange("p (k n) -> p k n", n=P)[:, :, 0:DH],
                                                src[:, rows].rearrange("p (k d) -> p k d", d=D)
                                                [:, :, bass.ds(t // CH * DH, DH)])\
                                    .then_inc((vs_half, vs_ready)[i], 1)

                        AHEAD = 4
                        for i, v in enumerate((vsh, vsl)):
                            dve.memset(v[:, :].rearrange("p (k n) -> p k n", n=P)[:, :, DH:P], 1.0).then_inc(vs_ones, 1)
                        for t in range(CH):
                            copy_v(t)
                        for g in range(LA):
                            for k in range(16):
                                reduce_max(k, U0 * 16 + g * 16 + k)
                            negate_max(U0 + g)
                            if g < LA - 1:
                                copy_row(U0 + g, slice(g * CT, g * CT + CT))

                        def unit(u, odd, maxed, next_maxed, next_v):
                            U = U0 + u
                            for k in range(AHEAD, 16):
                                if maxed:
                                    reduce_max(k, (U + LA) * 16 + k)
                                if k == 4 and (maxed or u == MAXED):
                                    copy_row(U + LA - 1, bass.ds((u + LA - 1) * CT, CT))
                                if k == 8 and next_v:
                                    copy_v(u + CH)
                            if maxed:
                                negate_max(U + LA)
                            dve.wait_ge(p_free, (U + 1) * KB + 4)
                            dve.tensor_copy(osb[:, :], OB[:, :]).then_inc(o_free, 1)
                            if next_maxed:
                                reduce_max(0, (U + LA + 1) * 16)
                            dve.wait_ge(o_free, U + 9)
                            dve.reciprocal(rden[:, 0:CT // 2], osb[DH:P, 0:CT // 2]).then_inc(o_rec, 1)
                            if next_maxed:
                                reduce_max(1, (U + LA + 1) * 16 + 1)
                            dve.reciprocal(rden[:, CT // 2:CT], osb[DH:P, CT // 2:CT]).then_inc(o_rec, 1)
                            if next_maxed:
                                reduce_max(2, (U + LA + 1) * 16 + 2)
                            dve.wait_ge(o_rec, 2 * U + 2)
                            rows = slice(DH * odd, DH * odd + DH)
                            dve.tensor_tensor(onorm[rows, :], osb[0:DH, :], rden[:, :], ALU.mult).then_inc(o_norm, 1)
                            if next_maxed:
                                reduce_max(3, (U + LA + 1) * 16 + 3)
                            dve.wait_ge(o_norm, U + 1)
                            cols = bass.ds(u * CT, CT)
                            high = cols
                            if odd:
                                high = bass.ds((u - CH) * CT, CT)
                                dve.wait_ge(o_low, U - CH + 1)
                                dve.nop(nofuse=True)
                                dve.tensor_copy(qf[0:DH, cols], qf[DH:P, high]).then_inc(o_moved, 1)
                                dve.wait_ge(o_moved, b * (UNITS // 2) + u // (2 * CH) * CH + u % CH + 1)
                            dve.nop(nofuse=True)
                            dve.tensor_copy(qf[rows, high], onorm[rows, :]).then_inc(o_high, 1)
                            dve.wait_ge(o_high, U + 1)
                            dve.tensor_tensor(qf[DH:P, cols], onorm[rows, :], qf[rows, high], ALU.subtract)\
                                .then_inc(o_low, 1)

                        for k in range(AHEAD):
                            reduce_max(k, (U0 + LA) * 16 + k)
                        with dve.Fori(0, H // 2 - 1) as pair:
                            for odd in range(2):
                                with dve.Fori(0, CH) as qb:
                                    unit(pair * (2 * CH) + odd * CH + qb, odd, True, True, True)
                        for u in range(UNITS - 2 * CH, UNITS):
                            unit(u, u // CH % 2, u < MAXED, u + 1 < MAXED, u < UNITS - CH)

            with ExitStack() as mlp:
                x2th = sb(mlp, "x2th", [P, DC, N], F16)
                x2tl = sb(mlp, "x2tl", [P, DC, N], F16)

                with ExitStack() as ph:
                    wh = {n: sb(ph, f"dwh_{n}", [P, DC, D], F16) for n in ("o", "xq", "xo")}
                    wl = {n: sb(ph, f"dwl_{n}", [P, DC, D], F16) for n in ("o", "xq", "xo")}
                    kbh = sb(ph, "kbh", [P, DC, 4 * CTX], F16)
                    kbl = sb(ph, "kbl", [P, DC, 4 * CTX], F16)
                    vxh = sb(ph, "vxh", [P, D], F16)
                    vxl = sb(ph, "vxl", [P, D], F16)
                    bo_b = sb(ph, "bo_b", [P, D], F32)
                    xbq_b = sb(ph, "xbq_b", [P, D], F32)
                    xbo_b = sb(ph, "xbo_b", [P, D], F32)

                    OB4 = banks[4:8]

                    def out_project(pe, c, j):
                        o_cols = bass.ds(c * CT + j * P, P)
                        mm3(pe, OB4[j][:, :], lambda d: q_hh[:, 2 * d, o_cols], lambda d: q_hh[:, 2 * d + 1, o_cols],
                            lambda d: wh["o"][:, d, :], lambda d: wl["o"][:, d, :]).then_inc(d_o_done, 1)

                    xr = sb(ph, "xr", [P, TPC, D], F32)
                    tok0 = sb(ph, "tok0", [P, TPC, D], F32)
                    tok = sb(ph, "tok", [P, TPC, D], F32)
                    st = sb(ph, "st_d", [P, 2 * TPC, 6], F32)
                    mv = sb(ph, "mv_d", [P, 2 * TPC, 2], F32)
                    rs = sb(ph, "rs_d", [P, 2, 2 * TPC], F32)

                    def load_x(sp, n):
                        for j in range(TPC):
                            sp.wait_ge(d_x1, n * TPC + j + 1)
                            sp.dma_start(xr[:, j, :], x_rows[bass.ds(n * CT + j * P, P), :]).then_inc(d_x_in[j], 16)

                    def add_bo(pool, n, j):
                        pool.wait_ge(d_x_in[j], n * 16 + 16)
                        pool.tensor_tensor(xr[:, j, :], xr[:, j, :], bo_b[:, :], ALU.add).then_inc(d_xb, 1)

                    def norm_scale(pool, s, n, j):
                        k = s * TPC + j
                        pool.wait_ge(d_stat[s], n * TPC + j + 1)
                        pool.nop(nofuse=True)
                        pool.tensor_scalar(rs[:, 0, k:k + 1], mv[:, k, 1:2], LN_EPS, None, ALU.add)\
                            .then_inc(d_var[s], 1)
                        pool.wait_ge(d_var[s], n * TPC + j + 1)
                        pool.tensor_tensor(rs[:, 1, k:k + 1], rs[:, 0, k:k + 1], neg_half[:, 0:1], ALU.pow)\
                            .then_inc(d_rs[s], 1)

                    def stats(dve, s, n, j, src):
                        k = s * TPC + j
                        dve.bn_stats(st[:, k, :], src).then_inc(d_bn[s], 1)
                        dve.wait_ge(d_bn[s], n * TPC + j + 1)
                        dve.nop(nofuse=True)
                        dve.bn_aggr(mv[:, k, :], st[:, k, :]).then_inc(d_stat[s], 1)

                    def norm(dve, s, n, c, j):
                        k = s * TPC + j
                        dve.wait_ge(d_rs[s], n * TPC + j + 1)
                        dve.tensor_scalar((tok if s else tok0)[:, j, :],
                                          x2[:, bass.ds(c * (TPC * D) + j * D, D)], mv[:, k, 0:1],
                                          rs[:, 1, k:k + 1], ALU.subtract, ALU.mult)\
                            .then_inc(d_n1 if s else d_n0, 1)

                    def residual1(dve, n, c, j):
                        cols = bass.ds(c * (TPC * D) + j * D, D)
                        dve.wait_ge(d_xb, n * TPC + j + 1)
                        dve.wait_ge(d_o_done, n * TPC + j + 1)
                        dve.scalar_tensor_tensor(out=x2[:, cols], in0=OB4[j][:, :], scalar=INV_WS,
                                                 in1=xr[:, j, :], op0=ALU.mult, op1=ALU.add)\
                            .then_inc(d_x1, 1)
                        dve.wait_ge(d_x1, n * TPC + j + 5)
                        dve.nop(nofuse=True)
                        stats(dve, 0, n, j, x2[:, cols])

                    with ExitStack() as cp:
                        for n_ in ("xk", "xv"):
                            wh[n_] = sb(cp, f"cwh_{n_}", [P, DC, D], F16)
                            wl[n_] = sb(cp, f"cwl_{n_}", [P, DC, D], F16)
                        cx = sb(cp, "cx", [P, D], F32)
                        cth = sb(cp, "cth", [P, D], F16)
                        ctl = sb(cp, "ctl", [P, D], F16)
                        kx = sb(cp, "kx", [P, D], F32)
                        vx = sb(cp, "vx", [P, D], F32)
                        xbk_b = sb(cp, "xbk_b", [P, D], F32)
                        xbv_b = sb(cp, "xbv_b", [P, D], F32)
                        block = cp.enter_context(nc.Block())

                        @block.sync
                        def _(sp):
                            sp.dma_start(cx[:, :], ctx_rows[bass.ds(b * CTX, CTX), :]).then_inc(c_ctx, 16)
                            for dst, src in ((bo_b, b_o), (xbk_b, xb_k), (xbv_b, xb_v), (xbq_b, xb_q), (xbo_b, xb_o)):
                                sp.dma_start(dst[:, :], bcast(src)).then_inc(c_in, 16)
                            load_x(sp, b * CH)
                            load_pieces(sp, b, PIECES_P3[H - 1:], stage3, source)
                            sp.wait_ge(c_in, b * 80 + 80)
                            sp.nop(nofuse=True)

                        @block.gpsimd
                        def _(pool):
                            pool.memset(kbh[:, :, :], 0.0).then_inc(c_zero, 1)
                            pool.memset(kbl[:, :, :], 0.0).then_inc(c_zero, 1)
                            pool.wait_ge(c_in, b * 80 + 80)
                            for j in range(TPC):
                                add_bo(pool, b * CH, j)
                            for j in range(TPC):
                                norm_scale(pool, 0, b * CH, j)

                        @block.tensor
                        def _(pe):
                            def transposes(src):
                                for d in range(DC):
                                    mm = pe.transpose(banks[0][:, d * P:(d + 1) * P], src[:, d * P:(d + 1) * P],
                                                      ident[:, :])
                                mm.then_inc(c_t, 1)

                            def project(name, bank):
                                mm3(pe, bank[:, :], lambda d: cth[:, d * P:(d + 1) * P],
                                    lambda d: ctl[:, d * P:(d + 1) * P], lambda d: wh[name][:, d, :],
                                    lambda d: wl[name][:, d, :]).then_inc(c_mm, 1)

                            pe.wait_ge(c_ctx, b * 16 + 16)
                            transposes(cx)
                            pe.wait_ge(c_l, b * 6 + 1)
                            pe.wait_ge(w_split, pieces_split(b, PIECES_P3[:2]))
                            project("xk", banks[1])
                            pe.wait_ge(w_split, pieces_split(b, PIECES_P3[:4]))
                            project("xv", banks[2])
                            pe.wait_ge(c_tok, b * 2 + 1)
                            transposes(kx)
                            pe.wait_ge(w_split, pieces_split(b, PIECES_P3[:6]))
                            for j in range(TPC):
                                out_project(pe, 0, j)

                        @block.scalar
                        def _(act):
                            act.wait_ge(c_t, b * 2 + 1)
                            act.activation(cth[:, :], banks[0][:, :], ACT.Copy).then_inc(c_h, 1)
                            split_high(act, b, PIECES_P3[:6], stage3, wh)
                            act.wait_ge(c_zero, b * 2 + 2)
                            act.wait_ge(c_t, b * 2 + 2)
                            for a in range(4):
                                act.activation(kbh[32 * a:32 * a + 32, :, a * CTX:(a + 1) * CTX],
                                               banks[0][32 * a:32 * a + 32, :].rearrange("p (c n) -> p c n", c=DC),
                                               ACT.Copy, scale=XSCALE).then_inc(c_h, 1)
                            act.wait_ge(c_tok, b * 2 + 2)
                            act.activation(vxh[:, :], vx[:, :], ACT.Copy).then_inc(c_h, 1)
                            split_high(act, b, PIECES_P3[6:], stage3, wh)

                        @block.vector
                        def _(dve):
                            dve.wait_ge(c_h, b * 6 + 1)
                            dve.tensor_tensor(ctl[:, :], banks[0][:, :], cth[:, :], ALU.subtract).then_inc(c_l, 1)
                            split_low(dve, b, PIECES_P3[:4], stage3, wh, wl)
                            for i, (dst, bias) in enumerate(((kx, xbk_b), (vx, xbv_b))):
                                dve.wait_ge(c_mm, b * 2 + i + 1)
                                dve.wait_ge(c_in, b * 80 + 80)
                                dve.scalar_tensor_tensor(out=dst[:, :], in0=banks[1 + i][:, :], scalar=INV_WS,
                                                         in1=bias[:, :], op0=ALU.mult, op1=ALU.add).then_inc(c_tok, 1)
                                if i == 0:
                                    split_low(dve, b, PIECES_P3[4:6], stage3, wh, wl)
                            for a in range(4):
                                dve.wait_ge(c_h, b * 6 + 2 + a)
                                part = slice(32 * a, 32 * a + 32)
                                dve.scalar_tensor_tensor(out=kbl[part, :, a * CTX:(a + 1) * CTX],
                                                         in0=banks[0][part, :].rearrange("p (c n) -> p c n", c=DC),
                                                         scalar=XSCALE, in1=kbh[part, :, a * CTX:(a + 1) * CTX],
                                                         op0=ALU.mult, op1=ALU.subtract).then_inc(c_l, 1)
                            dve.wait_ge(c_h, b * 6 + 6)
                            dve.tensor_tensor(vxl[:, :], vx[:, :], vxh[:, :], ALU.subtract).then_inc(c_l, 1)
                            for j in range(TPC):
                                residual1(dve, b * CH, 0, j)
                                split_low(dve, b, PIECES_P3[6 + j:7 + j], stage3, wh, wl)
                                norm(dve, 0, b * CH, 0, j)

                    with ExitStack() as tp:
                        th = sb(tp, "th", [P, TPC, D], F16)
                        tl = sb(tp, "tl", [P, TPC, D], F16)
                        px = sb(tp, "px", [P, 2, 8 * CTX], F32)
                        pth = sb(tp, "pth", [P, 2, 8 * CTX], F16)
                        ptl = sb(tp, "ptl", [P, 2, 8 * CTX], F16)
                        nmx = sb(tp, "nmx", [P, 2, 8], F32)
                        sm = sb(tp, "sm", [P, TPC, XH], F32)
                        rsm = sb(tp, "rsm", [P, TPC, XH], F32)
                        TB = banks[0:2]
                        PB = banks[2:4]
                        SU = [banks[4:6], banks[6:8]]
                        block = tp.enter_context(nc.Block())

                        TURNS = [(3, 0), (0, 2), (3, 1), (0, 3), (1, 0), (3, 2), (1, 1), (3, 3), (1, 2), (1, 3)] + \
                                [(2, j) for j in range(TPC)] + [(4, 0), (4, 1)]

                        def turns(c, first):
                            if first:
                                return b * (CH * 16) + 2, [t for t in TURNS if t[0] != 3]
                            return b * (CH * 16) + c * 16 - 2, TURNS

                        def bodies(eng, body):
                            body(0, True, False)
                            with eng.Fori(1, CH - 1) as c:
                                body(c, False, False)
                            body(CH - 1, False, True)

                        LAST = [(3, j) for j in range(TPC)]
                        LAST0 = (b + 1) * (CH * 16) - TPC

                        @block.sync
                        def _(sp):
                            with sp.Fori(1, CH) as c:
                                load_x(sp, b * CH + c)

                        @block.gpsimd
                        def _(pool):
                            def add_xbo(n, c, j):
                                cols = bass.ds(c * (TPC * D) + j * D, D)
                                pool.wait_ge(d_n0, n * TPC + j + 1)
                                pool.tensor_tensor(x2[:, cols], x2[:, cols], xbo_b[:, :], ALU.add).then_inc(d_xb2, 1)

                            def body(c, first, last):
                                n = b * CH + c
                                if not last:
                                    for j in range(TPC):
                                        add_bo(pool, n + 1, j)
                                for s, j in NORMS:
                                    if s == 1 or not last:
                                        norm_scale(pool, s, n + 1 - s, j)
                                if not last:
                                    for j in range(TPC):
                                        add_xbo(n + 1, c + 1, j)

                            NORMS = [(0, 0), (0, 1), (0, 2), (1, 0), (0, 3), (1, 1), (1, 2), (1, 3)]
                            for j in range(TPC):
                                add_xbo(b * CH, 0, j)
                            bodies(pool, body)

                        @block.tensor
                        def _(pe):
                            def transposes(before, i, src, j):
                                pe.wait_ge(d_tl, before + i + 1)
                                for d in range(DC):
                                    mm = pe.transpose(TB[i % 2][:, d * P:(d + 1) * P], src[:, j, d * P:(d + 1) * P],
                                                      ident[:, :])
                                mm.then_inc(d_t_done, 1)

                            def body(c, first, last):
                                n = b * CH + c
                                before, order = turns(c, first)

                                def turn(s, j):
                                    if s in (0, 4):
                                        pe.wait_ge(d_n0, (n + s // 4) * TPC + j + 1)
                                    elif s == 1:
                                        pe.wait_ge(d_q, n * TPC + j + 1)
                                    elif s == 2:
                                        pe.wait_ge(d_o, n * TPC + max(j + 1, min(j + 3, TPC)))
                                    else:
                                        pe.wait_ge(d_n1, (n - 1) * TPC + j + 1)
                                    transposes(before, order.index((s, j)), tok0 if s in (0, 4) else tok, j)

                                def split(s, j):
                                    if s == 0 and j < 2:
                                        return before + j + 1
                                    return before + order.index((s, j)) + 3

                                def project(s, j, name, done):
                                    pe.wait_ge(d_tl, split(s, j))
                                    mm3(pe, PB[j % 2][:, :], lambda d: th[:, j, d * P:(d + 1) * P],
                                        lambda d: tl[:, j, d * P:(d + 1) * P], lambda d: wh[name][:, d, :],
                                        lambda d: wl[name][:, d, :]).then_inc(done, 1)

                                def query(j):
                                    if j >= 2:
                                        pe.wait_ge(d_q, n * TPC + j - 1)
                                    elif not first:
                                        pe.wait_ge(d_x2, (n - 1) * TPC + j + 3)
                                    project(0, j, "xq", d_q_done)
                                    if not first:
                                        turn(3, j)

                                query(0)
                                turn(0, 2)
                                query(1)
                                turn(0, 3)
                                turn(1, 0)
                                query(2)

                                def cross_scores(v):
                                    j, half = v // 2, v % 2
                                    pe.wait_ge(d_tl, split(1, j))
                                    if v >= 2:
                                        pe.wait_ge(d_ex, n * 8 + v - 1)
                                    for i in range(2):
                                        d = 2 * half + i
                                        bank = SU[v % 2][i][:, :]
                                        qh, ql = th[:, j, d * P:(d + 1) * P], tl[:, j, d * P:(d + 1) * P]
                                        pe.matmul(bank, qh, kbh[:, d, :], start=True, stop=False)
                                        pe.matmul(bank, qh, kbl[:, d, :], start=False, stop=False)
                                        mm = pe.matmul(bank, ql, kbh[:, d, :], start=False, stop=True)
                                    mm.then_inc(d_s_done, 1)

                                def transpose_probs(v):
                                    pe.wait_ge(d_ex, n * 8 + v + 1)
                                    pe.wait_ge(d_ptl, (n * 8 + v) * 2 + 2)
                                    for hh in range(8):
                                        mm = pe.transpose(PB[hh // 4][:, hh % 4 * P:hh % 4 * P + P],
                                                          px[:, v % 2, hh * CTX:(hh + 1) * CTX], ident[:, :])
                                    mm.then_inc(d_pt_done, 1)

                                def cross_values(v):
                                    j, half = v // 2, v % 2
                                    pe.wait_ge(d_ptl, (n * 8 + v) * 2 + 4)
                                    if half == 0 and j >= 2:
                                        pe.wait_ge(d_o, n * TPC + j - 1)
                                    elif half == 0:
                                        pe.wait_ge(d_tl, split(1, TPC - 1))
                                    for hh in range(8):
                                        cols = slice((8 * half + hh) * XD, (8 * half + hh + 1) * XD)
                                        ph_, pl_ = (t[:, v % 2, hh * CTX:(hh + 1) * CTX] for t in (pth, ptl))
                                        pe.matmul(TB[j % 2][:, cols], ph_, vxh[:, cols], start=True, stop=False)
                                        pe.matmul(TB[j % 2][:, cols], ph_, vxl[:, cols], start=False, stop=False)
                                        mm = pe.matmul(TB[j % 2][:, cols], pl_, vxh[:, cols], start=False, stop=True)
                                    mm.then_inc(d_av_done, 1)

                                pe.wait_ge(d_x1, n * TPC + 2 * TPC)
                                cross_scores(0)
                                cross_scores(1)
                                turn(1, 1)
                                query(3)
                                turn(1, 2)
                                turn(1, 3)
                                for v in range(8):
                                    if v + 2 < 8:
                                        cross_scores(v + 2)
                                    transpose_probs(v)
                                    if v:
                                        cross_values(v - 1)
                                    if v == 6 and not last:
                                        out_project(pe, c + 1, 0)
                                        out_project(pe, c + 1, 1)
                                    if v == 7 and not last:
                                        out_project(pe, c + 1, 2)
                                cross_values(7)
                                turn(2, 0)
                                if not last:
                                    out_project(pe, c + 1, 3)
                                pe.wait_ge(d_ptl, n * 16 + 18)
                                for j in range(TPC):
                                    if j + 1 < TPC:
                                        turn(2, j + 1)
                                    if j >= 2:
                                        pe.wait_ge(d_x2, n * TPC + j - 1)
                                    project(2, j, "xo", d_xo_done)
                                    if j >= 2 and not last:
                                        turn(4, j - 2)

                            for j in range(2):
                                pe.wait_ge(d_n0, b * (CH * TPC) + j + 1)
                                transposes(b * (CH * 16), j, tok0, j)
                            bodies(pe, body)
                            for i, (_, j) in enumerate(LAST):
                                pe.wait_ge(d_n1, (b + 1) * (CH * TPC) - TPC + j + 1)
                                transposes(LAST0, i, tok, j)

                        @block.scalar
                        def _(act):
                            def high(before, i, dst):
                                act.wait_ge(d_t_done, before + i + 1)
                                act.activation(dst, TB[i % 2][:, :], ACT.Copy).then_inc(d_th, 1)

                            def body(c, first, last):
                                n = b * CH + c
                                before, order = turns(c, first)

                                def high_of(i):
                                    s, j = order[i]
                                    high(before, i, x2th[:, :, bass.ds((c - 1) * CT + j * P, P)] if s == 3
                                         else th[:, j, :])

                                def exponentials(v):
                                    act.wait_ge(d_nmx, (n * 8 + v) * 2 + 2)
                                    act.wait_ge(d_pt_done, n * 8 + v + 1)
                                    for hh in range(8):
                                        ex = act.activation(
                                            px[:, v % 2, hh * CTX:(hh + 1) * CTX],
                                            SU[v % 2][hh // 4][:, hh % 4 * CTX:(hh % 4 + 1) * CTX], ACT.Exp,
                                            bias=nmx[:, v % 2, hh:hh + 1],
                                            accum_out=sm[:, v // 2, 8 * (v % 2) + hh:8 * (v % 2) + hh + 1])
                                    ex.then_inc(d_ex, 1)

                                def probs_high(v):
                                    act.wait_ge(d_pt_done, n * 8 + v + 3)
                                    act.activation(pth[:, v % 2, 0:512], PB[0][:, :], ACT.Copy).then_inc(d_pth[0], 1)

                                early, queries = order.index((1, 1)) + 1, order.index((1, 3)) + 1
                                for i in range(early):
                                    high_of(i)
                                exponentials(0)
                                for i in range(early, queries):
                                    high_of(i)
                                for v in range(8):
                                    if v + 1 < 8:
                                        exponentials(v + 1)
                                    probs_high(v)
                                for i in range(queries, len(order) - 2 * last):
                                    high_of(i)

                            for j in range(2):
                                high(b * (CH * 16), j, th[:, j, :])
                            bodies(act, body)
                            for i, (_, j) in enumerate(LAST):
                                high(LAST0, i, x2th[:, :, (CH - 1) * CT + j * P:(CH - 1) * CT + j * P + P])

                        @block.vector
                        def _(dve):
                            def low(before, i, dst, high):
                                dve.wait_ge(d_th, before + i + 1)
                                dve.tensor_tensor(dst, TB[i % 2][:, :], high, ALU.subtract).then_inc(d_tl, 1)

                            def residual2(n, c, j):
                                cols = bass.ds(c * (TPC * D) + j * D, D)
                                dve.wait_ge(d_xb2, n * TPC + j + 1)
                                dve.wait_ge(d_xo_done, n * TPC + j + 1)
                                dve.scalar_tensor_tensor(out=x2[:, cols], in0=PB[j % 2][:, :], scalar=INV_WS,
                                                         in1=x2[:, cols], op0=ALU.mult, op1=ALU.add)\
                                    .then_inc(d_x2, 1)
                                dve.wait_ge(d_x2, n * TPC + j + 1)
                                dve.nop(nofuse=True)
                                stats(dve, 1, n, j, x2[:, cols])

                            def body(c, first, last):
                                n = b * CH + c
                                before, order = turns(c, first)

                                def low_of(s, j):
                                    if s == 3:
                                        toks = bass.ds((c - 1) * CT + j * P, P)
                                        dst, high = x2tl[:, :, toks], x2th[:, :, toks]
                                    else:
                                        dst, high = tl[:, j, :], th[:, j, :]
                                    low(before, order.index((s, j)), dst, high)

                                def query(j):
                                    dve.wait_ge(d_q_done, n * TPC + j + 1)
                                    dve.scalar_tensor_tensor(out=tok[:, j, :], in0=PB[j % 2][:, :], scalar=INV_WS,
                                                             in1=xbq_b[:, :], op0=ALU.mult, op1=ALU.add)\
                                        .then_inc(d_q, 1)

                                def cross_max(v):
                                    u = n * 8 + v
                                    dve.wait_ge(d_s_done, u + 1)
                                    for i in range(2):
                                        dve.tensor_reduce(nmx[:, v % 2, 4 * i:4 * i + 4],
                                                          SU[v % 2][i][:, :].rearrange("p (h k) -> p h k", k=CTX),
                                                          AX_X, ALU.max, negate=True).then_inc(d_nmx, 1)

                                def probs_low(v):
                                    dve.wait_ge(d_pt_done, n * 8 + v + 3)
                                    dve.tensor_copy(pth[:, v % 2, 512:1024], PB[1][:, :]).then_inc(d_pth[1], 1)
                                    for i in range(2):
                                        dve.wait_ge(d_pth[i], n * 8 + v + 1)
                                        dve.tensor_tensor(ptl[:, v % 2, i * 512:i * 512 + 512], PB[i][:, :],
                                                          pth[:, v % 2, i * 512:i * 512 + 512], ALU.subtract)\
                                            .then_inc(d_ptl, 1)

                                def output(j):
                                    dve.wait_ge(d_ex, n * 8 + 2 * j + 2)
                                    dve.reciprocal(rsm[:, j, :], sm[:, j, :]).then_inc(d_rec, 1)
                                    dve.wait_ge(d_rec, n * TPC + j + 1)
                                    dve.wait_ge(d_av_done, n * 8 + 2 * j + 2)
                                    dve.tensor_tensor(tok[:, j, :].rearrange("p (h d) -> p h d", d=XD),
                                                      TB[j % 2][:, :].rearrange("p (h d) -> p h d", d=XD),
                                                      rsm[:, j, :].rearrange("p (h a) -> p h a", a=1)
                                                      .broadcast_to([P, XH, XD]), ALU.mult).then_inc(d_o, 1)

                                def tile_left(j):
                                    if not first:
                                        low_of(3, j)

                                tile_left(0)
                                low_of(0, 2)
                                query(0)
                                tile_left(1)
                                low_of(0, 3)
                                query(1)
                                low_of(1, 0)
                                tile_left(2)
                                query(2)
                                cross_max(0)
                                low_of(1, 1)
                                cross_max(1)
                                tile_left(3)
                                query(3)
                                low_of(1, 2)
                                low_of(1, 3)
                                for v in range(8):
                                    if v + 2 < 8:
                                        cross_max(v + 2)
                                    probs_low(v)
                                    if v >= 2 and v % 2 == 0:
                                        output(v // 2 - 1)
                                if not last:
                                    residual1(dve, n + 1, c + 1, 0)
                                    residual1(dve, n + 1, c + 1, 1)
                                output(TPC - 1)
                                low_of(2, 0)
                                if not last:
                                    residual1(dve, n + 1, c + 1, 2)
                                low_of(2, 1)
                                if not last:
                                    norm(dve, 0, n + 1, c + 1, 0)
                                    norm(dve, 0, n + 1, c + 1, 1)
                                residual2(n, c, 0)
                                if not last:
                                    residual1(dve, n + 1, c + 1, 3)
                                low_of(2, 2)
                                if not last:
                                    norm(dve, 0, n + 1, c + 1, 2)
                                residual2(n, c, 1)
                                if not last:
                                    norm(dve, 0, n + 1, c + 1, 3)
                                low_of(2, 3)
                                residual2(n, c, 2)
                                if not last:
                                    low_of(4, 0)
                                norm(dve, 1, n, c, 0)
                                residual2(n, c, 3)
                                if not last:
                                    low_of(4, 1)
                                for j in range(1, TPC):
                                    norm(dve, 1, n, c, j)

                            for j in range(2):
                                low(b * (CH * 16), j, tl[:, j, :], th[:, j, :])
                            bodies(dve, body)
                            for i, (_, j) in enumerate(LAST):
                                toks = slice((CH - 1) * CT + j * P, (CH - 1) * CT + j * P + P)
                                low(LAST0, i, x2tl[:, :, toks], x2th[:, :, toks])

                with ExitStack() as ph:
                    stage = [sb(ph, f"stage_f{i}", [P, 2, D], F32) for i in range(4)]
                    names = ("w10", "w11", "w20", "w21")
                    wh = {n_: sb(ph, f"fwh_{n_}", [P, DC, D], F16) for n_ in names}
                    wl = {n_: sb(ph, f"fwl_{n_}", [P, DC, D], F16) for n_ in names}
                    col = sb(ph, "col", [P, DC], F32)
                    sc = sb(ph, "sc", [1, E], F32)
                    best = sb(ph, "best", [1, 8], F32)
                    idx = sb(ph, "idx", [1, 8], U32)
                    b1c = sb(ph, "b1c", [P, 2, DC], F32)
                    b2r = sb(ph, "b2r", [P, 2, D], F32)
                    b2s = sb(ph, "b2s", [P, 2, D], F32)
                    g32 = sb(ph, "g32", [P, 2, CT], F32)
                    gh = sb(ph, "gh", [P, 2, DC, CT], F16)
                    gl = sb(ph, "gl", [P, 2, DC, CT], F16)
                    yt = sb(ph, "yt_f", [P, 2, D], F32)
                    F1 = banks[0:2]
                    F2 = banks[2:4]
                    block = ph.enter_context(nc.Block())

                    @block.sync
                    def _(sp):
                        sp.wait_ge(r_idx, b + 1)
                        sp.nop(nofuse=True)
                        expert = [sp.value_load(idx[0:1, k:k + 1], min_val=0, max_val=E - 1) for k in range(2)]

                        def rows_of(w, e):
                            v = w[bass.ds(e, 1), :, :].rearrange("a (c p) n -> p (a c) n", p=P)
                            return [[v[64 * half:64 * half + 64, 2 * i:2 * i + 2, :] for half in range(2)]
                                    for i in range(2)]

                        src = {"w10": rows_of(w1, expert[0]), "w11": rows_of(w1, expert[1]),
                               "w20": rows_of(w2, expert[0]), "w21": rows_of(w2, expert[1])}
                        load_pieces(sp, b, PIECES_P4[:2], stage, src)
                        for k in range(2):
                            sp.dma_start(b1c[:, k, :], b1[bass.ds(expert[k], 1), :, :].rearrange("a p c -> p (a c)"))\
                                .then_inc(f_b, 16)
                            sp.dma_start(b2r[:, k, :], b2[bass.ds(expert[k], 1), :].broadcast_to([P, D])).then_inc(f_b, 16)
                        load_pieces(sp, b, PIECES_P4[2:], stage, src)
                        with sp.Fori(0, CH) as c:
                            n = b * CH + c
                            for j in range(TPC):
                                sp.wait_ge(f_y, n * TPC + j + 3)
                                sp.dma_start(out_rows[bass.ds(n * CT + j * P, P), :], yt[:, j % 2, :])\
                                    .then_inc(y_out[j % 2], 16)
                        for s in range(2):
                            sp.wait_ge(y_out[s], (b + 1) * (CH * 32) + 16)
                        sp.nop(nofuse=True)

                    @block.gpsimd
                    def _(pool):
                        pool.wait_ge(f_b2, 2 * b + 2)
                        pool.nop(nofuse=True)
                        with pool.Fori(0, CH) as c:
                            n = b * CH + c
                            for j in range(TPC):
                                cols = bass.ds(c * (TPC * D) + j * D, D)
                                pool.tensor_tensor(x2[:, cols], x2[:, cols], b2s[:, 1, :], ALU.add).then_inc(f_xb, 1)

                    @block.tensor
                    def _(pe):
                        pe.wait_ge(r_col, b + 1)
                        for d in range(DC):
                            mm = pe.matmul(F1[0][0:1, 0:E], col[:, d:d + 1], wr_sb[:, d, :], start=(d == 0),
                                           stop=(d == DC - 1))
                        mm.then_inc(r_mm, 1)
                        pe.wait_ge(r_sc, b + 1)
                        pe.nop(nofuse=True)
                        with pe.Fori(0, CH) as c:
                            n = b * CH + c
                            toks = bass.ds(c * CT, CT)
                            for w in range(8):
                                k, ec = w // DC, w % DC
                                pe.wait_ge(f_g, n * 8 + w + 1)
                                if ec == 0:
                                    pe.wait_ge(w_split, pieces_split(b, PIECES_P4[:2 * k + 2]))
                                ecols = slice(ec * P, ec * P + P)
                                mm3(pe, F1[w % 2][:, :], lambda d: wh[f"w1{k}"][:, d, ecols],
                                    lambda d: wl[f"w1{k}"][:, d, ecols], lambda d: x2th[:, d, toks],
                                    lambda d: x2tl[:, d, toks]).then_inc(f1_done, 1)
                            pe.wait_ge(w_split, pieces_split(b, PIECES_P4))
                            for j in range(TPC):
                                pe.wait_ge(f_y, n * TPC + j + 1)
                                cols = slice(j * P, j * P + P)
                                for w in range(8):
                                    k, ec = w // DC, w % DC
                                    if j == 0:
                                        pe.wait_ge(f_gl, n * 8 + w + 1)
                                    bank = F2[j % 2][:, :]
                                    pe.matmul(bank, gh[:, k, ec, cols], wh[f"w2{k}"][:, ec, :], start=(w == 0),
                                              stop=False)
                                    pe.matmul(bank, gh[:, k, ec, cols], wl[f"w2{k}"][:, ec, :], start=False,
                                              stop=False)
                                    mm = pe.matmul(bank, gl[:, k, ec, cols], wh[f"w2{k}"][:, ec, :], start=False,
                                                   stop=(w == 7))
                                mm.then_inc(f2_done, 1)

                    @block.scalar
                    def _(act):
                        split_high(act, b, PIECES_P4[:2], stage, wh)
                        act.wait_ge(f_b, b * 64 + 64)
                        act.nop(nofuse=True)
                        act.preload_act_table(ACT.Gelu)

                        def chunk(c, splits):
                            n = b * CH + c
                            for w in range(8):
                                k, ec = w // DC, w % DC
                                act.wait_ge(f1_done, n * 8 + w + 1)
                                if w >= 2:
                                    act.wait_ge(f_gl, n * 8 + w - 1)
                                act.activation(g32[:, w % 2, :], F1[w % 2][:, :], ACT.Gelu, bias=b1c[:, k, ec:ec + 1],
                                               scale=INV_WS).then_inc(f_g, 1)
                                if splits and w < 6:
                                    split_high(act, b, PIECES_P4[2 + w:3 + w], stage, wh)

                        chunk(0, True)
                        with act.Fori(1, CH) as c:
                            chunk(c, False)

                    @block.vector
                    def _(dve):
                        dve.tensor_tensor(col[:, :], x2th[:, :, 0], x2tl[:, :, 0], ALU.add).then_inc(r_col, 1)
                        dve.wait_ge(r_mm, b + 1)
                        dve.tensor_tensor(sc[:, :], F1[0][0:1, 0:E], br_sb[:, :], ALU.add).then_inc(r_sc, 1)
                        dve.wait_ge(r_sc, b + 1)
                        dve.nop(nofuse=True)
                        dve.max(best[:, :], sc[:, :]).then_inc(r_top, 1)
                        dve.wait_ge(r_top, b + 1)
                        dve.nop(nofuse=True)
                        dve.max_index(idx[:, :], best[:, :], sc[:, :]).then_inc(r_idx, 1)
                        split_low(dve, b, PIECES_P4[:2], stage, wh, wl)
                        dve.wait_ge(f_b, b * 64 + 64)
                        dve.tensor_tensor(b2s[:, 0, :], b2r[:, 0, :], b2r[:, 1, :], ALU.add).then_inc(f_b2, 1)
                        dve.wait_ge(f_b2, 2 * b + 1)
                        dve.tensor_scalar(b2s[:, 1, :], b2s[:, 0, :], 0.5, None, ALU.mult).then_inc(f_b2, 1)

                        def chunk(c, splits):
                            n = b * CH + c
                            dve.wait_ge(f2_done, n * TPC + 4)
                            for w in range(8):
                                k, ec = w // DC, w % DC
                                dve.wait_ge(f_g, n * 8 + w + 3)
                                dve.tensor_copy(gh[:, k, ec, :], g32[:, w % 2, :]).then_inc(f_gh, 1)
                                dve.wait_ge(f_gh, n * 8 + w + 1)
                                dve.tensor_tensor(gl[:, k, ec, :], g32[:, w % 2, :], gh[:, k, ec, :], ALU.subtract)\
                                    .then_inc(f_gl, 1)
                                if splits and w < 6:
                                    split_low(dve, b, PIECES_P4[2 + w:3 + w], stage, wh, wl)
                            for j in range(TPC):
                                cols = bass.ds(c * (TPC * D) + j * D, D)
                                dve.wait_ge(f2_done, n * TPC + j + 5)
                                dve.wait_ge(f_xb, n * TPC + j + 1)
                                dve.wait_ge(y_out[j % 2], n * 32 + 16 * (j // 2) + 16)
                                dve.scalar_tensor_tensor(out=yt[:, j % 2, :], in0=F2[j % 2][:, :], scalar=0.5 * INV_WS,
                                                         in1=x2[:, cols], op0=ALU.mult, op1=ALU.add).then_inc(f_y, 1)

                        chunk(0, True)
                        with dve.Fori(1, CH) as c:
                            chunk(c, False)


_INS = ["x", "ctx_1024", "L0_attn_ln_gamma", "L0_attn_ln_beta", "L0_attn_q_gamma", "L0_attn_k_gamma", "L0_attn_w_q",
        "L0_attn_w_k", "L0_attn_w_v", "L0_attn_w_o", "L0_attn_b_o", "L0_xattn_Wq", "L0_xattn_bq", "L0_xattn_Wk",
        "L0_xattn_bk", "L0_xattn_Wv", "L0_xattn_bv", "L0_xattn_Wo", "L0_xattn_bo", "L0_ffn_Wr", "L0_ffn_br",
        "L0_ffn_W1", "L0_ffn_b1", "L0_ffn_W2", "L0_ffn_b2"]
_TRANSPOSED = ("L0_attn_w_q", "L0_attn_w_k", "L0_attn_w_v", "L0_attn_w_o")


def kernel(**inputs):
    import numpy as _np
    import concourse.bacc as _bacc
    from concourse import mybir as _mybir
    from concourse.bass_utils import run_bass_kernel_spmd as _run

    nc = _bacc.Bacc("TRN2", target_bir_lowering=False, num_devices=1)
    arrays, args = {}, []
    for name in _INS:
        a = _np.asarray(inputs[name])
        if name == "L0_ffn_b1":
            a = a.reshape(a.shape[0], -1, P).transpose(0, 2, 1)
        a = _np.ascontiguousarray(a.T if name in _TRANSPOSED else a)
        arrays[f"in_{name}"] = a
        args.append(nc.dram_tensor(f"in_{name}", a.shape, _mybir.dt.from_np(a.dtype), kind="ExternalInput").ap())
    shape = inputs["x"].shape
    y = nc.dram_tensor("out_0", shape, _mybir.dt.from_np(_np.dtype("float32")), kind="ExternalOutput").ap()
    decoder_layer(nc, *args, y)
    r = _run(nc, [arrays], core_ids=[0])
    return r.results[0]["out_0"]
```
